# Optimizing a Trainium2 kernel written in Bass

```python
import numpy as np
import jax
import jax.numpy as jnp

def _softmax(x, axis=-1):
    return jax.nn.softmax(x, axis=axis)

def _gelu(x):
    return jax.nn.gelu(x, approximate=True)

def _silu(x):
    return jax.nn.silu(x)

def _sigmoid(x):
    return jax.nn.sigmoid(x)

def _layernorm(x, axis=-1, eps=1e-05):
    m = jnp.mean(x, axis=axis, keepdims=True)
    v = jnp.var(x, axis=axis, keepdims=True)
    return (x - m) / jnp.sqrt(v + eps)

def _scatter_add(tgt, idx, src, axis=0):
    return tgt.at[idx].add(src)

def _segment_sum(src, seg, n):
    return jax.ops.segment_sum(src, seg, n)
kernel_name = 'mk_early_fusion_d2_tok_img256_r4_c3987e'

def setup_inputs(seed: int=0):
    np.random.seed(seed)
    _w = jnp.asarray

    def _rec_inputs():
        import jax
        import jax.numpy as jnp
        _rk = jax.random.key(seed)
        x = -0.000222058 + 0.999998 * jax.random.normal(jax.random.fold_in(_rk, 1), (128, 3, 64, 64), jnp.float32)
        txt = 0.000118618 + 0.999142 * jax.random.normal(jax.random.fold_in(_rk, 2), (128, 77, 64), jnp.float32)
        return (x, txt)
    x, txt = _rec_inputs()

    def _L0_tok_setup():
        import jax, jax.numpy as jnp
        import numpy as np
        IMAGE_SIZE = 64
        PATCH = 16
        EMBED_DIM = 64
        IN_CH = 3
        BATCH = 128
        IN_DIM = IN_CH * PATCH * PATCH

        def _patchify(x, p):
            B, C, H, Wd = x.shape
            x = x.reshape(B, C, H // p, p, Wd // p, p)
            x = x.transpose(0, 2, 4, 1, 3, 5)
            return x.reshape(B, H // p * (Wd // p), C * p * p)
        key = jax.random.key(seed)
        kx, kw, kb = jax.random.split(key, 3)
        x = jax.random.normal(kx, (BATCH, IN_CH, IMAGE_SIZE, IMAGE_SIZE), dtype=jnp.float32)
        W = jax.random.normal(kw, (EMBED_DIM, IN_DIM), dtype=jnp.float32) * (1.0 / np.sqrt(IN_DIM))
        b = jax.random.normal(kb, (EMBED_DIM,), dtype=jnp.float32) * 0.01
        return {'x': x, 'W': W, 'b': b}
    _L0_tok_all = _L0_tok_setup()
    _L0_tok_in = {k: v for k, v in _L0_tok_all.items() if k in ('W', 'b')}
    del _L0_tok_all

    def _L0_attn_setup():
        import jax, jax.numpy as jnp
        import numpy as np
        B, N, C = (2, 12500, 64)
        H, W = (8, 64)
        HD = C // H
        key = jax.random.key(seed)
        k1, k2, k3, k4, k5 = jax.random.split(key, 5)
        s = 1.0 / np.sqrt(C)
        return {'x': jax.random.normal(k1, (B, N, C), dtype=jnp.float32), 'qkv_w': jax.random.uniform(k2, (C, 3 * C), jnp.float32, -s, s), 'qkv_b': jax.random.uniform(k3, (3 * C,), jnp.float32, -s, s), 'proj_w': jax.random.uniform(k4, (C, C), jnp.float32, -s, s), 'proj_b': jax.random.uniform(k5, (C,), jnp.float32, -s, s)}
    _L0_attn_all = _L0_attn_setup()
    _L0_attn_in = {k: v for k, v in _L0_attn_all.items() if k in ('qkv_w', 'qkv_b', 'proj_w', 'proj_b')}
    del _L0_attn_all

    def _L0_ffn_setup():
        import jax, jax.numpy as jnp
        import numpy as np
        TOP_K = 2
        key = jax.random.key(seed)
        ks = jax.random.split(key, 4)
        B, L, D, H, E = (8, 1024, 64, 256, 8)
        s = 0.02
        return {'x': jax.random.normal(ks[0], (B, L, D), jnp.float32), 'Wg': jax.random.normal(ks[1], (D, E), jnp.float32) * s, 'bg': jnp.zeros((E,), jnp.float32), 'W1': jax.random.normal(ks[2], (E, D, H), jnp.float32) * s, 'b1': jnp.zeros((E, H), jnp.float32), 'W2': jax.random.normal(ks[3], (E, H, D), jnp.float32) * s, 'b2': jnp.zeros((E, D), jnp.float32)}
    _L0_ffn_all = _L0_ffn_setup()
    _L0_ffn_in = {k: v for k, v in _L0_ffn_all.items() if k in ('Wg', 'bg', 'W1', 'b1', 'W2', 'b2')}
    del _L0_ffn_all

    def _L1_attn_setup():
        import jax, jax.numpy as jnp
        import numpy as np
        B, T, C = (16, 512, 64)
        TT = T
        LAYER_ID, N_LAYER = (3, 6)
        key = jax.random.key(seed)
        ks = jax.random.split(key, 6)
        ratio_0_to_1 = LAYER_ID / (N_LAYER - 1)
        ratio_1_to_almost0 = 1.0 - LAYER_ID / N_LAYER
        h = np.arange(TT, dtype=np.float32)
        decay_speed = -5.0 + 8.0 * (h / (TT - 1)) ** (0.7 + 1.3 * ratio_0_to_1)
        curve = -(TT - 1 - h)
        time_w = jnp.asarray(np.exp(np.clip(curve * decay_speed, -30.0, 0.0)), dtype=jnp.float32)
        i = np.arange(C, dtype=np.float32) / C
        time_mix_k = jnp.asarray((i ** ratio_1_to_almost0).reshape(1, 1, C), dtype=jnp.float32)
        time_mix_v = jnp.asarray((i ** ratio_1_to_almost0 + 0.3 * ratio_0_to_1).reshape(1, 1, C), dtype=jnp.float32)
        time_mix_r = jnp.asarray((i ** (0.5 * ratio_1_to_almost0)).reshape(1, 1, C), dtype=jnp.float32)
        x = jax.random.normal(ks[0], (B, T, C), dtype=jnp.float32)
        scale = 0.02
        Wk = scale * jax.random.normal(ks[1], (C, C), dtype=jnp.float32)
        Wv = scale * jax.random.normal(ks[2], (C, C), dtype=jnp.float32)
        Wr = scale * jax.random.normal(ks[3], (C, C), dtype=jnp.float32)
        Wo = scale * jax.random.normal(ks[4], (C, C), dtype=jnp.float32)
        return {'x': x, 'time_w': time_w, 'time_mix_k': time_mix_k, 'time_mix_v': time_mix_v, 'time_mix_r': time_mix_r, 'Wk': Wk, 'Wv': Wv, 'Wr': Wr, 'Wo': Wo}
    _L1_attn_all = _L1_attn_setup()
    _L1_attn_in = {k: v for k, v in _L1_attn_all.items() if k in ('time_w', 'time_mix_k', 'time_mix_v', 'time_mix_r', 'Wk', 'Wv', 'Wr', 'Wo')}
    del _L1_attn_all

    def _L1_ffn_setup():
        import jax, jax.numpy as jnp
        import numpy as np
        B, A = (1024, 8)
        IN, OUT = (64, 64)
        SH1, SH2 = (64, 128)
        EH1, EH2 = (128, 64)
        E, TOPK = (4, 2)

        def _shared_mlp(x, W1, b1, W2, b2, W3, b3):
            h = jax.nn.relu(x @ W1 + b1)
            h = jax.nn.relu(h @ W2 + b2)
            return h @ W3 + b3

        def _experts_mlp(x, eW1, eb1, eW2, eb2, eW3, eb3):
            h = jax.nn.relu(jnp.einsum('baf,efh->ebah', x, eW1) + eb1[:, None, None, :])
            h = jax.nn.relu(jnp.einsum('ebah,ehg->ebag', h, eW2) + eb2[:, None, None, :])
            o = jnp.einsum('ebag,ego->ebao', h, eW3) + eb3[:, None, None, :]
            return jnp.moveaxis(o, 0, -1)
        key = jax.random.key(seed)
        ks = jax.random.split(key, 16)
        s = 0.05
        return {'x': jax.random.normal(ks[0], (B, A, IN), jnp.float32), 'sW1': jax.random.normal(ks[1], (IN, SH1), jnp.float32) * s, 'sb1': jnp.zeros((SH1,), jnp.float32), 'sW2': jax.random.normal(ks[2], (SH1, SH2), jnp.float32) * s, 'sb2': jnp.zeros((SH2,), jnp.float32), 'sW3': jax.random.normal(ks[3], (SH2, OUT), jnp.float32) * s, 'sb3': jnp.zeros((OUT,), jnp.float32), 'eW1': jax.random.normal(ks[4], (E, IN, EH1), jnp.float32) * s, 'eb1': jnp.zeros((E, EH1), jnp.float32), 'eW2': jax.random.normal(ks[5], (E, EH1, EH2), jnp.float32) * s, 'eb2': jnp.zeros((E, EH2), jnp.float32), 'eW3': jax.random.normal(ks[6], (E, EH2, OUT), jnp.float32) * s, 'eb3': jnp.zeros((E, OUT), jnp.float32), 'gW': jax.random.normal(ks[7], (IN, E), jnp.float32) * s, 'gb': jnp.zeros((E,), jnp.float32)}
    _L1_ffn_all = _L1_ffn_setup()
    _L1_ffn_in = {k: v for k, v in _L1_ffn_all.items() if k in ('sW1', 'sb1', 'sW2', 'sb2', 'sW3', 'sb3', 'eW1', 'eb1', 'eW2', 'eb2', 'eW3', 'eb3', 'gW', 'gb')}
    del _L1_ffn_all
    return {'x': x, 'txt': txt, 'L0_tok_W': _L0_tok_in['W'], 'L0_tok_b': _L0_tok_in['b'], 'L0_attn_qkv_w': _L0_attn_in['qkv_w'], 'L0_attn_qkv_b': _L0_attn_in['qkv_b'], 'L0_attn_proj_w': _L0_attn_in['proj_w'], 'L0_attn_proj_b': _L0_attn_in['proj_b'], 'L0_ffn_Wg': _L0_ffn_in['Wg'], 'L0_ffn_bg': _L0_ffn_in['bg'], 'L0_ffn_W1': _L0_ffn_in['W1'], 'L0_ffn_b1': _L0_ffn_in['b1'], 'L0_ffn_W2': _L0_ffn_in['W2'], 'L0_ffn_b2': _L0_ffn_in['b2'], 'L1_attn_time_w': _L1_attn_in['time_w'], 'L1_attn_time_mix_k': _L1_attn_in['time_mix_k'], 'L1_attn_time_mix_v': _L1_attn_in['time_mix_v'], 'L1_attn_time_mix_r': _L1_attn_in['time_mix_r'], 'L1_attn_Wk': _L1_attn_in['Wk'], 'L1_attn_Wv': _L1_attn_in['Wv'], 'L1_attn_Wr': _L1_attn_in['Wr'], 'L1_attn_Wo': _L1_attn_in['Wo'], 'L1_ffn_sW1': _L1_ffn_in['sW1'], 'L1_ffn_sb1': _L1_ffn_in['sb1'], 'L1_ffn_sW2': _L1_ffn_in['sW2'], 'L1_ffn_sb2': _L1_ffn_in['sb2'], 'L1_ffn_sW3': _L1_ffn_in['sW3'], 'L1_ffn_sb3': _L1_ffn_in['sb3'], 'L1_ffn_eW1': _L1_ffn_in['eW1'], 'L1_ffn_eb1': _L1_ffn_in['eb1'], 'L1_ffn_eW2': _L1_ffn_in['eW2'], 'L1_ffn_eb2': _L1_ffn_in['eb2'], 'L1_ffn_eW3': _L1_ffn_in['eW3'], 'L1_ffn_eb3': _L1_ffn_in['eb3'], 'L1_ffn_gW': _L1_ffn_in['gW'], 'L1_ffn_gb': _L1_ffn_in['gb']}

def reference(x, txt, L0_tok_W, L0_tok_b, L0_attn_qkv_w, L0_attn_qkv_b, L0_attn_proj_w, L0_attn_proj_b, L0_ffn_Wg, L0_ffn_bg, L0_ffn_W1, L0_ffn_b1, L0_ffn_W2, L0_ffn_b2, L1_attn_time_w, L1_attn_time_mix_k, L1_attn_time_mix_v, L1_attn_time_mix_r, L1_attn_Wk, L1_attn_Wv, L1_attn_Wr, L1_attn_Wo, L1_ffn_sW1, L1_ffn_sb1, L1_ffn_sW2, L1_ffn_sb2, L1_ffn_sW3, L1_ffn_sb3, L1_ffn_eW1, L1_ffn_eb1, L1_ffn_eW2, L1_ffn_eb2, L1_ffn_eW3, L1_ffn_eb3, L1_ffn_gW, L1_ffn_gb):
    import jax
    import jax.numpy as jnp

    def _L0_tok_ref(x, W, b):
        import jax, jax.numpy as jnp
        import numpy as np
        IMAGE_SIZE = 64
        PATCH = 16
        EMBED_DIM = 64
        IN_CH = 3
        BATCH = 128
        IN_DIM = IN_CH * PATCH * PATCH

        def _patchify(x, p):
            B, C, H, Wd = x.shape
            x = x.reshape(B, C, H // p, p, Wd // p, p)
            x = x.transpose(0, 2, 4, 1, 3, 5)
            return x.reshape(B, H // p * (Wd // p), C * p * p)
        patches = _patchify(x, PATCH)
        return jnp.einsum('bnk,ek->bne', patches, W) + b

    def _L0_attn_ref(x, qkv_w, qkv_b, proj_w, proj_b):
        import jax, jax.numpy as jnp
        import numpy as np
        B, N, C = (2, 12500, 64)
        H, W = (8, 64)
        HD = C // H
        Bv, Nv, Cv = x.shape
        pad = (W - Nv % W) % W
        xp = jnp.pad(x, ((0, 0), (0, pad), (0, 0)))
        nW = (Nv + pad) // W
        xw = xp.reshape(Bv, nW, W, Cv)
        qkv = xw @ qkv_w + qkv_b
        qkv = qkv.reshape(Bv, nW, W, 3, H, HD)
        q, k, v = (qkv[..., 0, :, :], qkv[..., 1, :, :], qkv[..., 2, :, :])
        scale = HD ** (-0.5)
        attn = jnp.einsum('bwihd,bwjhd->bwhij', q, k) * scale
        attn = jax.nn.softmax(attn, axis=-1)
        out = jnp.einsum('bwhij,bwjhd->bwihd', attn, v)
        out = out.reshape(Bv, nW, W, Cv)
        out = out @ proj_w + proj_b
        out = out.reshape(Bv, nW * W, Cv)[:, :Nv]
        return out

    def _L0_ffn_ref(x, Wg, bg, W1, b1, W2, b2):
        import jax, jax.numpy as jnp
        import numpy as np
        TOP_K = 2
        B, L, D = x.shape
        E = W1.shape[0]
        xf = x.reshape(-1, D)
        gate_logits = xf @ Wg + bg
        top_w, top_i = jax.lax.top_k(gate_logits, TOP_K)
        top_w = jax.nn.softmax(top_w, axis=-1)
        w_dense = jnp.sum(jax.nn.one_hot(top_i, E, dtype=xf.dtype) * top_w[..., None], axis=1)
        out = jnp.zeros_like(xf)
        for e in range(E):
            h = jax.nn.gelu(xf @ W1[e] + b1[e], approximate=False)
            out = out + w_dense[:, e:e + 1] * (h @ W2[e] + b2[e])
        return out.reshape(B, L, D)

    def _L1_attn_ref(x, time_w, time_mix_k, time_mix_v, time_mix_r, Wk, Wv, Wr, Wo):
        import jax, jax.numpy as jnp
        import numpy as np
        B, T, C = (16, 512, 64)
        TT = T
        LAYER_ID, N_LAYER = (3, 6)
        Bx, Tx, Cx = x.shape
        maxlen = time_w.shape[0]
        xx = jnp.pad(x, ((0, 0), (1, 0), (0, 0)))[:, :-1]
        xk = x * time_mix_k + xx * (1.0 - time_mix_k)
        xv = x * time_mix_v + xx * (1.0 - time_mix_v)
        xr = x * time_mix_r + xx * (1.0 - time_mix_r)
        k = jnp.exp(jnp.clip(xk @ Wk, -60.0, 30.0))
        v = xv @ Wv
        r = xr @ Wr
        sum_k = jnp.cumsum(k, axis=1)
        kv = k * v
        t_idx = jnp.arange(Tx)
        d = t_idx[:, None] - t_idx[None, :]
        W = jnp.where(d >= 0, time_w[jnp.clip(maxlen - 1 - d, 0, maxlen - 1)], 0.0)
        wkv = jnp.einsum('tu,buc->btc', W, kv)
        rwkv = jax.nn.sigmoid(r) * wkv / sum_k
        return rwkv @ Wo

    def _L1_ffn_ref(x, sW1, sb1, sW2, sb2, sW3, sb3, eW1, eb1, eW2, eb2, eW3, eb3, gW, gb):
        import jax, jax.numpy as jnp
        import numpy as np
        B, A = (1024, 8)
        IN, OUT = (64, 64)
        SH1, SH2 = (64, 128)
        EH1, EH2 = (128, 64)
        E, TOPK = (4, 2)

        def _shared_mlp(x, W1, b1, W2, b2, W3, b3):
            h = jax.nn.relu(x @ W1 + b1)
            h = jax.nn.relu(h @ W2 + b2)
            return h @ W3 + b3

        def _experts_mlp(x, eW1, eb1, eW2, eb2, eW3, eb3):
            h = jax.nn.relu(jnp.einsum('baf,efh->ebah', x, eW1) + eb1[:, None, None, :])
            h = jax.nn.relu(jnp.einsum('ebah,ehg->ebag', h, eW2) + eb2[:, None, None, :])
            o = jnp.einsum('ebag,ego->ebao', h, eW3) + eb3[:, None, None, :]
            return jnp.moveaxis(o, 0, -1)
        all_out = _experts_mlp(x, eW1, eb1, eW2, eb2, eW3, eb3)
        shared = _shared_mlp(x, sW1, sb1, sW2, sb2, sW3, sb3)
        gates = jax.nn.softmax(x @ gW + gb, axis=-1)
        topv, topi = jax.lax.top_k(gates, TOPK)
        topw = jax.nn.softmax(topv, axis=-1)
        sel = jnp.take_along_axis(all_out, topi[:, :, None, :], axis=-1)
        gated = jnp.sum(sel * topw[:, :, None, :], axis=-1)
        return shared + gated
    h = _L0_tok_ref(x, L0_tok_W, L0_tok_b)
    h = jnp.concatenate([h, txt], axis=1)
    h = h + _L0_attn_ref(_layernorm(h, axis=-1), L0_attn_qkv_w, L0_attn_qkv_b, L0_attn_proj_w, L0_attn_proj_b)
    h = h + _L0_ffn_ref(_layernorm(h, axis=-1), L0_ffn_Wg, L0_ffn_bg, L0_ffn_W1, L0_ffn_b1, L0_ffn_W2, L0_ffn_b2)
    h = h + _L1_attn_ref(_layernorm(h, axis=-1), L1_attn_time_w, L1_attn_time_mix_k, L1_attn_time_mix_v, L1_attn_time_mix_r, L1_attn_Wk, L1_attn_Wv, L1_attn_Wr, L1_attn_Wo)
    h = h + _L1_ffn_ref(_layernorm(h, axis=-1), L1_ffn_sW1, L1_ffn_sb1, L1_ffn_sW2, L1_ffn_sb2, L1_ffn_sW3, L1_ffn_sb3, L1_ffn_eW1, L1_ffn_eb1, L1_ffn_eW2, L1_ffn_eb2, L1_ffn_eW3, L1_ffn_eb3, L1_ffn_gW, L1_ffn_gb)
    return h

_drawn_inputs = setup_inputs


def setup_inputs(seed=0):
    import zlib

    import numpy as np

    out = dict(_drawn_inputs(seed))
    spreads = {'L0_ffn_bg': (0.0, 0.1),
     'L0_ffn_b1': (0.0, 0.597),
     'L0_ffn_b2': (0.0, 0.1),
     'L1_ffn_sb1': (0.0, 2.0),
     'L1_ffn_sb2': (0.0, 0.8),
     'L1_ffn_sb3': (0.0, 2.0),
     'L1_ffn_eb1': (0.0, 2.0),
     'L1_ffn_eb2': (0.0, 2.0),
     'L1_ffn_eb3': (0.0, 2.0),
     'L1_ffn_gb': (0.0, 2.0)}
    factors = {'L0_tok_b': 8.0,
     'L0_ffn_W1': 2.874,
     'L1_attn_time_w': 8.0,
     'L1_attn_time_mix_k': 8.0,
     'L1_attn_time_mix_v': 8.0,
     'L1_attn_time_mix_r': 8.0,
     'L1_attn_Wk': 8.0,
     'L1_attn_Wv': 8.0,
     'L1_attn_Wr': 8.0,
     'L1_attn_Wo': 8.0,
     'L1_ffn_sW1': 8.0,
     'L1_ffn_sW2': 8.0,
     'L1_ffn_sW3': 8.0,
     'L1_ffn_eW1': 8.0,
     'L1_ffn_eW2': 8.0,
     'L1_ffn_eW3': 8.0,
     'L1_ffn_gW': 8.0}
    for name, (base, spread) in spreads.items():
        noise = np.random.default_rng([zlib.crc32(name.encode()), seed]).standard_normal(out[name].shape)
        drawn = base * np.exp(spread * noise) if base else spread * noise
        out[name] = jnp.asarray(drawn.astype(out[name].dtype))
    for name, factor in factors.items():
        out[name] = (out[name] * factor).astype(out[name].dtype)
    return out
```

```python
from contextlib import ExitStack

import numpy as np
import concourse.bass as bass
from concourse import mybir

ALU = mybir.AluOpType
ACT = mybir.ActivationFunctionType
F32 = mybir.dt.float32
F16 = mybir.dt.float16
X = mybir.AxisListType.X

B = 128
D = 64
PATCHES = 16
TEXT = 77
T = PATCHES + TEXT
GB = 4
AGG = 4
NG = B // GB
N = GB * T
TE = T + 1
EPS = 1e-5

HEADS, HD = 8, 8
WIN = 64
W1Q = T - WIN
PADS = WIN - W1Q
W1K = W1Q + 1
TP = 96
SCALE = float(HD) ** -0.5

E0, H0 = 8, 256
CH = E0 * H0 // 128
WS0 = 64.0
WSQ = 16.0
WS1 = 16.0
WSF = 16.0
E1 = 4


def wait(eng, sem, value):
    if isinstance(value, int) and value <= 0:
        return
    eng.wait_ge(sem, value)


def pipeline(eng, steps, first, loop_from, loop_to, last=NG):
    for i in range(first, loop_from):
        steps(i, i % 2)
    with eng.Fori(loop_from, loop_to, 2) as i:
        steps(i, loop_from % 2)
        steps(i + 1, (loop_from + 1) % 2)
    for i in range(loop_to, last + 1):
        steps(i, i % 2)


def exists(g):
    return not isinstance(g, int) or 0 <= g < NG


def pieces():
    f32 = dict(tokw=6 * D, tokb=1, qkvw=3 * D, qb=1, kb=1, vb=4 * D, vpad=2 * D, pb=D, wp=2 * D,
               hmask=HEADS, ident=128,
               g0w=E0, g0b=E0, rev0=E0, w1=E0 * H0, b1=CH, w2=CH * D, b2=D,
               kvrw=3 * D, mix=3, wo=128, tri=T, flip=T,
               g1w=E1, g1b=E1, rev1=E1, fw1=5 * 128, fb1=5, fw2s=128, fw2e=E1 * D, fb2=3, fw3=3 * D,
               fb3=D, sb3=1)
    f16 = dict(identh=128, onesh=TP, sel0=E0 * 128, sel1=2 * 128)
    return f32, f16


def offsets(cols):
    at, out = 0, {}
    for name, n in cols.items():
        out[name] = (at, at + n)
        at += n
    return out, at



F32_AT, F32_COLS = offsets(pieces()[0])
F16_AT, F16_COLS = offsets(pieces()[1])
SPLIT = dict(qkvw=(3 * D, WSQ), g0w=(E0, WS0), w1=(E0 * H0, WS0), b2=(D, 0.5), pb=(D, 1.0),
             kvra=(3 * D, WS1), kvrb=(3 * D, WS1), g1w=(E1, WSF), fw1=(5 * 128, WSF), fb3=(D, 0.5))


def rows(g, b=0):
    return slice(g * GB + b, g * GB + b + 1) if isinstance(g, int) else bass.ds(g * GB + b, 1)


def group(g):
    return slice(g * GB, g * GB + GB) if isinstance(g, int) else bass.ds(g * GB, GB)


class Core:

    def __init__(self, nc, ctx):
        self.nc, self.ctx = nc, ctx
        self.c32 = self.sb("consts32", [128, F32_COLS])
        self.c16 = self.sb("consts16", [128, F16_COLS], F16)
        self.H = self.sb("residual", [T, B, D])
        self.bank = [ctx.enter_context(nc.psum_tensor(f"bank{i}", [128, 512], F32)) for i in range(8)]
        self.hi = {n: self.sb(f"{n}_hi", [128, w], F16) for n, (w, _) in SPLIT.items()}
        self.lo = {n: self.sb(f"{n}_lo", [128, w], F16) for n, (w, _) in SPLIT.items()}
        self.stats = self.sb("stats", [T, 2, GB, 6])
        self.both = self.sb("means_squares", [T, 2, GB, 2])
        self.apart = self.sb("means_apart", [T, 2, GB])
        self.apart2 = self.sb("means_apart_squared", [T, 2, GB])
        self.var = self.sb("variances", [T, 2, GB])
        self.vareps = self.sb("var_eps", [T, 2, GB])
        self.rstd = self.sb("rstd", [T, 2, GB])
        self.time = self.sb("time_weights", [T, T])
        self.neghalf = self.sb("neghalf", [T, GB])
        self.eps = self.sb("eps", [T, GB])
        self.xc = self.sb("centred", [T, 2, GB, D])
        self.xn = self.sb("normed", [T, 2, GB, D])
        self.xs = self.sb("norm_parts", [T, 2, GB, 2 * D], F16)

    def sb(self, name, shape, dt=F32):
        return self.ctx.enter_context(self.nc.sbuf_tensor(name, shape, dt))

    def sem(self, name):
        return self.ctx.enter_context(self.nc.semaphore(name))

    def c(self, name):
        return self.c32[:, F32_AT[name][0]:F32_AT[name][1]]

    def ch(self, name):
        return self.c16[:, F16_AT[name][0]:F16_AT[name][1]]

    def half(self, i):
        return self.bank[i][:, :].bitcast(F16)

    def turned(self, i):
        return self.half(i)[:, 0:GB * TE].rearrange("p (b t) -> p b t", b=GB)[:, :, 0:T]


class Norm:

    def __init__(self, k, phase):
        self.k, self.nc = k, k.nc
        (self.bn, self.mv, self.eps, self.rstd, self.xc, self.xn, self.hi, self.lo, self.tr) = (
            k.sem(f"{phase}_{n}") for n in ("bn", "mv", "eps", "rstd", "xc", "xn", "hi", "lo", "turned"))

    def stats(self, dve, g, p, batches=range(GB)):
        k = self.k
        if 0 in batches:
            wait(dve, self.mv, AGG * (g - 2) + 2)
        for b in batches:
            self.nc.vector.bn_stats(k.stats[:, p, b, :], k.H[:, rows(g, b), :]).then_inc(self.bn, 1)

    def aggregate(self, dve, g, p, parts=range(3)):
        k, even, odd = self.k, 1, 4
        st = k.stats[:, p, :, :]
        if 0 in parts:
            dve.wait_ge(self.bn, GB * g + GB)
            wait(dve, self.xc, g - 1)
            self.nc.vector.tensor_tensor(k.both[:, p, :, :], st[:, :, even:even + 2], st[:, :, odd:odd + 2],
                                         ALU.add).then_inc(self.mv, 1)
            self.nc.vector.tensor_tensor(k.apart[:, p, :], st[:, :, even], st[:, :, odd],
                                         ALU.subtract).then_inc(self.mv, 1)
        if 1 in parts:
            dve.wait_ge(self.mv, AGG * g + 2)
            self.nc.vector.scalar_tensor_tensor(k.apart2[:, p, :], k.apart[:, p, :], 0.25, k.apart[:, p, :],
                                                ALU.mult, ALU.mult).then_inc(self.mv, 1)
        if 2 in parts:
            dve.wait_ge(self.mv, AGG * g + 3)
            wait(dve, self.eps, g - 1)
            self.nc.vector.scalar_tensor_tensor(k.var[:, p, :], k.both[:, p, :, 1], 1.0 / D, k.apart2[:, p, :],
                                                ALU.mult, ALU.add).then_inc(self.mv, 1)

    def root(self, pool, g, p):
        k = self.k
        pool.wait_ge(self.mv, AGG * g + AGG)
        wait(pool, self.rstd, g - 1)
        self.nc.gpsimd.tensor_tensor(k.vareps[:, p, :], k.var[:, p, :], k.eps[:, :], ALU.add).then_inc(self.eps, 1)
        pool.wait_ge(self.eps, g + 1)
        wait(pool, self.xn, g - 1)
        self.nc.gpsimd.tensor_tensor(k.rstd[:, p, :], k.vareps[:, p, :], k.neghalf[:, :],
                                     ALU.pow).then_inc(self.rstd, 1)

    def centre(self, dve, g, p):
        k = self.k
        dve.wait_ge(self.mv, AGG * g + 1)
        self.nc.vector.scalar_tensor_tensor(k.xc[:, p, :, :], k.both[:, p, :, 0:1].broadcast_to([T, GB, D]), -0.5,
                                            k.H[:, group(g), :], ALU.mult, ALU.add).then_inc(self.xc, 1)

    def scale(self, dve, g, p):
        k = self.k
        dve.wait_ge(self.rstd, g + 1)
        dve.wait_ge(self.xc, g + 1)
        wait(dve, self.lo, g - 1)
        self.nc.vector.tensor_tensor(k.xn[:, p, :, :], k.xc[:, p, :, :],
                                     k.rstd[:, p, :].unsqueeze(2).broadcast_to([T, GB, D]),
                                     ALU.mult).then_inc(self.xn, 1)

    def high(self, dve, g, p):
        k = self.k
        dve.wait_ge(self.xn, g + 1)
        wait(dve, self.tr, g - 1)
        self.nc.vector.tensor_copy(k.xs[:, p, :, 0:D], k.xn[:, p, :, :]).then_inc(self.hi, 1)

    def low(self, pool, g, p):
        k = self.k
        pool.wait_ge(self.hi, g + 1)
        self.nc.gpsimd.tensor_tensor(k.xs[:, p, :, D:2 * D], k.xn[:, p, :, :], k.xs[:, p, :, 0:D],
                                     ALU.subtract).then_inc(self.lo, 1)

    def turn(self, pe, g, p, out):
        k = self.k
        pe.wait_ge(self.lo, g + 1)
        for b in range(GB):
            last = self.nc.tensor.transpose(out[:, b * TE:b * TE + T], k.xs[:, p, b, :], k.ch("identh")[0:T, 0:T])
        last.then_inc(self.tr, 1)


def embed(k, a_x, a_txt, a_tw, a_f32, a_f16):
    nc = k.nc
    with ExitStack() as ctx:
        k.ctx = ctx
        NT, KC, TT = 4, 6, 512
        pixels = k.sb("pixels", [128, NT, KC, TT])
        tokens_t = k.sb("tokens_t", [128, 2, TT])
        tokens = k.sb("tokens", [128, 2, 4, 128])
        scaled = k.sb("scaled", [128, 2, E0 * H0])
        mixed = k.sb("mixed", [128, 2, 3, D])
        onemix = k.sb("onemix", [128, 3])
        hankel = k.sb("hankel", [T, T])
        s_tw, s_flip, s_time = k.sem("time_loaded"), k.sem("time_flipped"), k.sem("time_copied")
        s_const, s_txt, s_half = k.sem("consts_loaded"), k.sem("text_loaded"), k.sem("halves_set")
        s_pix = [k.sem(f"pixels_loaded{i}") for i in range(NT)]
        s_prod, s_bias = k.sem("tokens_multiplied"), k.sem("tokens_biased")
        s_turn, s_tok, s_put = k.sem("tokens_turned"), k.sem("tokens_copied"), k.sem("tokens_put")
        s_mix, s_scl, s_spl = k.sem("weights_mixed"), k.sem("weights_scaled"), k.sem("weights_split")
        block = ctx.enter_context(nc.Block())

        @block.sync
        def _(sp):
            sp.dma_start(k.c32[:, :], a_f32).then_inc(s_const, 16)
            sp.dma_start(k.c16[:, :], a_f16).then_inc(s_const, 16)
            backwards = bass.AP(tensor=a_tw.tensor, offset=1, ap=[[1, T], [1, T]])
            sp.dma_start(hankel[:, :], backwards).then_inc(s_tw, 16)
            for i in range(NT):
                sp.dma_start(pixels[:, i, :, :], a_x[i]).then_inc(s_pix[i], 16)
            sp.dma_start(k.H[PATCHES:T, :, :], a_txt).then_inc(s_txt, 16)
            for q in range(2):
                sp.wait_ge(s_tok, q + 1)
                for s in range(2):
                    for j in range(4):
                        b = (2 * q + s) * 32 + 8 * j
                        sp.dma_start(k.H[0:PATCHES, b:b + 8, :], tokens[:, q, j, s * D:s * D + D]).then_inc(s_put, 16)
            sp.wait_ge(s_put, 16 * 16)
            sp.wait_ge(s_txt, 16)

        @block.tensor
        def _(pe):
            pe.wait_ge(s_const, 32)
            tokw = k.c("tokw").rearrange("p (c e) -> p c e", c=KC)
            pe.wait_ge(s_tw, 16)
            nc.tensor.matmul(k.bank[6][0:T, 0:T], k.c("flip")[0:T, :], hankel[:, :], start=True, stop=True).then_inc(s_flip, 1)
            for q in range(2):
                for s in range(2):
                    pe.wait_ge(s_pix[2 * q + s], 16)
                for ci in range(KC):
                    for s in range(2):
                        last = nc.tensor.matmul(k.bank[q][s * D:s * D + D, :], tokw[:, ci, :],
                                                pixels[:, 2 * q + s, ci, :], start=ci == 0, stop=ci == KC - 1)
                last.then_inc(s_prod, 1)
                pe.wait_ge(s_bias, q + 1)
                for j in range(4):
                    last = nc.tensor.transpose(k.bank[2 + q][:, j * 128:(j + 1) * 128],
                                               tokens_t[:, q, j * 128:(j + 1) * 128], k.c("ident"))
                last.then_inc(s_turn, 1)

        @block.scalar
        def _(act):
            act.wait_ge(s_const, 32)
            act.wait_ge(s_flip, 1)
            nc.scalar.activation(k.time[:, :], k.bank[6][0:T, 0:T], ACT.Copy).then_inc(s_time, 1)
            for q in range(2):
                act.wait_ge(s_prod, q + 1)
                nc.scalar.activation(tokens_t[:, q, :], k.bank[q][:, :], ACT.Identity, bias=k.c("tokb")).then_inc(s_bias, 1)
            for q in range(2):
                act.wait_ge(s_turn, q + 1)
                nc.scalar.activation(tokens[:, q, :, :].rearrange("p j e -> p (j e)"), k.bank[2 + q][:, :],
                                     ACT.Copy).then_inc(s_tok, 1)

        @block.gpsimd
        def _(pool):
            nc.gpsimd.memset(k.neghalf[:, :], -0.5).then_inc(s_half, 1)
            nc.gpsimd.memset(k.eps[:, :], EPS).then_inc(s_half, 1)
            pool.wait_ge(s_half, 2)

        @block.vector
        def _(dve):
            dve.wait_ge(s_const, 32)
            nc.vector.tensor_scalar(onemix[:, :], k.c("mix"), -1.0, 1.0, ALU.mult, ALU.add).then_inc(s_mix, 1)
            dve.wait_ge(s_mix, 1)
            for m, mix in enumerate((k.c("mix"), onemix[:, :])):
                for n in range(3):
                    nc.vector.tensor_scalar(mixed[:, m, n, :], k.c("kvrw")[:, n * D:(n + 1) * D], mix[:, n:n + 1], None,
                                            ALU.mult).then_inc(s_mix, 1)
            dve.wait_ge(s_mix, 7)
            for name, by in (("vb", WSQ), ("vpad", WSQ), ("wp", 1 / WSQ)):
                nc.vector.tensor_scalar(k.c(name), k.c(name), by, None, ALU.mult).then_inc(s_mix, 1)
            for e in (1, 3):
                for w, by in ((k.c("fb1")[:, 1 + e:2 + e], WSF), (k.c("fw2e")[:, e * D:(e + 1) * D], 1 / WSF)):
                    nc.vector.tensor_scalar(w, w, by, None, ALU.mult).then_inc(s_mix, 1)
            for n, (name, (w, by)) in enumerate(SPLIT.items()):
                src = mixed[:, name == "kvrb", :, :].rearrange("p n e -> p (n e)") if name[:3] == "kvr" else k.c(name)
                wait(dve, s_spl, 2 * (n - 1))
                nc.vector.tensor_scalar(scaled[:, n % 2, 0:w], src, by, None, ALU.mult).then_inc(s_scl, 1)
                dve.wait_ge(s_scl, n + 1)
                nc.vector.tensor_copy(k.hi[name][:, :], scaled[:, n % 2, 0:w]).then_inc(s_spl, 1)
                dve.wait_ge(s_spl, 2 * n + 1)
                nc.vector.tensor_tensor(k.lo[name][:, :], scaled[:, n % 2, 0:w], k.hi[name][:, :],
                                        ALU.subtract).then_inc(s_spl, 1)


def attend(k):
    nc = k.nc
    with ExitStack() as ctx:
        k.ctx = ctx
        n = Norm(k, "a")
        xt = k.sb("a_xt", [128, 2, N], F16)
        qd = k.sb("a_q", [128, 2, 2, 2 * TP])
        ks = k.sb("a_k", [128, 2, 2, T + 1])
        km = k.sb("a_kmask", [128, 2, 2, HEADS, T + 1])
        v0 = k.sb("a_v0", [128, 2, 2, 4, 2, 16])
        v1 = k.sb("a_v1", [128, 2, 2, 4, 2, 16])
        mx = k.sb("a_max", [128, 2, 3, HEADS])
        e0 = k.sb("a_e0", [128, 2, 2, HEADS, WIN])
        e1 = k.sb("a_e1", [128, 2, HEADS, 32])
        sm = k.sb("a_sum", [128, 2, 3, HEADS])
        rs = k.sb("a_rsum", [128, 2, 3, HEADS])
        p0 = k.sb("a_p0t", [128, 2, 2, 512])
        p1 = k.sb("a_p1t", [128, 2, 256])
        ot = k.sb("a_ot", [128, 2, 384])
        S0, SW, TA, TB_, O, QK, XV = 0, 2, 3, 4, 5, 6, 7
        bank = k.bank
        (s_set, s_xt, s_qk, s_q, s_k, s_km, s_v, s_ve, s_s, s_mx, s_sub, s_exp, s_pad, s_sum, s_rs, s_p, s_pt, s_pe,
         s_o, s_oe, s_y, s_h) = (k.sem("a_" + x) for x in (
             "buffers_set", "x_columns", "qk_multiplied", "q_placed", "k_placed", "k_masked", "v_multiplied",
             "v_placed", "scores", "maxima", "less_max", "exps", "padding_weighted", "sums", "inverses", "probs",
             "probs_turned", "probs_t_copied", "gathered", "gathered_copied", "projected", "added"))
        block = ctx.enter_context(nc.Block())
        VE = 6
        SETS = 7
        hq, lq = k.hi["qkvw"], k.lo["qkvw"]

        def pair_cols(ap):
            return ap.rearrange("p (q s t) -> p q s t", q=2, s=2)

        @block.tensor
        def _(pe):
            def values(g, p):
                if not exists(g):
                    return
                pe.wait_ge(s_xt, g + 1)
                for b in range(GB):
                    for m, w in enumerate((hq, lq)):
                        out = bank[XV][0:T, 0:GB * D].rearrange("p (q j s f) -> p q s j f", q=2, j=4, s=2)
                        last = nc.tensor.matmul(out[:, b // 2, b % 2, :, :], xt[:, p, b * T:(b + 1) * T],
                                                w[:, 2 * D:3 * D], start=m == 0, stop=m == 1)
                last.then_inc(s_v, 1)

            def scores(g, p):
                if not exists(g):
                    return
                pe.wait_ge(s_q, 4 * g + 4)
                for q in range(2):
                    pe.wait_ge(s_km, 2 * g + q + 1)
                    wait(pe, s_sub, 3 * (g - 1) + q + 1)
                    nc.tensor.matmul(bank[S0 + q][:, :], qd[:, p, q, 0:2 * WIN],
                                     km[:, p, q, :, 0:WIN], start=True, stop=True).then_inc(s_s, 1)
                wait(pe, s_sub, 3 * g)
                for q in range(2):
                    last = nc.tensor.matmul(bank[SW][q * WIN:(q + 1) * WIN, 0:HEADS * W1K],
                                            qd[:, p, q, 2 * WIN:2 * TP],
                                            km[:, p, q, :, WIN:T + 1], start=True, stop=True)
                last.then_inc(s_s, 1)

            def project(g, p):
                if not exists(g):
                    return
                pe.wait_ge(s_oe, g + 1)
                pe.wait_ge(s_pe, 3 * g + 2)
                nc.tensor.matmul(bank[TB_][0:TP, 0:GB * D], k.ch("onesh"), k.hi["pb"][:, :].unsqueeze(1).broadcast_to([128, GB, D]),
                                 start=True, stop=False)
                nc.tensor.matmul(bank[TB_][0:TP, 0:GB * D], k.ch("onesh"), k.lo["pb"][:, :].unsqueeze(1).broadcast_to([128, GB, D]),
                                 start=False, stop=True)
                for b in range(GB):
                    q, s = b // 2, b % 2
                    y = bank[TB_][:, b * D:(b + 1) * D]
                    nc.tensor.matmul(y[0:WIN], ot[:, p, q * 128 + s * WIN:][:, 0:WIN], k.c("wp")[:, s * D:(s + 1) * D],
                                     start=False, stop=True, skip_group_check=True)
                    last = nc.tensor.matmul(y[WIN:TP], ot[:, p, 256 + q * 64 + s * 32:][:, 0:32],
                                            k.c("wp")[:, s * D:(s + 1) * D], start=False, stop=True,
                                            skip_group_check=True)
                last.then_inc(s_y, 1)

            def columns(g, p):
                if not exists(g):
                    return
                wait(pe, s_ve, VE * g)
                n.turn(pe, g, p, k.half(XV))

            def queries_keys(g, p):
                if not exists(g):
                    return
                pe.wait_ge(s_xt, g + 1)
                wait(pe, s_q, 4 * g)
                wait(pe, s_k, g)
                cols = pair_cols(xt[:, p, :])
                for m in range(2):
                    for s in range(2):
                        for i, w in enumerate((hq, lq)):
                            last = nc.tensor.matmul(bank[QK][s * D:(s + 1) * D, m * 2 * T:(m + 1) * 2 * T],
                                                    w[:, m * D:(m + 1) * D], cols[:, :, s, :], start=i == 0, stop=i == 1)
                last.then_inc(s_qk, 1)

            def turn_probs(g, p, part):
                if not exists(g):
                    return
                pe.wait_ge(s_p, 3 * g + part + 1)
                if part == 0:
                    wait(pe, s_pe, 3 * g)
                if part == 1:
                    wait(pe, s_h, g)
                if part == 2:
                    pe.wait_ge(s_pe, 3 * g + 1)
                if part < 2:
                    e = e0[:, p, part, :, :].rearrange("p h w -> p (h w)")
                    at = bank[TA if part == 0 else TB_]
                    for j in range(4):
                        last = nc.tensor.transpose(at[:, j * 128:(j + 1) * 128], e[:, j * 128:(j + 1) * 128], k.c("ident"))
                else:
                    e = e1[:, p, :, :].rearrange("p h w -> p (h w)")
                    for j in range(2):
                        last = nc.tensor.transpose(bank[TA][:, j * 128:(j + 1) * 128], e[:, j * 128:(j + 1) * 128], k.c("ident"))
                last.then_inc(s_pt, 1)

            def gather(g, p):
                if not exists(g):
                    return
                pe.wait_ge(s_ve, VE * g + VE)
                wait(pe, s_oe, g)
                for q in range(2):
                    pe.wait_ge(s_pe, 3 * g + q + 1)
                    for j in range(4):
                        nc.tensor.matmul(bank[O][32 * j:32 * j + 32, q * 128:(q + 1) * 128], v0[:, p, q, j, :, :].rearrange("p s f -> p (s f)"),
                                         p0[:, p, q, j * 128:(j + 1) * 128], start=True, stop=True)
                pe.wait_ge(s_pe, 3 * g + 3)
                for q in range(2):
                    for j in range(2):
                        last = nc.tensor.matmul(bank[O][64 * j:64 * j + 64, 256 + q * 64:256 + (q + 1) * 64],
                                                v1[:, p, q, 2 * j:2 * j + 2, :, :].rearrange("p j s f -> p (j s f)"),
                                                p1[:, p, j * 128 + q * 64:j * 128 + (q + 1) * 64], start=True, stop=True)
                last.then_inc(s_o, 1)

            def steps(i, p):
                values(i + 1, 1 - p)
                scores(i + 1, 1 - p)
                project(i - 1, 1 - p)
                columns(i + 2, p)
                turn_probs(i, p, 0)
                queries_keys(i + 2, p)
                turn_probs(i, p, 1)
                turn_probs(i, p, 2)
                gather(i, p)

            pe.wait_ge(s_set, SETS)
            pipeline(pe, steps, -3, 2, NG - 4)

        @block.scalar
        def _(act):
            def columns(g, p):
                if not exists(g):
                    return
                act.wait_ge(n.tr, g + 1)
                wait(act, s_qk, g - 1)
                wait(act, s_v, g - 1)
                nc.scalar.activation(xt[:, p, :].rearrange("p (b t) -> p b t", b=GB),
                                     k.turned(XV), ACT.Copy).then_inc(s_xt, 1)

            def place(g, p):
                if not exists(g):
                    return
                act.wait_ge(s_qk, g + 1)
                wait(act, s_s, 3 * (g - 1))
                for s in range(2):
                    src = bank[QK][s * D:(s + 1) * D, 0:2 * T].rearrange("p (q t) -> p q t", q=2)
                    for at, t, w in ((s * WIN, 0, WIN), (2 * WIN + s * 32, WIN, W1Q)):
                        nc.scalar.activation(qd[s * D:(s + 1) * D, p, :, at:at + w], src[:, :, t:t + w], ACT.Identity,
                                             bias=k.c("qb")[s * D:(s + 1) * D], scale=1.0 / WSQ).then_inc(s_q, 1)
                wait(act, s_km, 2 * (g - 1))
                nc.scalar.activation(ks[:, p, :, 0:T], bank[QK][:, 2 * T:4 * T].rearrange("p (q t) -> p q t", q=2),
                                     ACT.Identity, bias=k.c("kb"), scale=1.0 / WSQ).then_inc(s_k, 1)

            def exps(g, p, part):
                if not exists(g):
                    return
                act.wait_ge(s_sub, 3 * g + part + 1)
                e = e0[:, p, part, :, :] if part < 2 else e1[:, p, :, 0:W1K]
                nc.scalar.activation(e, e, ACT.Exp, scale=SCALE).then_inc(s_exp, 1)

            def copy_probs(g, p, part):
                if not exists(g):
                    return
                act.wait_ge(s_pt, 3 * g + part + 1)
                wait(act, s_o, g - 1)
                if part < 2:
                    nc.scalar.activation(p0[:, p, part, :], bank[TA if part == 0 else TB_][:, :], ACT.Copy).then_inc(s_pe, 1)
                else:
                    nc.scalar.activation(p1[:, p, :], bank[TA][:, 0:256], ACT.Copy).then_inc(s_pe, 1)

            def copy_gathered(g, p):
                if not exists(g):
                    return
                act.wait_ge(s_o, g + 1)
                wait(act, s_y, g - 1)
                nc.scalar.activation(ot[:, p, :], bank[O][:, 0:384], ACT.Copy).then_inc(s_oe, 1)

            def steps(i, p):
                columns(i + 2, p)
                copy_probs(i, p, 0)
                exps(i + 1, 1 - p, 0)
                place(i + 2, p)
                copy_probs(i, p, 1)
                exps(i + 1, 1 - p, 1)
                copy_probs(i, p, 2)
                exps(i + 1, 1 - p, 2)
                copy_gathered(i, p)

            act.wait_ge(s_set, SETS)
            pipeline(act, steps, -3, 2, NG - 4)

        @block.gpsimd
        def _(pool):
            def mask_keys(g, p):
                if not exists(g):
                    return
                pool.wait_ge(s_k, g + 1)
                wait(pool, s_s, 3 * (g - 1))
                for q in range(2):
                    nc.gpsimd.tensor_tensor(km[:, p, q, :, :], ks[:, p, q, :].unsqueeze(1).broadcast_to([128, HEADS, T + 1]),
                                            k.c("hmask").unsqueeze(2).broadcast_to([128, HEADS, T + 1]),
                                            ALU.mult).then_inc(s_km, 1)

            def probs(g, p, part):
                if not exists(g):
                    return
                pool.wait_ge(s_rs, 3 * g + part + 1)
                e, w = (e0[:, p, part, :, :], WIN) if part < 2 else (e1[:, p, :, 0:W1K], W1K)
                nc.gpsimd.tensor_tensor(e, e, rs[:, p, part, :].unsqueeze(2).broadcast_to([128, HEADS, w]),
                                        ALU.mult).then_inc(s_p, 1)

            def steps(i, p):
                if exists(i + 3):
                    n.root(pool, i + 3, 1 - p)
                mask_keys(i + 2, p)
                probs(i + 1, 1 - p, 0)
                if exists(i + 3):
                    n.low(pool, i + 3, 1 - p)
                probs(i + 1, 1 - p, 1)
                probs(i + 1, 1 - p, 2)

            nc.gpsimd.memset(qd[:, :, :, :].rearrange("p a b c -> p (a b c)"), 0.0).then_inc(s_set, 1)
            nc.gpsimd.memset(v0[:, :, :, :, :, :].rearrange("p a b c d e -> p (a b c d e)"), 0.0).then_inc(s_set, 1)
            nc.gpsimd.memset(e1[:, :, :, :].rearrange("p a b c -> p (a b c)"), 0.0).then_inc(s_set, 1)
            for p in range(2):
                nc.gpsimd.tensor_copy(ks[:, p, :, T:T + 1], k.c("kb").unsqueeze(1).broadcast_to([128, 2, 1])).then_inc(s_set, 1)
                nc.gpsimd.tensor_copy(v1[:, p, :, :, :, :].rearrange("p q j s f -> p q (j s f)"),
                                      k.c("vpad").unsqueeze(1).broadcast_to([128, 2, 2 * D])).then_inc(s_set, 1)
            pool.wait_ge(s_set, SETS)
            pipeline(pool, steps, -3, 2, NG - 4)

        @block.vector
        def _(dve):
            def place_values(g, p):
                if not exists(g):
                    return
                dve.wait_ge(s_v, g + 1)
                wait(dve, s_o, g - 1)
                v = bank[XV][:, 0:GB * D].rearrange("p (j f) -> p j f", f=16)
                vb = k.c("vb").rearrange("p (j f) -> p j f", f=16)
                for h in range(2):
                    own = slice(h * HD, h * HD + HD)
                    dst = v0[h * WIN:(h + 1) * WIN, p, :, :, :, :].rearrange("p q j s f -> p (q j s) f")
                    nc.vector.tensor_tensor(dst[:, :, own], v[0:WIN, :, own], vb[0:WIN, :, own], ALU.add).then_inc(s_ve, 1)
                v = bank[XV][:, 0:GB * D].rearrange("p (i r s f) -> p i r s f", r=2, s=2, f=16)
                vb = k.c("vb").rearrange("p (i r s f) -> p i r s f", r=2, s=2, f=16)
                for h in range(4):
                    own, r = slice(h % 2 * HD, h % 2 * HD + HD), h // 2
                    dst = v1[32 * h:32 * h + W1Q, p, :, :, :, :].rearrange("p q (i r) s f -> p (q i) r s f", i=2)
                    nc.vector.tensor_tensor(dst[:, :, r, :, own], v[WIN:T, :, r, :, own], vb[WIN:T, :, r, :, own],
                                            ALU.add).then_inc(s_ve, 1)

            def maxima(g, p, part):
                if not exists(g):
                    return
                dve.wait_ge(s_s, 3 * g + part + 1)
                src = bank[S0 + part][:, :].rearrange("p (h w) -> p h w", h=HEADS) if part < 2 else \
                    bank[SW][:, 0:HEADS * W1K].rearrange("p (h w) -> p h w", h=HEADS)
                nc.vector.tensor_reduce(mx[:, p, part, :], src, X, ALU.max).then_inc(s_mx, 1)

            def less_max(g, p, part):
                if not exists(g):
                    return
                dve.wait_ge(s_mx, 3 * g + part + 1)
                wait(dve, s_pt, 3 * (g - 2) + part + 1)
                w = WIN if part < 2 else W1K
                src = bank[(S0 + part) if part < 2 else SW][:, 0:HEADS * w].rearrange("p (h w) -> p h w", h=HEADS)
                dst = e0[:, p, part, :, :] if part < 2 else e1[:, p, :, 0:W1K]
                nc.vector.tensor_tensor(dst, src, mx[:, p, part, :].unsqueeze(2).broadcast_to([128, HEADS, w]),
                                        ALU.subtract).then_inc(s_sub, 1)

            def weigh_padding(g, p):
                if not exists(g):
                    return
                dve.wait_ge(s_exp, 3 * g + 3)
                nc.vector.tensor_scalar(e1[:, p, :, W1Q], e1[:, p, :, W1Q], float(PADS), None, ALU.mult).then_inc(s_pad, 1)

            def sums(g, p, part):
                if not exists(g):
                    return
                dve.wait_ge(s_exp, 3 * g + part + 1)
                if part == 2:
                    dve.wait_ge(s_pad, g + 1)
                e = e0[:, p, part, :, :] if part < 2 else e1[:, p, :, 0:W1K]
                nc.vector.tensor_reduce(sm[:, p, part, :], e, X, ALU.add).then_inc(s_sum, 1)

            def inverses(g, p, part):
                if not exists(g):
                    return
                dve.wait_ge(s_sum, 3 * g + part + 1)
                wait(dve, s_p, 3 * (g - 2) + part + 1)
                nc.vector.reciprocal(rs[:, p, part, :], sm[:, p, part, :]).then_inc(s_rs, 1)

            def add(g, p):
                if not exists(g):
                    return
                dve.wait_ge(s_y, g + 1)
                nc.vector.tensor_tensor(k.H[:, group(g), :], k.H[:, group(g), :],
                                        bank[TB_][0:T, 0:GB * D].rearrange("p (b e) -> p b e", b=GB), ALU.add).then_inc(s_h, 1)

            def steps(i, p):
                place_values(i + 1, 1 - p)
                maxima(i + 1, 1 - p, 0)
                if exists(i + 3):
                    n.stats(dve, i + 3, 1 - p)
                less_max(i + 1, 1 - p, 0)
                maxima(i + 1, 1 - p, 1)
                if exists(i + 3):
                    n.aggregate(dve, i + 3, 1 - p)
                less_max(i + 1, 1 - p, 1)
                maxima(i + 1, 1 - p, 2)
                if exists(i + 3):
                    n.centre(dve, i + 3, 1 - p)
                less_max(i + 1, 1 - p, 2)
                add(i - 1, 1 - p)
                if exists(i + 3):
                    n.scale(dve, i + 3, 1 - p)
                sums(i + 1, 1 - p, 0)
                if exists(i + 3):
                    n.high(dve, i + 3, 1 - p)
                inverses(i + 1, 1 - p, 0)
                sums(i + 1, 1 - p, 1)
                weigh_padding(i + 1, 1 - p)
                inverses(i + 1, 1 - p, 1)
                sums(i + 1, 1 - p, 2)
                inverses(i + 1, 1 - p, 2)

            dve.wait_ge(s_set, SETS)
            pipeline(dve, steps, -3, 2, NG - 4)


class Gate:

    def __init__(self, k, phase, experts, weight_scale, softmax_first, weights, bias, rev):
        self.k, self.nc, self.E, self.by, self.soft = k, k.nc, experts, weight_scale, softmax_first
        self.w, self.bias, self.rev = weights, k.c(bias), k.c(rev)
        s = [T, GB, experts]
        (self.logits, self.equal, self.first, self.left, self.second, self.gates, self.either, self.sign, self.tilt,
         self.dense) = (k.sb(f"{phase}_{name}", s) for name in (
             "logits", "equal", "first", "left", "second", "gates", "either", "sign", "tilt", "dense"))
        (self.top, self.rank, self.top2, self.rank2, self.gap, self.half_tanh, self.total, self.inverse) = (
            k.sb(f"{phase}_{name}", [T, GB]) for name in (
                "top", "rank", "top2", "rank2", "gap", "half_tanh", "total", "inverse"))
        self.parts = k.sb(f"{phase}_parts", [T, GB, 128], F16)
        self.wt = k.sb(f"{phase}_wt", [128, 2, N], F16)
        (self.s_log, self.s_dve, self.s_act, self.s_pool, self.s_tr, self.s_wt, self.s_zero) = (
            k.sem(f"{phase}_g_" + n) for n in ("logits", "chain", "acted", "weighed", "turned", "placed", "zeroed"))
        self.OPS = 18 if softmax_first else 13
        self.ACTS = 2 if softmax_first else 1
        self.POOLS = 6

    def over(self, ap):
        return ap[:, :].unsqueeze(2).broadcast_to([T, GB, self.E])

    def multiply(self, pe, g, xt, out):
        for b in range(GB):
            for m, w in enumerate(self.w):
                last = self.nc.tensor.matmul(out[0:T, b * self.E:(b + 1) * self.E], xt[:, b * T:(b + 1) * T],
                                             w[:, 0:self.E], start=m == 0, stop=m == 1)
        last.then_inc(self.s_log, 1)

    def choose(self, dve, g, out, ops):
        v, E = self.nc.vector, self.E
        every = self.bias[0:T].unsqueeze(1).broadcast_to([T, GB, E])
        rev = self.rev[0:T].unsqueeze(1).broadcast_to([T, GB, E])
        logits = out[0:T, 0:GB * E].rearrange("p (b e) -> p b e", b=GB)
        gates = self.gates if self.soft else self.logits
        for o in ops:
            if o == 0:
                dve.wait_ge(self.s_log, g + 1)
                v.scalar_tensor_tensor(self.logits[:, :, :], logits, 1.0 / self.by, every, ALU.mult,
                                       ALU.add).then_inc(self.s_dve, 1)
                continue
            dve.wait_ge(self.s_dve, self.OPS * g + o)
            if self.soft and o <= 5:
                if o == 1:
                    v.tensor_reduce(self.top[:, :], self.logits[:, :, :], X, ALU.max).then_inc(self.s_dve, 1)
                if o == 2:
                    v.tensor_tensor(self.gates[:, :, :], self.logits[:, :, :], self.over(self.top),
                                    ALU.subtract).then_inc(self.s_dve, 1)
                if o == 3:
                    dve.wait_ge(self.s_act, self.ACTS * g + 1)
                    v.tensor_reduce(self.total[:, :], self.gates[:, :, :], X, ALU.add).then_inc(self.s_dve, 1)
                if o == 4:
                    v.reciprocal(self.inverse[:, :], self.total[:, :]).then_inc(self.s_dve, 1)
                if o == 5:
                    v.tensor_tensor(self.gates[:, :, :], self.gates[:, :, :], self.over(self.inverse),
                                    ALU.mult).then_inc(self.s_dve, 1)
                continue
            step = o - 5 if self.soft else o
            if step == 1:
                v.tensor_reduce(self.top[:, :], gates[:, :, :], X, ALU.max).then_inc(self.s_dve, 1)
            if step == 2:
                v.tensor_tensor(self.equal[:, :, :], gates[:, :, :], self.over(self.top),
                                ALU.is_equal).then_inc(self.s_dve, 1)
            if step == 3:
                v.tensor_tensor(self.equal[:, :, :], self.equal[:, :, :], rev, ALU.mult).then_inc(self.s_dve, 1)
            if step == 4:
                v.tensor_reduce(self.rank[:, :], self.equal[:, :, :], X, ALU.max).then_inc(self.s_dve, 1)
            if step == 5:
                wait(dve, self.s_pool, self.POOLS * g)
                v.tensor_tensor(self.first[:, :, :], self.equal[:, :, :], self.over(self.rank),
                                ALU.is_equal).then_inc(self.s_dve, 1)
            if step == 6:
                v.scalar_tensor_tensor(self.left[:, :, :], self.first[:, :, :], -3e38, gates[:, :, :], ALU.mult,
                                       ALU.add).then_inc(self.s_dve, 1)
            if step == 7:
                v.tensor_reduce(self.top2[:, :], self.left[:, :, :], X, ALU.max).then_inc(self.s_dve, 1)
            if step == 8:
                v.tensor_tensor(self.gap[:, :], self.top[:, :], self.top2[:, :], ALU.subtract).then_inc(self.s_dve, 1)
            if step == 9:
                v.tensor_tensor(self.equal[:, :, :], self.left[:, :, :], self.over(self.top2),
                                ALU.is_equal).then_inc(self.s_dve, 1)
            if step == 10:
                v.tensor_tensor(self.equal[:, :, :], self.equal[:, :, :], rev, ALU.mult).then_inc(self.s_dve, 1)
            if step == 11:
                v.tensor_reduce(self.rank2[:, :], self.equal[:, :, :], X, ALU.max).then_inc(self.s_dve, 1)
            if step == 12:
                v.tensor_tensor(self.second[:, :, :], self.equal[:, :, :], self.over(self.rank2),
                                ALU.is_equal).then_inc(self.s_dve, 1)

    def exponentiate(self, act, g):
        act.wait_ge(self.s_dve, self.OPS * g + 3)
        self.nc.scalar.activation(self.gates[:, :, :], self.gates[:, :, :], ACT.Exp).then_inc(self.s_act, 1)

    def tanh(self, act, g):
        act.wait_ge(self.s_dve, self.OPS * g + self.OPS - 4)
        self.nc.scalar.activation(self.half_tanh[:, :], self.gap[:, :], ACT.Tanh, scale=0.5).then_inc(self.s_act, 1)

    def weigh(self, pool, g):
        v, E, at = self.nc.gpsimd, self.E, self.POOLS * g
        pool.wait_ge(self.s_act, self.ACTS * g + self.ACTS)
        pool.wait_ge(self.s_dve, self.OPS * g + self.OPS)
        v.tensor_tensor(self.either[:, :, :], self.first[:, :, :], self.second[:, :, :], ALU.add).then_inc(self.s_pool, 1)
        v.tensor_tensor(self.sign[:, :, :], self.first[:, :, :], self.second[:, :, :], ALU.subtract).then_inc(self.s_pool, 1)
        pool.wait_ge(self.s_pool, at + 2)
        v.tensor_tensor(self.tilt[:, :, :], self.sign[:, :, :], self.over(self.half_tanh), ALU.mult).then_inc(self.s_pool, 1)
        pool.wait_ge(self.s_pool, at + 3)
        v.tensor_tensor(self.dense[:, :, :], self.either[:, :, :], self.tilt[:, :, :], ALU.add).then_inc(self.s_pool, 1)
        wait(pool, self.s_tr, g)
        v.tensor_tensor(self.parts[:, :, 0:E], self.either[:, :, :], self.tilt[:, :, :], ALU.add).then_inc(self.s_pool, 1)
        pool.wait_ge(self.s_pool, at + 5)
        v.tensor_tensor(self.parts[:, :, E:2 * E], self.dense[:, :, :], self.parts[:, :, 0:E], ALU.subtract).then_inc(self.s_pool, 1)

    def turn(self, pe, g, out):
        pe.wait_ge(self.s_pool, self.POOLS * g + self.POOLS)
        for b in range(GB):
            last = self.nc.tensor.transpose(out[:, b * TE:b * TE + T], self.parts[:, b, :], self.k.ch("identh")[0:T, 0:T])
        last.then_inc(self.s_tr, 1)

    def place(self, act, g, p, turned):
        act.wait_ge(self.s_tr, g + 1)
        self.nc.scalar.activation(self.wt[:, p, :].rearrange("p (b t) -> p b t", b=GB), turned, ACT.Copy).then_inc(self.s_wt, 1)


def columns_of(ap):
    return ap.rearrange("p (b t) -> p b t", b=GB)


def mix_experts(k):
    nc = k.nc
    with ExitStack() as ctx:
        k.ctx = ctx
        n = Norm(k, "e")
        gate = Gate(k, "e", E0, WS0, False, (k.hi["g0w"], k.lo["g0w"]), "g0b", "rev0")
        AHEAD, RING = 2, 4
        xt = k.sb("e_xt", [128, 2, N], F16)
        hid = k.sb("e_hidden", [128, RING, N])
        wh = k.sb("e_weighed", [128, RING, N])
        yt = k.sb("e_yt", [128, 2, N // 2])
        HB, WB, YB, XB, TB_ = 0, 2, 4, 6, 7
        bank = k.bank
        s_xt, s_h, s_g, s_wb, s_z, s_y, s_y2, s_yt, s_ytr, s_add = (k.sem("e_" + x) for x in (
            "x_columns", "hidden", "gelus", "weights_spread", "weighed", "chunks_added", "outputs", "outputs_copied",
            "outputs_turned", "added"))
        block = ctx.enter_context(nc.Block())
        w2 = k.c("w2").rearrange("p (c e) -> p c e", c=CH)
        b1 = k.c("b1")
        sel = k.ch("sel0").rearrange("p (e m) -> p e m", e=E0)

        @block.tensor
        def _(pe):
            def first(g, p, c):
                if not exists(g):
                    return
                if c == 0:
                    pe.wait_ge(s_xt, g + 1)
                wait(pe, s_g, CH * g + c - 1)
                for m, w in enumerate((k.hi["w1"], k.lo["w1"])):
                    last = nc.tensor.matmul(bank[HB + c % 2][:, 0:N], w[:, c * 128:(c + 1) * 128], xt[:, p, :],
                                            start=m == 0, stop=m == 1)
                last.then_inc(s_h, 1)

            def spread(g, p, e):
                if not exists(g):
                    return
                if e == 0:
                    pe.wait_ge(gate.s_wt, g + 1)
                wait(pe, s_z, CH * g + 2 * e - 2)
                nc.tensor.matmul(bank[WB + e % 2][:, 0:N], sel[:, e, :], gate.wt[:, p, :], start=True, stop=True).then_inc(s_wb, 1)

            def second(g, p, c):
                if not exists(g):
                    return
                pe.wait_ge(s_z, CH * g + c + 1)
                if c == 0:
                    wait(pe, s_yt, g - 1)
                for s in range(2):
                    last = nc.tensor.matmul(bank[YB + p][s * D:(s + 1) * D, 0:N // 2], w2[:, c, :],
                                            wh[:, c % RING, s * (N // 2):(s + 1) * (N // 2)], start=c == 0, stop=False)
                last.then_inc(s_y, 1)

            def biases(g, p):
                if not exists(g):
                    return
                for m, w in enumerate((k.hi["b2"], k.lo["b2"])):
                    for s in range(2):
                        last = nc.tensor.matmul(bank[YB + p][s * D:(s + 1) * D, 0:N // 2], w[:, :],
                                                gate.wt[:, p, s * (N // 2):(s + 1) * (N // 2)], start=False, stop=m == 1)
                last.then_inc(s_y2, 1)

            def turn_outputs(g, p):
                if not exists(g):
                    return
                pe.wait_ge(s_yt, g + 1)
                for b in range(2):
                    last = nc.tensor.transpose(bank[TB_][0:T, b * 128:(b + 1) * 128], yt[:, p, b * T:(b + 1) * T], k.c("ident"))
                last.then_inc(s_ytr, 1)

            def steps(i, p):
                q = 1 - p
                for c in range(CH):
                    ahead = c + AHEAD
                    first(i if ahead < CH else i + 1, p if ahead < CH else q, ahead % CH)
                    if c == 0 and exists(i + 1):
                        wait(pe, gate.s_dve, gate.OPS * (i + 1) - gate.OPS + 1)
                        n.turn(pe, i + 1, q, k.half(XB))
                    if c == 2 and exists(i + 1):
                        pe.wait_ge(s_xt, i + 2)
                        gate.multiply(pe, i + 1, xt[:, q, :], bank[XB])
                    if c == 3:
                        turn_outputs(i - 1, q)
                    if c == 12 and exists(i + 1):
                        wait(pe, s_add, i)
                        gate.turn(pe, i + 1, k.half(TB_))
                    if c % 2 == 0:
                        e = c // 2 + 1
                        spread(i if e < E0 else i + 1, p if e < E0 else q, e % E0)
                    second(i, p, c)
                biases(i, p)

            pe.wait_ge(gate.s_zero, 1)
            pipeline(pe, steps, -1, 2, NG - 4)

        @block.scalar
        def _(act):
            def gelu(g, p, c):
                if not exists(g):
                    return
                act.wait_ge(s_h, CH * g + c + 1)
                wait(act, s_z, CH * g + c - RING + 1)
                nc.scalar.activation(hid[:, c % RING, :], bank[HB + c % 2][:, 0:N], ACT.Gelu, bias=b1[:, c:c + 1],
                                     scale=1.0 / WS0).then_inc(s_g, 1)

            def steps(i, p):
                q = 1 - p
                for c in range(CH):
                    ahead = c + AHEAD
                    gelu(i if ahead < CH else i + 1, p if ahead < CH else q, ahead % CH)
                    if c == 0 and exists(i - 1):
                        act.wait_ge(s_y2, i)
                        wait(act, s_ytr, i - 2)
                        nc.scalar.activation(yt[:, q, :], bank[YB + q][:, 0:N // 2], ACT.Copy).then_inc(s_yt, 1)
                    if c == 0 and exists(i + 1):
                        act.wait_ge(n.tr, i + 2)
                        wait(act, s_h, CH * i)
                        wait(act, gate.s_log, i)
                        nc.scalar.activation(columns_of(xt[:, q, :]), k.turned(XB), ACT.Copy).then_inc(s_xt, 1)
                    if c == 8 and exists(i + 1):
                        gate.tanh(act, i + 1)
                    if c == 12 and exists(i + 1):
                        wait(act, s_y2, i)
                        gate.place(act, i + 1, q, k.turned(TB_))

            pipeline(act, steps, -1, 2, NG - 4)

        @block.gpsimd
        def _(pool):
            def steps(i, p):
                q = 1 - p
                if exists(i + 1):
                    gate.weigh(pool, i + 1)
                if exists(i + 2):
                    n.root(pool, i + 2, p)
                    n.low(pool, i + 2, p)

            nc.gpsimd.memset(gate.parts[:, :, :].rearrange("p b c -> p (b c)"), 0.0).then_inc(gate.s_zero, 1)
            pool.wait_ge(gate.s_zero, 1)
            pipeline(pool, steps, -2, 2, NG - 4)

        @block.vector
        def _(dve):
            def weigh(g, c):
                if not exists(g):
                    return
                dve.wait_ge(s_g, CH * g + c + 1)
                if c % 2 == 0:
                    dve.wait_ge(s_wb, E0 * g + c // 2 + 1)
                wait(dve, s_y, CH * g + c - RING + 1)
                nc.vector.tensor_tensor(wh[:, c % RING, :], hid[:, c % RING, :], bank[WB + c // 2 % 2][:, 0:N],
                                        ALU.mult).then_inc(s_z, 1)

            def steps(i, p):
                q = 1 - p
                for c in range(CH):
                    weigh(i, c)
                    if 2 <= c < 9 and exists(i + 1):
                        gate.choose(dve, i + 1, bank[XB], range(2 * c - 4, min(2 * c - 2, gate.OPS)))
                    if c == 5 and exists(i - 1):
                        dve.wait_ge(s_ytr, i)
                        out = bank[TB_][0:T, 0:GB * D].rearrange("p (b s e) -> p s b e", b=2, s=2)
                        h = k.H[:, group(i - 1), :].rearrange("p (s b) e -> p s b e", s=2)
                        nc.vector.tensor_tensor(h, h, out, ALU.add).then_inc(s_add, 1)
                    if exists(i + 2):
                        if c == 9:
                            n.stats(dve, i + 2, p)
                        if c == 10:
                            n.aggregate(dve, i + 2, p)
                        if c == 11:
                            n.centre(dve, i + 2, p)
                        if c == 14:
                            n.scale(dve, i + 2, p)
                        if c == 15:
                            n.high(dve, i + 2, p)

            pipeline(dve, steps, -2, 2, NG - 4)


def mix_time(k):
    nc = k.nc
    with ExitStack() as ctx:
        k.ctx = ctx
        n = Norm(k, "t")
        xt = k.sb("t_xt", [128, 2, GB, TE], F16)
        kc = k.sb("t_clipped", [T, 2, GB, D])
        ek = k.sb("t_exp_k", [T, 2, GB, D])
        er = k.sb("t_exp_r", [T, 2, GB, D])
        v = k.sb("t_v", [T, 2, GB, D])
        kv = k.sb("t_kv", [T, 2, GB, D])
        den = k.sb("t_den", [T, GB, D])
        inv = k.sb("t_inv", [T, GB, D])
        rw = k.sb("t_rw", [T, 2, GB, D])
        rt = k.sb("t_rwt", [128, 2, 2 * T])
        KVR, SUM, XB, RT, OUT = 0, 2, 4, 5, 6
        bank = k.bank
        (s_set, s_xt, s_kvr, s_clip, s_ek, s_er, s_v, s_kv, s_sum, s_den, s_inv, s_rw, s_rtr, s_rt, s_out, s_add) = (
            k.sem("t_" + x) for x in ("zeroed", "x_columns", "kvr", "clipped", "exp_k", "exp_r", "v_copied", "kv", "sums",
                                      "denominators", "inverses", "rw", "rw_turned", "rw_copied", "outputs", "added"))
        block = ctx.enter_context(nc.Block())

        def kvr(q, which):
            return bank[KVR + q][0:T, 0:6 * D].rearrange("p (b n e) -> p b n e", b=2, n=3)[:, :, which, :]

        @block.tensor
        def _(pe):
            def sums(g, p):
                if not exists(g):
                    return
                pe.wait_ge(s_kv, g + 1)
                wait(pe, s_rw, g - 1)
                nc.tensor.matmul(bank[SUM + p][0:T, 0:GB * D], k.time[:, :], kv[:, p, :, :].rearrange("p b e -> p (b e)"),
                                 start=True, stop=True)
                nc.tensor.matmul(bank[SUM + p][0:T, GB * D:2 * GB * D], k.c("tri")[0:T, :],
                                 ek[:, p, :, :].rearrange("p b e -> p (b e)"), start=True, stop=True).then_inc(s_sum, 1)

            def multiply(g, p):
                if not exists(g):
                    return
                pe.wait_ge(s_xt, g + 1)
                for b in range(GB):
                    if b % 2 == 0:
                        wait(pe, s_clip, 2 * g - 2 + b // 2 + 1)
                        wait(pe, s_er, 2 * g - 2 + b // 2 + 1)
                        wait(pe, s_v, 2 * g - 2 + b // 2 + 1)
                    terms = [(1, k.hi["kvra"]), (1, k.lo["kvra"]), (0, k.hi["kvrb"]), (0, k.lo["kvrb"])]
                    for m, (at, w) in enumerate(terms):
                        last = nc.tensor.matmul(bank[KVR + b // 2][0:T, b % 2 * 3 * D:(b % 2 + 1) * 3 * D],
                                                xt[:, p, b, at:at + T], w[:, :], start=m == 0, stop=m == 3)
                    if b % 2 == 1:
                        last.then_inc(s_kvr, 1)

            def turn_quotients(g, p):
                if not exists(g):
                    return
                pe.wait_ge(s_rw, g + 1)
                wait(pe, s_rt, g)
                for s in range(2):
                    last = nc.tensor.transpose(bank[RT][:, s * T:(s + 1) * T],
                                               rw[:, p, 2 * s:2 * s + 2, :].rearrange("p b e -> p (b e)"),
                                               k.c("ident")[0:T, 0:T])
                last.then_inc(s_rtr, 1)

            def output(g, p):
                if not exists(g):
                    return
                pe.wait_ge(s_rt, g + 1)
                wait(pe, s_add, g)
                for s in range(2):
                    last = nc.tensor.matmul(bank[OUT][0:T, s * 128:(s + 1) * 128], rt[:, p, s * T:(s + 1) * T],
                                            k.c("wo"), start=True, stop=True)
                last.then_inc(s_out, 1)

            def steps(i, p):
                q = 1 - p
                sums(i + 1, q)
                turn_quotients(i, p)
                multiply(i + 2, p)
                output(i, p)
                if exists(i + 3):
                    wait(pe, s_xt, i + 3)
                    n.turn(pe, i + 3, q, k.half(XB))

            pipeline(pe, steps, -4, 2, NG - 6)

        @block.scalar
        def _(act):
            def steps(i, p):
                q = 1 - p
                if exists(i):
                    act.wait_ge(s_rtr, i + 1)
                    wait(act, s_out, i - 1)
                    nc.scalar.activation(rt[:, p, :], bank[RT][:, 0:2 * T], ACT.Copy).then_inc(s_rt, 1)
                g = i + 2
                if exists(g):
                    wait(act, s_den, g - 1)
                    wait(act, s_kv, g - 1)
                    for b in range(2):
                        act.wait_ge(s_clip, 2 * g + b + 1)
                        nc.scalar.activation(er[:, p, 2 * b:2 * b + 2, :], kvr(b, 2), ACT.Exp, scale=-1.0 / WS1).then_inc(s_er, 1)
                        nc.scalar.activation(v[:, p, 2 * b:2 * b + 2, :], kvr(b, 1), ACT.Copy, scale=1.0 / WS1).then_inc(s_v, 1)
                    wait(act, s_sum, g - 1)
                    nc.scalar.activation(ek[:, p, :, :], kc[:, p, :, :], ACT.Exp, scale=1.0 / WS1).then_inc(s_ek, 1)
                if exists(i + 3):
                    act.wait_ge(n.tr, i + 4)
                    wait(act, s_kvr, 2 * (i + 2))
                    nc.scalar.activation(xt[:, q, :, 1:TE], k.turned(XB), ACT.Copy).then_inc(s_xt, 1)

            act.wait_ge(s_set, 1)
            pipeline(act, steps, -4, 2, NG - 6)

        @block.gpsimd
        def _(pool):
            def steps(i, p):
                if exists(i + 4):
                    n.root(pool, i + 4, p)
                if exists(i + 2):
                    g = i + 2
                    pool.wait_ge(s_ek, g + 1)
                    pool.wait_ge(s_v, 2 * g + 2)
                    wait(pool, s_sum, g - 1)
                    nc.gpsimd.tensor_tensor(kv[:, p, :, :], ek[:, p, :, :], v[:, p, :, :], ALU.mult).then_inc(s_kv, 1)
                if exists(i + 4):
                    n.low(pool, i + 4, p)

            nc.gpsimd.memset(xt[:, :, :, :].rearrange("p a b c -> p (a b c)"), 0.0).then_inc(s_set, 1)
            pool.wait_ge(s_set, 1)
            pipeline(pool, steps, -4, 2, NG - 6)

        @block.vector
        def _(dve):
            def clip(g, p, b):
                if not exists(g):
                    return
                if b == 0:
                    wait(dve, s_ek, g - 1)
                dve.wait_ge(s_kvr, 2 * g + b + 1)
                nc.vector.tensor_scalar(kc[:, p, 2 * b:2 * b + 2, :], kvr(b, 0), 30.0 * WS1, -60.0 * WS1,
                                        ALU.min, ALU.max).then_inc(s_clip, 1)

            def steps(i, p):
                q = 1 - p
                ahead = exists(i + 4)
                sums = bank[SUM + q][0:T, :].rearrange("p (w b e) -> p w b e", w=2, b=GB)
                if ahead:
                    n.stats(dve, i + 4, p)
                if exists(i + 1):
                    g = i + 1
                    dve.wait_ge(s_sum, g + 1)
                    dve.wait_ge(s_er, 2 * g + 2)
                    wait(dve, s_inv, g)
                    nc.vector.scalar_tensor_tensor(den[:, :, :], er[:, q, :, :], 1.0, sums[:, 1], ALU.add, ALU.mult).then_inc(s_den, 1)
                if ahead:
                    n.aggregate(dve, i + 4, p)
                    n.centre(dve, i + 4, p)
                clip(i + 2, p, 0)
                clip(i + 2, p, 1)
                if exists(i + 1):
                    g = i + 1
                    dve.wait_ge(s_den, g + 1)
                    wait(dve, s_rw, g)
                    nc.vector.reciprocal(inv[:, :, :], den[:, :, :]).then_inc(s_inv, 1)
                if ahead:
                    n.scale(dve, i + 4, p)
                if exists(i + 1):
                    g = i + 1
                    dve.wait_ge(s_inv, g + 1)
                    wait(dve, s_rtr, g - 1)
                    nc.vector.tensor_tensor(rw[:, q, :, :], inv[:, :, :], sums[:, 0], ALU.mult).then_inc(s_rw, 1)
                if ahead:
                    n.high(dve, i + 4, p)
                if exists(i):
                    dve.wait_ge(s_out, i + 1)
                    nc.vector.tensor_tensor(k.H[:, group(i), :], k.H[:, group(i), :],
                                            bank[OUT][0:T, 0:GB * D].rearrange("p (b e) -> p b e", b=GB),
                                            ALU.add).then_inc(s_add, 1)

            pipeline(dve, steps, -4, 2, NG - 6)


def mix_mlps(k, a_out):
    nc = k.nc
    with ExitStack() as ctx:
        k.ctx = ctx
        n = Norm(k, "m")
        gate = Gate(k, "m", E1, WSF, True, (k.hi["g1w"], k.lo["g1w"]), "g1b", "rev1")
        xt = k.sb("m_xt", [128, 2, N], F16)
        h1 = k.sb("m_h1", [128, 5, N])
        h2 = k.sb("m_h2", [128, 2, 3, N])
        hw = k.sb("m_h2w", [128, 2, 2, N])
        yt = k.sb("m_yt", [128, 2, N // 2])
        H1B, H2B, WB, YB, XB, TB_ = 0, 2, 4, 5, 6, 7
        bank = k.bank
        (s_xt, s_h1, s_a1, s_d1, s_h2, s_a2, s_wb, s_z, s_y, s_yt, s_ytr, s_add, s_store) = (k.sem("m_" + x) for x in (
            "x_columns", "first_layers", "firsts_by_scalar", "firsts_by_vector", "second_layers", "seconds", "weights_spread",
            "weighed", "outputs", "outputs_copied", "outputs_turned", "added", "stored"))
        block = ctx.enter_context(nc.Block())
        ORDER = (1, 2, 3, 4, 0)
        fb1, fb2 = k.c("fb1"), k.c("fb2")
        w2e = k.c("fw2e").rearrange("p (e m) -> p e m", e=E1)
        w3 = k.c("fw3").rearrange("p (i m) -> p i m", i=3)
        sel = k.ch("sel1").rearrange("p (j m) -> p j m", j=2)

        @block.sync
        def _(sp):
            def steps(i, p):
                sp.wait_ge(s_add, i + 1)
                sp.dma_start(a_out[:, group(i), :], k.H[:, group(i), :]).then_inc(s_store, 16)

            with sp.Fori(0, NG) as i:
                steps(i, 0)
            sp.wait_ge(s_store, 16 * NG)

        @block.tensor
        def _(pe):
            def first(g, p, j):
                if not exists(g):
                    return
                c = ORDER[j]
                if j % 2 == 0:
                    wait(pe, s_a1, 3 * g + j // 2)
                else:
                    wait(pe, s_d1, 2 * g + j // 2)
                for m, w in enumerate((k.hi["fw1"], k.lo["fw1"])):
                    last = nc.tensor.matmul(bank[H1B + j % 2][:, 0:N], w[:, c * 128:(c + 1) * 128], xt[:, p, :],
                                            start=m == 0, stop=m == 1)
                last.then_inc(s_h1, 1)

            def second(g, p, j):
                if not exists(g):
                    return
                pe.wait_ge(s_a1, 3 * g + j + 1)
                if j < 2:
                    pe.wait_ge(s_d1, 2 * g + j + 1)
                wait(pe, s_a2, 3 * g + j - 1 if j else 3 * g)
                at = bank[H2B + j % 2]
                if j < 2:
                    for s in range(2):
                        last = nc.tensor.matmul(at[s * D:(s + 1) * D, 0:N], w2e[:, 2 * j + s, :], h1[:, 1 + 2 * j + s, :],
                                                start=True, stop=True)
                else:
                    last = nc.tensor.matmul(at[:, 0:N], k.c("fw2s"), h1[:, 0, :], start=True, stop=True)
                last.then_inc(s_h2, 1)

            def spread(g, p, j):
                if not exists(g):
                    return
                if j == 0:
                    pe.wait_ge(gate.s_wt, g + 1)
                wait(pe, s_z, 2 * g + j)
                nc.tensor.matmul(bank[WB][:, 0:N], sel[:, j, :], gate.wt[:, p, :], start=True, stop=True).then_inc(s_wb, 1)

            def third(g, p):
                if not exists(g):
                    return
                pe.wait_ge(s_z, 2 * g + 2)
                pe.wait_ge(s_a2, 3 * g + 3)
                wait(pe, s_yt, g)
                for s in range(2):
                    cols = slice(s * (N // 2), (s + 1) * (N // 2))
                    out = bank[YB][s * D:(s + 1) * D, 0:N // 2]
                    nc.tensor.matmul(out, w3[:, 0, :], h2[:, p, 0, cols], start=True, stop=False)
                for s in range(2):
                    cols = slice(s * (N // 2), (s + 1) * (N // 2))
                    out = bank[YB][s * D:(s + 1) * D, 0:N // 2]
                    for m, w in enumerate((k.hi["fb3"], k.lo["fb3"])):
                        nc.tensor.matmul(out, w[:, :], gate.wt[:, p, cols], start=False, stop=False)
                for j in range(2):
                    for s in range(2):
                        cols = slice(s * (N // 2), (s + 1) * (N // 2))
                        last = nc.tensor.matmul(bank[YB][s * D:(s + 1) * D, 0:N // 2], w3[:, 1 + j, :], hw[:, p, j, cols],
                                                start=False, stop=j == 1)
                last.then_inc(s_y, 1)

            def turn_outputs(g, p):
                if not exists(g):
                    return
                pe.wait_ge(s_yt, g + 1)
                wait(pe, s_add, g)
                for b in range(2):
                    last = nc.tensor.transpose(bank[TB_][0:T, b * 128:(b + 1) * 128], yt[:, p, b * T:(b + 1) * T], k.c("ident"))
                last.then_inc(s_ytr, 1)

            def steps(i, p):
                q = 1 - p
                first(i, p, 0)
                first(i, p, 1)
                first(i, p, 2)
                second(i, p, 0)
                first(i, p, 3)
                if exists(i - 1):
                    wait(pe, s_add, i - 2)
                    gate.turn(pe, i - 1, k.half(TB_))
                if exists(i + 1):
                    wait(pe, gate.s_dve, gate.OPS * i + 1)
                    n.turn(pe, i + 1, q, k.half(XB))
                first(i, p, 4)
                spread(i - 1, q, 0)
                second(i, p, 1)
                spread(i - 1, q, 1)
                turn_outputs(i - 2, p)
                second(i, p, 2)
                if exists(i + 1):
                    pe.wait_ge(s_xt, i + 2)
                    gate.multiply(pe, i + 1, xt[:, q, :], bank[XB])
                third(i - 1, q)

            pe.wait_ge(gate.s_zero, 1)
            pipeline(pe, steps, -1, 4, NG - 4, NG + 1)

        @block.scalar
        def _(act):
            def first(g, p, j):
                if not exists(g):
                    return
                c = ORDER[j]
                act.wait_ge(s_h1, 5 * g + j + 1)
                wait(act, s_h2, 3 * (g - 1) + j // 2 + 1)
                nc.scalar.activation(h1[:, c, :], bank[H1B][:, 0:N], ACT.Relu, bias=fb1[:, c:c + 1], scale=1.0 / WSF).then_inc(s_a1, 1)

            def second(g, p, j):
                if not exists(g):
                    return
                c = (j + 1) % 3
                act.wait_ge(s_h2, 3 * g + j + 1)
                wait(act, s_y, g - 1)
                nc.scalar.activation(h2[:, p, c, :], bank[H2B + j % 2][:, 0:N], ACT.Relu, bias=fb2[:, c:c + 1]).then_inc(s_a2, 1)

            def steps(i, p):
                q = 1 - p
                first(i, p, 0)
                if exists(i):
                    gate.exponentiate(act, i)
                if exists(i - 2):
                    act.wait_ge(s_y, i - 1)
                    wait(act, s_ytr, i - 3)
                    nc.scalar.activation(yt[:, p, :], bank[YB][:, 0:N // 2], ACT.Identity, bias=k.c("sb3")).then_inc(s_yt, 1)
                first(i, p, 2)
                second(i, p, 0)
                if exists(i - 1):
                    wait(act, s_y, i - 2)
                    gate.place(act, i - 1, q, k.turned(TB_))
                if exists(i + 1):
                    act.wait_ge(n.tr, i + 2)
                    wait(act, s_h1, 5 * i)
                    wait(act, gate.s_log, i)
                    nc.scalar.activation(columns_of(xt[:, q, :]), k.turned(XB), ACT.Copy).then_inc(s_xt, 1)
                first(i, p, 4)
                second(i, p, 1)
                second(i, p, 2)
                if exists(i):
                    gate.tanh(act, i)

            pipeline(act, steps, -1, 4, NG - 4, NG + 1)

        @block.gpsimd
        def _(pool):
            def steps(i, p):
                if exists(i + 2):
                    n.root(pool, i + 2, p)
                if exists(i):
                    gate.weigh(pool, i)
                if exists(i + 2):
                    n.low(pool, i + 2, p)

            nc.gpsimd.memset(gate.parts[:, :, :].rearrange("p b c -> p (b c)"), 0.0).then_inc(gate.s_zero, 1)
            pool.wait_ge(gate.s_zero, 1)
            pipeline(pool, steps, -2, 4, NG - 4, NG + 1)

        @block.vector
        def _(dve):
            def first(g, p, j):
                if not exists(g):
                    return
                c = ORDER[j]
                dve.wait_ge(s_h1, 5 * g + j + 1)
                wait(dve, s_h2, 3 * (g - 1) + j // 2 + 1)
                nc.vector.tensor_scalar(h1[:, c, :], bank[H1B + 1][:, 0:N], fb1[:, c:c + 1], 0.0, ALU.add, ALU.max).then_inc(s_d1, 1)

            def weigh(g, p, j):
                if not exists(g):
                    return
                dve.wait_ge(s_wb, 2 * g + j + 1)
                dve.wait_ge(s_a2, 3 * g + j + 1)
                wait(dve, s_y, g - 1)
                nc.vector.tensor_tensor(hw[:, p, j, :], h2[:, p, 1 + j, :], bank[WB][:, 0:N], ALU.mult).then_inc(s_z, 1)

            def choose(g, *ops):
                if exists(g):
                    gate.choose(dve, g, bank[XB], ops)

            def steps(i, p):
                q = 1 - p
                two = exists(i + 2)
                choose(i, 0)
                first(i, p, 1)
                choose(i, 1)
                if two:
                    n.stats(dve, i + 2, p, (0, 1))
                choose(i, 2)
                if two:
                    n.stats(dve, i + 2, p, (2, 3))
                if two:
                    n.aggregate(dve, i + 2, p, (0,))
                if two:
                    n.aggregate(dve, i + 2, p, (1,))
                choose(i, 3)
                if two:
                    n.centre(dve, i + 2, p)
                    n.aggregate(dve, i + 2, p, (2,))
                choose(i, 4)
                first(i, p, 3)
                choose(i, 5, 6)
                weigh(i - 1, q, 0)
                choose(i, 7, 8, 9)
                weigh(i - 1, q, 1)
                choose(i, 10, 11)
                if exists(i - 2):
                    dve.wait_ge(s_ytr, i - 1)
                    out = bank[TB_][0:T, 0:GB * D].rearrange("p (b s e) -> p s b e", b=2, s=2)
                    h = k.H[:, group(i - 2), :].rearrange("p (s b) e -> p s b e", s=2)
                    nc.vector.tensor_tensor(h, h, out, ALU.add).then_inc(s_add, 1)
                choose(i, 12)
                if two:
                    n.scale(dve, i + 2, p)
                choose(i, 13, 14)
                if two:
                    n.high(dve, i + 2, p)
                choose(i, 15, 16, 17)

            pipeline(dve, steps, -2, 4, NG - 4, NG + 1)


def build(nc, a_x, a_txt, a_tw, a_f32, a_f16, a_out):
    with ExitStack() as ctx:
        k = Core(nc, ctx)
        embed(k, a_x, a_txt, a_tw, a_f32, a_f16)
        attend(k)
        mix_experts(k)
        mix_time(k)
        mix_mlps(k, a_out)


def lay_out(inputs):
    z = {n: np.asarray(a) for n, a in inputs.items()}
    f = {}

    def put(name, rows_, array):
        a = f.setdefault(name, np.zeros((128, pieces()[0][name]), np.float32))
        a[rows_] = array

    both = [slice(0, D), slice(D, 2 * D)]
    everywhere = slice(0, 128)
    x = z["x"].reshape(4, 4, 8, 3, 4, 16, 4, 16).transpose(0, 3, 5, 7, 1, 4, 6, 2)
    x = np.ascontiguousarray(x.reshape(4, 6, 128, 512).transpose(0, 2, 1, 3))
    txt = np.ascontiguousarray(z["txt"].transpose(1, 0, 2))
    put("tokw", everywhere, z["L0_tok_W"].T.reshape(6, 128, D).transpose(1, 0, 2).reshape(128, 6 * D))
    qkvb = z["L0_attn_qkv_b"]
    for r in both:
        put("tokb", r, z["L0_tok_b"][:, None])
        put("qkvw", r, z["L0_attn_qkv_w"])
        put("qb", r, qkvb[0:D, None])
        put("kb", r, qkvb[D:2 * D, None])
    bv = np.repeat(qkvb[2 * D:].reshape(4, 1, 16), 2, 1)
    put("vb", everywhere, np.tile(bv.reshape(-1), 2))
    vpad = np.zeros((128, 4, 2, 16), np.float32)
    for h in range(4):
        own = slice(h % 2 * HD, h % 2 * HD + HD)
        vpad[32 * h + W1Q, h // 2::2, :, own] = bv[h // 2::2, :, own]
    put("vpad", everywhere, vpad.reshape(128, 2 * D))
    put("pb", slice(0, 1), z["L0_attn_proj_b"])
    wp = np.zeros((4, 2, 16, 2, D), np.float32)
    for s in range(2):
        wp[:, s, :, s] = z["L0_attn_proj_w"].reshape(4, 16, D)
    put("wp", everywhere, wp.reshape(128, 2 * D))
    feature = np.arange(128) % D
    put("hmask", everywhere, feature[:, None] // HD == np.arange(HEADS))
    put("ident", everywhere, np.eye(128))
    put("rev0", everywhere, np.arange(E0, 0, -1))
    put("rev1", everywhere, np.arange(E1, 0, -1))
    for r in both:
        put("g0w", r, z["L0_ffn_Wg"])
        put("w1", r, z["L0_ffn_W1"].transpose(1, 0, 2).reshape(D, E0 * H0))
        kvrw = np.concatenate([z["L1_attn_Wk"], z["L1_attn_Wv"], z["L1_attn_Wr"]], 1)
        put("kvrw", r, kvrw)
        put("mix", r, np.concatenate([z[f"L1_attn_time_mix_{n}"].reshape(1, D) for n in "kvr"]).T)
        put("g1w", r, z["L1_ffn_gW"])
        put("sb3", r, z["L1_ffn_sb3"][:, None])
    put("g0b", everywhere, z["L0_ffn_bg"])
    put("g1b", everywhere, z["L1_ffn_gb"])
    put("b1", everywhere, z["L0_ffn_b1"].reshape(CH, 128).T)
    put("w2", everywhere, z["L0_ffn_W2"].reshape(CH, 128, D).transpose(1, 0, 2).reshape(128, CH * D))
    for i in range(2):
        put("b2", slice(i * E0, (i + 1) * E0), z["L0_ffn_b2"])
        put("fb3", slice(i * E1, (i + 1) * E1), z["L1_ffn_eb3"])
    wo = np.zeros((2, D, 2, D), np.float32)
    for s in range(2):
        wo[s, :, s] = z["L1_attn_Wo"]
    put("wo", everywhere, wo.reshape(128, 128))
    put("flip", slice(0, T), np.eye(T)[::-1])
    put("tri", slice(0, T), np.triu(np.ones((T, T))))
    fw1 = np.zeros((D, 5, 128), np.float32)
    fw1[:, 0, 0:D] = z["L1_ffn_sW1"]
    fw1[:, 1:] = z["L1_ffn_eW1"].transpose(1, 0, 2)
    for r in both:
        put("fw1", r, fw1.reshape(D, 640))
    fb1 = np.zeros((128, 5), np.float32)
    fb1[0:D, 0] = z["L1_ffn_sb1"]
    fb1[:, 1:] = z["L1_ffn_eb1"].T
    put("fb1", everywhere, fb1)
    put("fw2s", slice(0, D), z["L1_ffn_sW2"])
    put("fw2e", everywhere, z["L1_ffn_eW2"].transpose(1, 0, 2).reshape(128, E1 * D))
    put("fb2", everywhere, np.stack([z["L1_ffn_sb2"], z["L1_ffn_eb2"][0:2].reshape(-1), z["L1_ffn_eb2"][2:4].reshape(-1)], 1))
    put("fw3", everywhere, np.concatenate([z["L1_ffn_sW3"], z["L1_ffn_eW3"][0:2].reshape(128, D),
                                           z["L1_ffn_eW3"][2:4].reshape(128, D)], 1))
    h = {n: np.zeros((128, w), np.float16) for n, w in pieces()[1].items()}
    h["identh"][:] = np.eye(128)
    h["onesh"][0] = 1
    sel0 = h["sel0"].reshape(128, E0, 128)
    for e in range(E0):
        sel0[[e, E0 + e], e] = 0.5
    sel1 = h["sel1"].reshape(128, 2, 2, D)
    for e in range(E1):
        sel1[[e, E1 + e], e // 2, e % 2] = 0.5
    tw = np.concatenate([z["L1_attn_time_w"], np.zeros(T, np.float32)])[::-1]
    return dict(x=x, txt=txt, tw=np.ascontiguousarray(tw), f32=np.concatenate([f[n] for n in pieces()[0]], 1),
                f16=np.concatenate([h[n] for n in pieces()[1]], 1))


def kernel(**inputs):
    import concourse.bacc as bacc
    from concourse.bass_utils import run_bass_kernel_spmd

    arrays = lay_out(inputs)
    nc = bacc.Bacc("TRN2", target_bir_lowering=False, num_devices=1)
    args = [nc.dram_tensor(f"in_{n}", a.shape, mybir.dt.from_np(a.dtype), kind="ExternalInput").ap()
            for n, a in arrays.items()]
    out = nc.dram_tensor("out", (T, B, D), F32, kind="ExternalOutput").ap()
    build(nc, *args, out)
    r = run_bass_kernel_spmd(nc, [{f"in_{n}": a for n, a in arrays.items()}], core_ids=[0])
    return np.ascontiguousarray(r.results[0]["out"].transpose(1, 0, 2))
```

```python
from contextlib import ExitStack

import numpy as np
import concourse.bass as bass
from concourse import mybir

ALU = mybir.AluOpType
ACT = mybir.ActivationFunctionType
F32 = mybir.dt.float32
F16 = mybir.dt.float16
X = mybir.AxisListType.X

B = 128
D = 64
PATCHES = 16
TEXT = 77
T = PATCHES + TEXT
GB = 4
AGG = 4
NG = B // GB
N = GB * T
TE = T + 1
EPS = 1e-5

HEADS, HD = 8, 8
WIN = 64
W1Q = T - WIN
PADS = WIN - W1Q
W1K = W1Q + 1
TP = 96
SCALE = float(HD) ** -0.5

E0, H0 = 8, 256
CH = E0 * H0 // 128
WS0 = 64.0
WSQ = 16.0
WS1 = 16.0
WSF = 16.0
E1 = 4


def wait(eng, sem, value):
    if isinstance(value, int) and value <= 0:
        return
    eng.wait_ge(sem, value)


def pipeline(eng, steps, first, loop_from, loop_to, last=NG):
    for i in range(first, loop_from):
        steps(i, i % 2)
    with eng.Fori(loop_from, loop_to, 2) as i:
        steps(i, loop_from % 2)
        steps(i + 1, (loop_from + 1) % 2)
    for i in range(loop_to, last + 1):
        steps(i, i % 2)


def exists(g):
    return not isinstance(g, int) or 0 <= g < NG


def pieces():
    f32 = dict(tokw=6 * D, tokb=1, qkvw=3 * D, qb=1, kb=1, vb=1, pb=D, wp=2 * D,
               hmask=HEADS, ident=128,
               g0w=E0, g0b=E0, rev0=E0, w1=E0 * H0, b1=CH, w2=CH * D, b2=D,
               kvrw=3 * D, mix=3, wo=128, tri=T, flip=T,
               g1w=E1, g1b=E1, rev1=E1, fw1=5 * 128, fb1=5, fw2s=128, fw2e=E1 * D, fb2=3, fw3=3 * D,
               fb3=D, sb3=1)
    f16 = dict(identh=128, onesh=TP, sel0=E0 * 128, sel1=2 * 128)
    return f32, f16


def offsets(cols):
    at, out = 0, {}
    for name, n in cols.items():
        out[name] = (at, at + n)
        at += n
    return out, at



F32_AT, F32_COLS = offsets(pieces()[0])
F16_AT, F16_COLS = offsets(pieces()[1])
SPLIT = dict(qkvw=(3 * D, WSQ), g0w=(E0, WS0), w1=(E0 * H0, WS0), b2=(D, 0.5), pb=(D, 1.0),
             kvra=(3 * D, WS1), kvrb=(3 * D, WS1), g1w=(E1, WSF), fw1=(5 * 128, WSF), fb3=(D, 0.5))


def rows(g, b=0):
    return slice(g * GB + b, g * GB + b + 1) if isinstance(g, int) else bass.ds(g * GB + b, 1)


def group(g):
    return slice(g * GB, g * GB + GB) if isinstance(g, int) else bass.ds(g * GB, GB)


class Core:

    def __init__(self, nc, ctx):
        self.nc, self.ctx = nc, ctx
        self.c32 = self.sb("consts32", [128, F32_COLS])
        self.c16 = self.sb("consts16", [128, F16_COLS], F16)
        self.H = self.sb("residual", [T, B, D])
        self.bank = [ctx.enter_context(nc.psum_tensor(f"bank{i}", [128, 512], F32)) for i in range(8)]
        self.hi = {n: self.sb(f"{n}_hi", [128, w], F16) for n, (w, _) in SPLIT.items()}
        self.lo = {n: self.sb(f"{n}_lo", [128, w], F16) for n, (w, _) in SPLIT.items()}
        self.stats = self.sb("stats", [T, 2, GB, 6])
        self.both = self.sb("means_squares", [T, 2, GB, 2])
        self.apart = self.sb("means_apart", [T, 2, GB])
        self.apart2 = self.sb("means_apart_squared", [T, 2, GB])
        self.var = self.sb("variances", [T, 2, GB])
        self.vareps = self.sb("var_eps", [T, 2, GB])
        self.rstd = self.sb("rstd", [T, 2, GB])
        self.time = self.sb("time_weights", [T, T])
        self.neghalf = self.sb("neghalf", [T, GB])
        self.eps = self.sb("eps", [T, GB])
        self.xc = self.sb("centred", [T, 2, GB, D])
        self.xn = self.sb("normed", [T, 2, GB, D])
        self.xs = self.sb("norm_parts", [T, 2, GB, 2 * D], F16)

    def sb(self, name, shape, dt=F32):
        return self.ctx.enter_context(self.nc.sbuf_tensor(name, shape, dt))

    def sem(self, name):
        return self.ctx.enter_context(self.nc.semaphore(name))

    def c(self, name):
        return self.c32[:, F32_AT[name][0]:F32_AT[name][1]]

    def ch(self, name):
        return self.c16[:, F16_AT[name][0]:F16_AT[name][1]]

    def half(self, i):
        return self.bank[i][:, :].bitcast(F16)

    def turned(self, i):
        return self.half(i)[:, 0:GB * TE].rearrange("p (b t) -> p b t", b=GB)[:, :, 0:T]


class Norm:

    def __init__(self, k, phase):
        self.k, self.nc = k, k.nc
        (self.bn, self.mv, self.eps, self.rstd, self.xc, self.xn, self.hi, self.lo, self.tr) = (
            k.sem(f"{phase}_{n}") for n in ("bn", "mv", "eps", "rstd", "xc", "xn", "hi", "lo", "turned"))

    def stats(self, dve, g, p, batches=range(GB)):
        k = self.k
        if 0 in batches:
            wait(dve, self.mv, AGG * (g - 2) + 2)
        for b in batches:
            self.nc.vector.bn_stats(k.stats[:, p, b, :], k.H[:, rows(g, b), :]).then_inc(self.bn, 1)

    def aggregate(self, dve, g, p, parts=range(3)):
        k, even, odd = self.k, 1, 4
        st = k.stats[:, p, :, :]
        if 0 in parts:
            dve.wait_ge(self.bn, GB * g + GB)
            wait(dve, self.xc, g - 1)
            self.nc.vector.tensor_tensor(k.both[:, p, :, :], st[:, :, even:even + 2], st[:, :, odd:odd + 2],
                                         ALU.add).then_inc(self.mv, 1)
            self.nc.vector.tensor_tensor(k.apart[:, p, :], st[:, :, even], st[:, :, odd],
                                         ALU.subtract).then_inc(self.mv, 1)
        if 1 in parts:
            dve.wait_ge(self.mv, AGG * g + 2)
            self.nc.vector.scalar_tensor_tensor(k.apart2[:, p, :], k.apart[:, p, :], 0.25, k.apart[:, p, :],
                                                ALU.mult, ALU.mult).then_inc(self.mv, 1)
        if 2 in parts:
            dve.wait_ge(self.mv, AGG * g + 3)
            wait(dve, self.eps, g - 1)
            self.nc.vector.scalar_tensor_tensor(k.var[:, p, :], k.both[:, p, :, 1], 1.0 / D, k.apart2[:, p, :],
                                                ALU.mult, ALU.add).then_inc(self.mv, 1)

    def root(self, pool, g, p):
        k = self.k
        pool.wait_ge(self.mv, AGG * g + AGG)
        wait(pool, self.rstd, g - 1)
        self.nc.gpsimd.tensor_tensor(k.vareps[:, p, :], k.var[:, p, :], k.eps[:, :], ALU.add).then_inc(self.eps, 1)
        pool.wait_ge(self.eps, g + 1)
        wait(pool, self.xn, g - 1)
        self.nc.gpsimd.tensor_tensor(k.rstd[:, p, :], k.vareps[:, p, :], k.neghalf[:, :],
                                     ALU.pow).then_inc(self.rstd, 1)

    def centre(self, dve, g, p):
        k = self.k
        dve.wait_ge(self.mv, AGG * g + 1)
        self.nc.vector.scalar_tensor_tensor(k.xc[:, p, :, :], k.both[:, p, :, 0:1].broadcast_to([T, GB, D]), -0.5,
                                            k.H[:, group(g), :], ALU.mult, ALU.add).then_inc(self.xc, 1)

    def scale(self, dve, g, p):
        k = self.k
        dve.wait_ge(self.rstd, g + 1)
        dve.wait_ge(self.xc, g + 1)
        wait(dve, self.lo, g - 1)
        self.nc.vector.tensor_tensor(k.xn[:, p, :, :], k.xc[:, p, :, :],
                                     k.rstd[:, p, :].unsqueeze(2).broadcast_to([T, GB, D]),
                                     ALU.mult).then_inc(self.xn, 1)

    def high(self, dve, g, p):
        k = self.k
        dve.wait_ge(self.xn, g + 1)
        wait(dve, self.tr, g - 1)
        self.nc.vector.tensor_copy(k.xs[:, p, :, 0:D], k.xn[:, p, :, :]).then_inc(self.hi, 1)

    def low(self, pool, g, p):
        k = self.k
        pool.wait_ge(self.hi, g + 1)
        self.nc.gpsimd.tensor_tensor(k.xs[:, p, :, D:2 * D], k.xn[:, p, :, :], k.xs[:, p, :, 0:D],
                                     ALU.subtract).then_inc(self.lo, 1)

    def turn(self, pe, g, p, out):
        k = self.k
        pe.wait_ge(self.lo, g + 1)
        for b in range(GB):
            last = self.nc.tensor.transpose(out[:, b * TE:b * TE + T], k.xs[:, p, b, :], k.ch("identh")[0:T, 0:T])
        last.then_inc(self.tr, 1)


def embed(k, a_x, a_txt, a_tw, a_f32, a_f16):
    nc = k.nc
    with ExitStack() as ctx:
        k.ctx = ctx
        NT, KC, TT = 4, 6, 512
        pixels = k.sb("pixels", [128, NT, KC, TT])
        tokens_t = k.sb("tokens_t", [128, 2, TT])
        tokens = k.sb("tokens", [128, 2, 4, 128])
        scaled = k.sb("scaled", [128, 2, E0 * H0])
        mixed = k.sb("mixed", [128, 2, 3, D])
        onemix = k.sb("onemix", [128, 3])
        hankel = k.sb("hankel", [T, T])
        s_tw, s_flip, s_time = k.sem("time_loaded"), k.sem("time_flipped"), k.sem("time_copied")
        s_const, s_txt, s_half = k.sem("consts_loaded"), k.sem("text_loaded"), k.sem("halves_set")
        s_pix = [k.sem(f"pixels_loaded{i}") for i in range(NT)]
        s_prod, s_bias = k.sem("tokens_multiplied"), k.sem("tokens_biased")
        s_turn, s_tok, s_put = k.sem("tokens_turned"), k.sem("tokens_copied"), k.sem("tokens_put")
        s_mix, s_scl, s_spl = k.sem("weights_mixed"), k.sem("weights_scaled"), k.sem("weights_split")
        block = ctx.enter_context(nc.Block())

        @block.sync
        def _(sp):
            sp.dma_start(k.c32[:, :], a_f32).then_inc(s_const, 16)
            sp.dma_start(k.c16[:, :], a_f16).then_inc(s_const, 16)
            backwards = bass.AP(tensor=a_tw.tensor, offset=1, ap=[[1, T], [1, T]])
            sp.dma_start(hankel[:, :], backwards).then_inc(s_tw, 16)
            for i in range(NT):
                sp.dma_start(pixels[:, i, :, :], a_x[i]).then_inc(s_pix[i], 16)
            sp.dma_start(k.H[PATCHES:T, :, :], a_txt).then_inc(s_txt, 16)
            for q in range(2):
                sp.wait_ge(s_tok, q + 1)
                for s in range(2):
                    for j in range(4):
                        b = (2 * q + s) * 32 + 8 * j
                        sp.dma_start(k.H[0:PATCHES, b:b + 8, :], tokens[:, q, j, s * D:s * D + D]).then_inc(s_put, 16)
            sp.wait_ge(s_put, 16 * 16)
            sp.wait_ge(s_txt, 16)

        @block.tensor
        def _(pe):
            pe.wait_ge(s_const, 32)
            tokw = k.c("tokw").rearrange("p (c e) -> p c e", c=KC)
            pe.wait_ge(s_tw, 16)
            nc.tensor.matmul(k.bank[6][0:T, 0:T], k.c("flip")[0:T, :], hankel[:, :], start=True, stop=True).then_inc(s_flip, 1)
            for q in range(2):
                for s in range(2):
                    pe.wait_ge(s_pix[2 * q + s], 16)
                for ci in range(KC):
                    for s in range(2):
                        last = nc.tensor.matmul(k.bank[q][s * D:s * D + D, :], tokw[:, ci, :],
                                                pixels[:, 2 * q + s, ci, :], start=ci == 0, stop=ci == KC - 1)
                last.then_inc(s_prod, 1)
                pe.wait_ge(s_bias, q + 1)
                for j in range(4):
                    last = nc.tensor.transpose(k.bank[2 + q][:, j * 128:(j + 1) * 128],
                                               tokens_t[:, q, j * 128:(j + 1) * 128], k.c("ident"))
                last.then_inc(s_turn, 1)

        @block.scalar
        def _(act):
            act.wait_ge(s_const, 32)
            act.wait_ge(s_flip, 1)
            nc.scalar.activation(k.time[:, :], k.bank[6][0:T, 0:T], ACT.Copy).then_inc(s_time, 1)
            for q in range(2):
                act.wait_ge(s_prod, q + 1)
                nc.scalar.activation(tokens_t[:, q, :], k.bank[q][:, :], ACT.Identity, bias=k.c("tokb")).then_inc(s_bias, 1)
            for q in range(2):
                act.wait_ge(s_turn, q + 1)
                nc.scalar.activation(tokens[:, q, :, :].rearrange("p j e -> p (j e)"), k.bank[2 + q][:, :],
                                     ACT.Copy).then_inc(s_tok, 1)

        @block.gpsimd
        def _(pool):
            nc.gpsimd.memset(k.neghalf[:, :], -0.5).then_inc(s_half, 1)
            nc.gpsimd.memset(k.eps[:, :], EPS).then_inc(s_half, 1)
            pool.wait_ge(s_half, 2)

        @block.vector
        def _(dve):
            dve.wait_ge(s_const, 32)
            nc.vector.tensor_scalar(onemix[:, :], k.c("mix"), -1.0, 1.0, ALU.mult, ALU.add).then_inc(s_mix, 1)
            dve.wait_ge(s_mix, 1)
            for m, mix in enumerate((k.c("mix"), onemix[:, :])):
                for n in range(3):
                    nc.vector.tensor_scalar(mixed[:, m, n, :], k.c("kvrw")[:, n * D:(n + 1) * D], mix[:, n:n + 1], None,
                                            ALU.mult).then_inc(s_mix, 1)
            dve.wait_ge(s_mix, 7)
            for name, by in (("vb", WSQ), ("wp", 1 / WSQ)):
                nc.vector.tensor_scalar(k.c(name), k.c(name), by, None, ALU.mult).then_inc(s_mix, 1)
            for e in (1, 3):
                for w, by in ((k.c("fb1")[:, 1 + e:2 + e], WSF), (k.c("fw2e")[:, e * D:(e + 1) * D], 1 / WSF)):
                    nc.vector.tensor_scalar(w, w, by, None, ALU.mult).then_inc(s_mix, 1)
            for n, (name, (w, by)) in enumerate(SPLIT.items()):
                src = mixed[:, name == "kvrb", :, :].rearrange("p n e -> p (n e)") if name[:3] == "kvr" else k.c(name)
                wait(dve, s_spl, 2 * (n - 1))
                nc.vector.tensor_scalar(scaled[:, n % 2, 0:w], src, by, None, ALU.mult).then_inc(s_scl, 1)
                dve.wait_ge(s_scl, n + 1)
                nc.vector.tensor_copy(k.hi[name][:, :], scaled[:, n % 2, 0:w]).then_inc(s_spl, 1)
                dve.wait_ge(s_spl, 2 * n + 1)
                nc.vector.tensor_tensor(k.lo[name][:, :], scaled[:, n % 2, 0:w], k.hi[name][:, :],
                                        ALU.subtract).then_inc(s_spl, 1)


def attend(k):
    nc = k.nc
    with ExitStack() as ctx:
        k.ctx = ctx
        n = Norm(k, "a")
        xt = k.sb("a_xt", [128, 2, N], F16)
        qd = k.sb("a_q", [128, 2, 2, 2 * TP])
        ks = k.sb("a_k", [128, 2, 2, T + 1])
        km = k.sb("a_kmask", [128, 2, 2, HEADS, T + 1])
        v0 = k.sb("a_v0", [128, 2, 2, 4, 2, 16])
        v1 = k.sb("a_v1", [128, 2, 2, 4, 2, 16])
        mx = k.sb("a_max", [128, 2, 3, HEADS])
        e0 = k.sb("a_e0", [128, 2, 2, HEADS, WIN])
        e1 = k.sb("a_e1", [128, 2, HEADS, 32])
        sm = k.sb("a_sum", [128, 2, 3, HEADS])
        rs = k.sb("a_rsum", [128, 2, 3, HEADS])
        p0 = k.sb("a_p0t", [128, 2, 2, 512])
        p1 = k.sb("a_p1t", [128, 2, 256])
        ot = k.sb("a_ot", [128, 2, 384])
        S0, SW, TA, TB_, O, QK, XV = 0, 2, 3, 4, 5, 6, 7
        bank = k.bank
        (s_set, s_xt, s_qk, s_q, s_k, s_km, s_v, s_ve, s_s, s_mx, s_sub, s_exp, s_pad, s_sum, s_rs, s_p, s_pt, s_pe,
         s_o, s_oe, s_y, s_h) = (k.sem("a_" + x) for x in (
             "buffers_set", "x_columns", "qk_multiplied", "q_placed", "k_placed", "k_masked", "v_multiplied",
             "v_placed", "scores", "maxima", "less_max", "exps", "padding_weighted", "sums", "inverses", "probs",
             "probs_turned", "probs_t_copied", "gathered", "gathered_copied", "projected", "added"))
        block = ctx.enter_context(nc.Block())
        VE = 6
        SETS = 6
        hq, lq = k.hi["qkvw"], k.lo["qkvw"]

        def pair_cols(ap):
            return ap.rearrange("p (q s t) -> p q s t", q=2, s=2)

        @block.tensor
        def _(pe):
            def values(g, p):
                if not exists(g):
                    return
                pe.wait_ge(s_xt, g + 1)
                for b in range(GB):
                    for m, w in enumerate((hq, lq)):
                        out = bank[XV][0:T, 0:GB * D].rearrange("p (q j s f) -> p q s j f", q=2, j=4, s=2)
                        last = nc.tensor.matmul(out[:, b // 2, b % 2, :, :], xt[:, p, b * T:(b + 1) * T],
                                                w[:, 2 * D:3 * D], start=m == 0, stop=m == 1)
                last.then_inc(s_v, 1)

            def scores(g, p):
                if not exists(g):
                    return
                pe.wait_ge(s_q, 4 * g + 4)
                for q in range(2):
                    pe.wait_ge(s_km, 2 * g + q + 1)
                    wait(pe, s_sub, 3 * (g - 1) + q + 1)
                    nc.tensor.matmul(bank[S0 + q][:, :], qd[:, p, q, 0:2 * WIN],
                                     km[:, p, q, :, 0:WIN], start=True, stop=True).then_inc(s_s, 1)
                wait(pe, s_sub, 3 * g)
                for q in range(2):
                    last = nc.tensor.matmul(bank[SW][q * WIN:(q + 1) * WIN, 0:HEADS * W1K],
                                            qd[:, p, q, 2 * WIN:2 * TP],
                                            km[:, p, q, :, WIN:T + 1], start=True, stop=True)
                last.then_inc(s_s, 1)

            def project(g, p):
                if not exists(g):
                    return
                pe.wait_ge(s_oe, g + 1)
                pe.wait_ge(s_pe, 3 * g + 2)
                nc.tensor.matmul(bank[TB_][0:TP, 0:GB * D], k.ch("onesh"), k.hi["pb"][:, :].unsqueeze(1).broadcast_to([128, GB, D]),
                                 start=True, stop=False)
                nc.tensor.matmul(bank[TB_][0:TP, 0:GB * D], k.ch("onesh"), k.lo["pb"][:, :].unsqueeze(1).broadcast_to([128, GB, D]),
                                 start=False, stop=True)
                for b in range(GB):
                    q, s = b // 2, b % 2
                    y = bank[TB_][:, b * D:(b + 1) * D]
                    nc.tensor.matmul(y[0:WIN], ot[:, p, q * 128 + s * WIN:][:, 0:WIN], k.c("wp")[:, s * D:(s + 1) * D],
                                     start=False, stop=True, skip_group_check=True)
                    last = nc.tensor.matmul(y[WIN:TP], ot[:, p, 256 + q * 64 + s * 32:][:, 0:32],
                                            k.c("wp")[:, s * D:(s + 1) * D], start=False, stop=True,
                                            skip_group_check=True)
                last.then_inc(s_y, 1)

            def columns(g, p):
                if not exists(g):
                    return
                wait(pe, s_ve, VE * (g - 1))
                n.turn(pe, g, p, k.half(XV))

            def queries_keys(g, p):
                if not exists(g):
                    return
                pe.wait_ge(s_xt, g + 1)
                wait(pe, s_q, 4 * g)
                wait(pe, s_k, g)
                cols = pair_cols(xt[:, p, :])
                for m in range(2):
                    for s in range(2):
                        for i, w in enumerate((hq, lq)):
                            last = nc.tensor.matmul(bank[QK][s * D:(s + 1) * D, m * 2 * T:(m + 1) * 2 * T],
                                                    w[:, m * D:(m + 1) * D], cols[:, :, s, :], start=i == 0, stop=i == 1)
                last.then_inc(s_qk, 1)

            def turn_probs(g, p, part):
                if not exists(g):
                    return
                pe.wait_ge(s_p, 3 * g + part + 1)
                if part == 0:
                    wait(pe, s_pe, 3 * g)
                if part == 1:
                    wait(pe, s_h, g)
                if part == 2:
                    pe.wait_ge(s_pe, 3 * g + 1)
                if part < 2:
                    e = e0[:, p, part, :, :].rearrange("p h w -> p (h w)")
                    at = bank[TA if part == 0 else TB_]
                    for j in range(4):
                        last = nc.tensor.transpose(at[:, j * 128:(j + 1) * 128], e[:, j * 128:(j + 1) * 128], k.c("ident"))
                else:
                    e = e1[:, p, :, :].rearrange("p h w -> p (h w)")
                    for j in range(2):
                        last = nc.tensor.transpose(bank[TA][:, j * 128:(j + 1) * 128], e[:, j * 128:(j + 1) * 128], k.c("ident"))
                last.then_inc(s_pt, 1)

            def gather(g, p):
                if not exists(g):
                    return
                pe.wait_ge(s_ve, VE * g + VE)
                wait(pe, s_oe, g)
                for q in range(2):
                    pe.wait_ge(s_pe, 3 * g + q + 1)
                    for j in range(4):
                        nc.tensor.matmul(bank[O][32 * j:32 * j + 32, q * 128:(q + 1) * 128], v0[:, p, q, j, :, :].rearrange("p s f -> p (s f)"),
                                         p0[:, p, q, j * 128:(j + 1) * 128], start=True, stop=True)
                pe.wait_ge(s_pe, 3 * g + 3)
                for q in range(2):
                    for j in range(2):
                        last = nc.tensor.matmul(bank[O][64 * j:64 * j + 64, 256 + q * 64:256 + (q + 1) * 64],
                                                v1[:, p, q, 2 * j:2 * j + 2, :, :].rearrange("p j s f -> p (j s f)"),
                                                p1[:, p, j * 128 + q * 64:j * 128 + (q + 1) * 64], start=True, stop=True)
                last.then_inc(s_o, 1)

            def steps(i, p):
                queries_keys(i + 2, p)
                turn_probs(i, p, 0)
                values(i + 1, 1 - p)
                turn_probs(i, p, 1)
                turn_probs(i, p, 2)
                gather(i, p)
                scores(i + 2, p)
                project(i, p)
                columns(i + 3, 1 - p)

            pe.wait_ge(s_set, SETS)
            pipeline(pe, steps, -4, 2, NG - 6)

        @block.scalar
        def _(act):
            def columns(g, p):
                if not exists(g):
                    return
                act.wait_ge(n.tr, g + 1)
                wait(act, s_qk, g - 1)
                wait(act, s_v, g - 1)
                nc.scalar.activation(xt[:, p, :].rearrange("p (b t) -> p b t", b=GB),
                                     k.turned(XV), ACT.Copy).then_inc(s_xt, 1)

            def place_keys(g, p):
                if not exists(g):
                    return
                act.wait_ge(s_qk, g + 1)
                wait(act, s_km, 2 * (g - 1))
                nc.scalar.activation(ks[:, p, :, 0:T], bank[QK][:, 2 * T:4 * T].rearrange("p (q t) -> p q t", q=2),
                                     ACT.Identity, bias=k.c("kb"), scale=1.0 / WSQ).then_inc(s_k, 1)

            def place_queries(g, p):
                if not exists(g):
                    return
                wait(act, s_s, 3 * (g - 1))
                for s in range(2):
                    src = bank[QK][s * D:(s + 1) * D, 0:2 * T].rearrange("p (q t) -> p q t", q=2)
                    for at, t, w in ((s * WIN, 0, WIN), (2 * WIN + s * 32, WIN, W1Q)):
                        nc.scalar.activation(qd[s * D:(s + 1) * D, p, :, at:at + w], src[:, :, t:t + w], ACT.Identity,
                                             bias=k.c("qb")[s * D:(s + 1) * D], scale=1.0 / WSQ).then_inc(s_q, 1)

            def place_values(g, p):
                if not exists(g):
                    return
                act.wait_ge(s_v, g + 1)
                wait(act, s_o, g - 1)
                v = bank[XV][:, 0:GB * D].rearrange("p (j f) -> p j f", f=16)
                for h in range(2):
                    own = slice(h * HD, h * HD + HD)
                    dst = v0[h * WIN:(h + 1) * WIN, p, :, :, :, :].rearrange("p q j s f -> p (q j s) f")
                    nc.scalar.activation(dst[:, :, own], v[0:WIN, :, own], ACT.Copy).then_inc(s_ve, 1)
                v = bank[XV][:, 0:GB * D].rearrange("p (i r s f) -> p i r s f", r=2, s=2, f=16)
                for h in range(4):
                    own, r = slice(h % 2 * HD, h % 2 * HD + HD), h // 2
                    dst = v1[32 * h:32 * h + W1Q, p, :, :, :, :].rearrange("p q (i r) s f -> p (q i) r s f", i=2)
                    nc.scalar.activation(dst[:, :, r, :, own], v[WIN:T, :, r, :, own], ACT.Copy).then_inc(s_ve, 1)

            def exps(g, p, part):
                if not exists(g):
                    return
                act.wait_ge(s_sub, 3 * g + part + 1)
                e = e0[:, p, part, :, :] if part < 2 else e1[:, p, :, 0:W1K]
                nc.scalar.activation(e, e, ACT.Exp, scale=SCALE).then_inc(s_exp, 1)

            def copy_probs(g, p, part):
                if not exists(g):
                    return
                act.wait_ge(s_pt, 3 * g + part + 1)
                wait(act, s_o, g - 1)
                if part < 2:
                    nc.scalar.activation(p0[:, p, part, :], bank[TA if part == 0 else TB_][:, :], ACT.Copy).then_inc(s_pe, 1)
                else:
                    nc.scalar.activation(p1[:, p, :], bank[TA][:, 0:256], ACT.Copy).then_inc(s_pe, 1)

            def copy_gathered(g, p):
                if not exists(g):
                    return
                act.wait_ge(s_o, g + 1)
                wait(act, s_y, g - 1)
                nc.scalar.activation(ot[:, p, :], bank[O][:, 0:384], ACT.Identity, bias=k.c("vb")).then_inc(s_oe, 1)

            def steps(i, p):
                place_keys(i + 2, p)
                copy_probs(i, p, 0)
                copy_probs(i, p, 1)
                exps(i + 1, 1 - p, 0)
                copy_probs(i, p, 2)
                place_queries(i + 2, p)
                exps(i + 1, 1 - p, 1)
                place_values(i + 1, 1 - p)
                exps(i + 1, 1 - p, 2)
                copy_gathered(i, p)
                columns(i + 3, 1 - p)

            act.wait_ge(s_set, SETS)
            pipeline(act, steps, -4, 2, NG - 6)

        @block.gpsimd
        def _(pool):
            def mask_keys(g, p):
                if not exists(g):
                    return
                pool.wait_ge(s_k, g + 1)
                wait(pool, s_s, 3 * (g - 1))
                for q in range(2):
                    nc.gpsimd.tensor_tensor(km[:, p, q, :, :], ks[:, p, q, :].unsqueeze(1).broadcast_to([128, HEADS, T + 1]),
                                            k.c("hmask").unsqueeze(2).broadcast_to([128, HEADS, T + 1]),
                                            ALU.mult).then_inc(s_km, 1)

            def probs(g, p, part):
                if not exists(g):
                    return
                pool.wait_ge(s_rs, 3 * g + part + 1)
                e, w = (e0[:, p, part, :, :], WIN) if part < 2 else (e1[:, p, :, 0:W1K], W1K)
                nc.gpsimd.tensor_tensor(e, e, rs[:, p, part, :].unsqueeze(2).broadcast_to([128, HEADS, w]),
                                        ALU.mult).then_inc(s_p, 1)

            def steps(i, p):
                if exists(i + 3):
                    n.low(pool, i + 3, 1 - p)
                mask_keys(i + 2, p)
                if exists(i + 4):
                    n.root(pool, i + 4, p)
                for part in range(3):
                    probs(i + 1, 1 - p, part)

            nc.gpsimd.memset(qd[:, :, :, :].rearrange("p a b c -> p (a b c)"), 0.0).then_inc(s_set, 1)
            nc.gpsimd.memset(v0[:, :, :, :, :, :].rearrange("p a b c d e -> p (a b c d e)"), 0.0).then_inc(s_set, 1)
            nc.gpsimd.memset(v1[:, :, :, :, :, :].rearrange("p a b c d e -> p (a b c d e)"), 0.0).then_inc(s_set, 1)
            nc.gpsimd.memset(e1[:, :, :, :].rearrange("p a b c -> p (a b c)"), 0.0).then_inc(s_set, 1)
            for p in range(2):
                nc.gpsimd.tensor_copy(ks[:, p, :, T:T + 1], k.c("kb").unsqueeze(1).broadcast_to([128, 2, 1])).then_inc(s_set, 1)
            pool.wait_ge(s_set, SETS)
            pipeline(pool, steps, -4, 2, NG - 6)

        @block.vector
        def _(dve):
            def maxima(g, p, part):
                if not exists(g):
                    return
                dve.wait_ge(s_s, 3 * g + part + 1)
                src = bank[S0 + part][:, :].rearrange("p (h w) -> p h w", h=HEADS) if part < 2 else \
                    bank[SW][:, 0:HEADS * W1K].rearrange("p (h w) -> p h w", h=HEADS)
                nc.vector.tensor_reduce(mx[:, p, part, :], src, X, ALU.max).then_inc(s_mx, 1)

            def less_max(g, p, part):
                if not exists(g):
                    return
                dve.wait_ge(s_mx, 3 * g + part + 1)
                wait(dve, s_pt, 3 * (g - 2) + part + 1)
                w = WIN if part < 2 else W1K
                src = bank[(S0 + part) if part < 2 else SW][:, 0:HEADS * w].rearrange("p (h w) -> p h w", h=HEADS)
                dst = e0[:, p, part, :, :] if part < 2 else e1[:, p, :, 0:W1K]
                nc.vector.tensor_tensor(dst, src, mx[:, p, part, :].unsqueeze(2).broadcast_to([128, HEADS, w]),
                                        ALU.subtract).then_inc(s_sub, 1)

            def weigh_padding(g, p):
                if not exists(g):
                    return
                dve.wait_ge(s_exp, 3 * g + 3)
                nc.vector.tensor_scalar(e1[:, p, :, W1Q], e1[:, p, :, W1Q], float(PADS), None, ALU.mult).then_inc(s_pad, 1)

            def sums(g, p, part):
                if not exists(g):
                    return
                dve.wait_ge(s_exp, 3 * g + part + 1)
                if part == 2:
                    dve.wait_ge(s_pad, g + 1)
                e = e0[:, p, part, :, :] if part < 2 else e1[:, p, :, 0:W1K]
                nc.vector.tensor_reduce(sm[:, p, part, :], e, X, ALU.add).then_inc(s_sum, 1)

            def inverses(g, p, part):
                if not exists(g):
                    return
                dve.wait_ge(s_sum, 3 * g + part + 1)
                wait(dve, s_p, 3 * (g - 2) + part + 1)
                nc.vector.reciprocal(rs[:, p, part, :], sm[:, p, part, :]).then_inc(s_rs, 1)

            def add(g, p):
                if not exists(g):
                    return
                dve.wait_ge(s_y, g + 1)
                nc.vector.tensor_tensor(k.H[:, group(g), :], k.H[:, group(g), :],
                                        bank[TB_][0:T, 0:GB * D].rearrange("p (b e) -> p b e", b=GB), ALU.add).then_inc(s_h, 1)

            def steps(i, p):
                q, ahead = 1 - p, exists(i + 4)
                if exists(i + 3):
                    n.scale(dve, i + 3, q)
                maxima(i + 1, q, 0)
                if exists(i + 3):
                    n.high(dve, i + 3, q)
                less_max(i + 1, q, 0)
                maxima(i + 1, q, 1)
                if ahead:
                    n.stats(dve, i + 4, p)
                less_max(i + 1, q, 1)
                if ahead:
                    n.aggregate(dve, i + 4, p, (0,))
                maxima(i + 1, q, 2)
                if ahead:
                    n.aggregate(dve, i + 4, p, (1,))
                    n.centre(dve, i + 4, p)
                less_max(i + 1, q, 2)
                if ahead:
                    n.aggregate(dve, i + 4, p, (2,))
                sums(i + 1, q, 0)
                inverses(i + 1, q, 0)
                sums(i + 1, q, 1)
                weigh_padding(i + 1, q)
                inverses(i + 1, q, 1)
                sums(i + 1, q, 2)
                inverses(i + 1, q, 2)
                add(i, p)

            dve.wait_ge(s_set, SETS)
            pipeline(dve, steps, -4, 2, NG - 6)


class Gate:

    def __init__(self, k, phase, experts, weight_scale, softmax_first, weights, bias, rev):
        self.k, self.nc, self.E, self.by, self.soft = k, k.nc, experts, weight_scale, softmax_first
        self.w, self.bias, self.rev = weights, k.c(bias), k.c(rev)
        s = [T, GB, experts]
        (self.logits, self.less, self.equal, self.first, self.exps, self.left, self.less2, self.equal2, self.second,
         self.either, self.sign, self.tilt, self.dense) = (k.sb(f"{phase}_{name}", s) for name in (
             "logits", "less_top", "equal", "first", "exps", "left", "less_top2", "equal2", "second", "either", "sign",
             "tilt", "dense"))
        (self.top, self.rank, self.top2, self.rank2, self.gap, self.half_tanh, self.total, self.inverse) = (
            k.sb(f"{phase}_{name}", [T, GB]) for name in (
                "top", "rank", "top2", "rank2", "gap", "half_tanh", "total", "inverse"))
        self.parts = k.sb(f"{phase}_parts", [T, GB, 128], F16)
        self.wt = k.sb(f"{phase}_wt", [128, 2, N], F16)
        (self.s_log, self.s_dve, self.s_act, self.s_pool, self.s_tr, self.s_wt, self.s_zero) = (
            k.sem(f"{phase}_g_" + n) for n in ("logits", "chain", "acted", "weighed", "turned", "placed", "zeroed"))
        self.OPS = 15 if softmax_first else 12
        self.ACTS = 2 if softmax_first else 1
        self.POOLS = 6

    def over(self, ap):
        return ap[:, :].unsqueeze(2).broadcast_to([T, GB, self.E])

    def multiply(self, pe, g, xt, out):
        for b in range(GB):
            for m, w in enumerate(self.w):
                last = self.nc.tensor.matmul(out[0:T, b * self.E:(b + 1) * self.E], xt[:, b * T:(b + 1) * T],
                                             w[:, 0:self.E], start=m == 0, stop=m == 1)
        last.then_inc(self.s_log, 1)

    def choose(self, dve, g, out, ops):
        v, E, at = self.nc.vector, self.E, self.OPS * g
        every = self.bias[0:T].unsqueeze(1).broadcast_to([T, GB, E])
        rev = self.rev[0:T].unsqueeze(1).broadcast_to([T, GB, E])
        logits = out[0:T, 0:GB * E].rearrange("p (b e) -> p b e", b=GB)
        done = self.s_dve
        for o in ops:
            if o == 0:
                dve.wait_ge(self.s_log, g + 1)
                v.scalar_tensor_tensor(self.logits[:, :, :], logits, 1.0 / self.by, every, ALU.mult,
                                       ALU.add).then_inc(done, 1)
            if o == 1:
                dve.wait_ge(done, at + 1)
                v.tensor_reduce(self.top[:, :], self.logits[:, :, :], X, ALU.max).then_inc(done, 1)
            if o == 2:
                dve.wait_ge(done, at + 2)
                v.tensor_tensor(self.less[:, :, :], self.logits[:, :, :], self.over(self.top),
                                ALU.subtract).then_inc(done, 1)
            if o == 3:
                dve.wait_ge(done, at + 3)
                v.scalar_tensor_tensor(self.equal[:, :, :], self.less[:, :, :], 0.0, rev, ALU.is_equal,
                                       ALU.mult).then_inc(done, 1)
            if o == 4:
                dve.wait_ge(done, at + 4)
                v.tensor_reduce(self.rank[:, :], self.equal[:, :, :], X, ALU.max).then_inc(done, 1)
            if o == 5:
                dve.wait_ge(done, at + 5)
                wait(dve, self.s_pool, self.POOLS * g)
                v.tensor_tensor(self.first[:, :, :], self.equal[:, :, :], self.over(self.rank),
                                ALU.is_equal).then_inc(done, 1)
            if o < 6:
                continue
            if self.soft:
                if o == 6:
                    dve.wait_ge(self.s_act, self.ACTS * g + 1)
                    v.tensor_reduce(self.total[:, :], self.exps[:, :, :], X, ALU.add).then_inc(done, 1)
                if o == 7:
                    dve.wait_ge(done, at + 6)
                    v.scalar_tensor_tensor(self.left[:, :, :], self.first[:, :, :], -3e38, self.exps[:, :, :],
                                           ALU.mult, ALU.add).then_inc(done, 1)
                if o == 8:
                    dve.wait_ge(done, at + 7)
                    v.reciprocal(self.inverse[:, :], self.total[:, :]).then_inc(done, 1)
                if o == 9:
                    dve.wait_ge(done, at + 8)
                    v.tensor_reduce(self.top2[:, :], self.left[:, :, :], X, ALU.max).then_inc(done, 1)
                if o == 10:
                    dve.wait_ge(done, at + 10)
                    v.tensor_tensor(self.less2[:, :, :], self.left[:, :, :], self.over(self.top2),
                                    ALU.subtract).then_inc(done, 1)
                if o == 11:
                    dve.wait_ge(done, at + 10)
                    v.scalar_tensor_tensor(self.gap[:, :], self.top2[:, :], 1.0, self.inverse[:, :], ALU.subtract,
                                           ALU.mult).then_inc(done, 1)
                if o == 12:
                    dve.wait_ge(done, at + 11)
                    v.scalar_tensor_tensor(self.equal2[:, :, :], self.less2[:, :, :], 0.0, rev, ALU.is_equal,
                                           ALU.mult).then_inc(done, 1)
                if o == 13:
                    dve.wait_ge(done, at + 13)
                    v.tensor_reduce(self.rank2[:, :], self.equal2[:, :, :], X, ALU.max).then_inc(done, 1)
                if o == 14:
                    dve.wait_ge(done, at + 14)
                    v.tensor_tensor(self.second[:, :, :], self.equal2[:, :, :], self.over(self.rank2),
                                    ALU.is_equal).then_inc(done, 1)
            else:
                dve.wait_ge(done, at + o)
                if o == 6:
                    v.scalar_tensor_tensor(self.left[:, :, :], self.first[:, :, :], -3e38, self.less[:, :, :],
                                           ALU.mult, ALU.add).then_inc(done, 1)
                if o == 7:
                    v.tensor_reduce(self.top2[:, :], self.left[:, :, :], X, ALU.max).then_inc(done, 1)
                if o == 8:
                    v.tensor_tensor(self.less2[:, :, :], self.left[:, :, :], self.over(self.top2),
                                    ALU.subtract).then_inc(done, 1)
                if o == 9:
                    v.scalar_tensor_tensor(self.equal2[:, :, :], self.less2[:, :, :], 0.0, rev, ALU.is_equal,
                                           ALU.mult).then_inc(done, 1)
                if o == 10:
                    v.tensor_reduce(self.rank2[:, :], self.equal2[:, :, :], X, ALU.max).then_inc(done, 1)
                if o == 11:
                    v.tensor_tensor(self.second[:, :, :], self.equal2[:, :, :], self.over(self.rank2),
                                    ALU.is_equal).then_inc(done, 1)

    def exponentiate(self, act, g):
        act.wait_ge(self.s_dve, self.OPS * g + 3)
        self.nc.scalar.activation(self.exps[:, :, :], self.less[:, :, :], ACT.Exp).then_inc(self.s_act, 1)

    def tanh(self, act, g):
        act.wait_ge(self.s_dve, self.OPS * g + (12 if self.soft else 8))
        self.nc.scalar.activation(self.half_tanh[:, :], (self.gap if self.soft else self.top2)[:, :], ACT.Tanh,
                                  scale=-0.5).then_inc(self.s_act, 1)

    def weigh(self, pool, g):
        v, E, at = self.nc.gpsimd, self.E, self.POOLS * g
        pool.wait_ge(self.s_act, self.ACTS * g + self.ACTS)
        pool.wait_ge(self.s_dve, self.OPS * g + self.OPS)
        v.tensor_tensor(self.either[:, :, :], self.first[:, :, :], self.second[:, :, :], ALU.add).then_inc(self.s_pool, 1)
        v.tensor_tensor(self.sign[:, :, :], self.first[:, :, :], self.second[:, :, :], ALU.subtract).then_inc(self.s_pool, 1)
        pool.wait_ge(self.s_pool, at + 2)
        v.tensor_tensor(self.tilt[:, :, :], self.sign[:, :, :], self.over(self.half_tanh), ALU.mult).then_inc(self.s_pool, 1)
        pool.wait_ge(self.s_pool, at + 3)
        v.tensor_tensor(self.dense[:, :, :], self.either[:, :, :], self.tilt[:, :, :], ALU.add).then_inc(self.s_pool, 1)
        wait(pool, self.s_tr, g)
        v.tensor_tensor(self.parts[:, :, 0:E], self.either[:, :, :], self.tilt[:, :, :], ALU.add).then_inc(self.s_pool, 1)
        pool.wait_ge(self.s_pool, at + 5)
        v.tensor_tensor(self.parts[:, :, E:2 * E], self.dense[:, :, :], self.parts[:, :, 0:E], ALU.subtract).then_inc(self.s_pool, 1)

    def turn(self, pe, g, out):
        pe.wait_ge(self.s_pool, self.POOLS * g + self.POOLS)
        for b in range(GB):
            last = self.nc.tensor.transpose(out[:, b * TE:b * TE + T], self.parts[:, b, :], self.k.ch("identh")[0:T, 0:T])
        last.then_inc(self.s_tr, 1)

    def place(self, act, g, p, turned):
        act.wait_ge(self.s_tr, g + 1)
        self.nc.scalar.activation(self.wt[:, p, :].rearrange("p (b t) -> p b t", b=GB), turned, ACT.Copy).then_inc(self.s_wt, 1)


def columns_of(ap):
    return ap.rearrange("p (b t) -> p b t", b=GB)


def mix_experts(k):
    nc = k.nc
    with ExitStack() as ctx:
        k.ctx = ctx
        n = Norm(k, "e")
        gate = Gate(k, "e", E0, WS0, False, (k.hi["g0w"], k.lo["g0w"]), "g0b", "rev0")
        AHEAD, RING = 3, 4
        xt = k.sb("e_xt", [128, 2, N], F16)
        hid = k.sb("e_hidden", [128, RING, N])
        wh = k.sb("e_weighed", [128, RING, N])
        yt = k.sb("e_yt", [128, 2, N // 2])
        HB, WB, YB, XB, TB_ = 0, 2, 4, 6, 7
        bank = k.bank
        s_xt, s_h, s_g, s_wb, s_z, s_y, s_y2, s_yt, s_ytr, s_add = (k.sem("e_" + x) for x in (
            "x_columns", "hidden", "gelus", "weights_spread", "weighed", "chunks_added", "outputs", "outputs_copied",
            "outputs_turned", "added"))
        block = ctx.enter_context(nc.Block())
        w2 = k.c("w2").rearrange("p (c e) -> p c e", c=CH)
        b1 = k.c("b1")
        sel = k.ch("sel0").rearrange("p (e m) -> p e m", e=E0)

        @block.tensor
        def _(pe):
            def first(g, p, c):
                if not exists(g):
                    return
                if c == 0:
                    pe.wait_ge(s_xt, g + 1)
                wait(pe, s_g, CH * g + c - 1)
                for m, w in enumerate((k.hi["w1"], k.lo["w1"])):
                    last = nc.tensor.matmul(bank[HB + c % 2][:, 0:N], w[:, c * 128:(c + 1) * 128], xt[:, p, :],
                                            start=m == 0, stop=m == 1)
                last.then_inc(s_h, 1)

            def spread(g, p, e):
                if not exists(g):
                    return
                if e == 0:
                    pe.wait_ge(gate.s_wt, g + 1)
                wait(pe, s_z, CH * g + 2 * e - 2)
                nc.tensor.matmul(bank[WB + e % 2][:, 0:N], sel[:, e, :], gate.wt[:, p, :], start=True, stop=True).then_inc(s_wb, 1)

            def second(g, p, c):
                if not exists(g):
                    return
                pe.wait_ge(s_z, CH * g + c + 1)
                if c == 0:
                    wait(pe, s_yt, g - 1)
                for s in range(2):
                    last = nc.tensor.matmul(bank[YB + p][s * D:(s + 1) * D, 0:N // 2], w2[:, c, :],
                                            wh[:, c % RING, s * (N // 2):(s + 1) * (N // 2)], start=c == 0, stop=False)
                last.then_inc(s_y, 1)

            def biases(g, p):
                if not exists(g):
                    return
                for m, w in enumerate((k.hi["b2"], k.lo["b2"])):
                    for s in range(2):
                        last = nc.tensor.matmul(bank[YB + p][s * D:(s + 1) * D, 0:N // 2], w[:, :],
                                                gate.wt[:, p, s * (N // 2):(s + 1) * (N // 2)], start=False, stop=m == 1)
                last.then_inc(s_y2, 1)

            def turn_outputs(g, p):
                if not exists(g):
                    return
                pe.wait_ge(s_yt, g + 1)
                for b in range(2):
                    last = nc.tensor.transpose(bank[TB_][0:T, b * 128:(b + 1) * 128], yt[:, p, b * T:(b + 1) * T], k.c("ident"))
                last.then_inc(s_ytr, 1)

            def steps(i, p):
                q = 1 - p
                for c in range(CH):
                    ahead = c + AHEAD
                    first(i if ahead < CH else i + 1, p if ahead < CH else q, ahead % CH)
                    if c == 10 and exists(i + 2):
                        wait(pe, gate.s_dve, gate.OPS * (i + 1) + 1)
                        n.turn(pe, i + 2, p, k.half(XB))
                    if c == 14 and exists(i + 2):
                        pe.wait_ge(s_xt, i + 3)
                        gate.multiply(pe, i + 2, xt[:, p, :], bank[XB])
                    if c == 3:
                        turn_outputs(i - 1, q)
                    if c == 13 and exists(i + 1):
                        wait(pe, s_add, i)
                        gate.turn(pe, i + 1, k.half(TB_))
                    if c % 2 == 0:
                        e = c // 2 + 1
                        spread(i if e < E0 else i + 1, p if e < E0 else q, e % E0)
                    second(i, p, c)
                biases(i, p)

            pe.wait_ge(gate.s_zero, 1)
            pipeline(pe, steps, -2, 2, NG - 4)

        @block.scalar
        def _(act):
            def gelu(g, p, c):
                if not exists(g):
                    return
                act.wait_ge(s_h, CH * g + c + 1)
                wait(act, s_z, CH * g + c - RING + 1)
                nc.scalar.activation(hid[:, c % RING, :], bank[HB + c % 2][:, 0:N], ACT.Gelu, bias=b1[:, c:c + 1],
                                     scale=1.0 / WS0).then_inc(s_g, 1)

            def steps(i, p):
                q = 1 - p
                for c in range(CH):
                    ahead = c + AHEAD
                    gelu(i if ahead < CH else i + 1, p if ahead < CH else q, ahead % CH)
                    if c == 1 and exists(i - 1):
                        act.wait_ge(s_y2, i)
                        wait(act, s_ytr, i - 2)
                        nc.scalar.activation(yt[:, q, :], bank[YB + q][:, 0:N // 2], ACT.Copy).then_inc(s_yt, 1)
                    if c == 8 and exists(i + 1):
                        gate.tanh(act, i + 1)
                    if c == 12 and exists(i + 2):
                        act.wait_ge(n.tr, i + 3)
                        wait(act, s_h, CH * (i + 1))
                        wait(act, gate.s_log, i + 1)
                        nc.scalar.activation(columns_of(xt[:, p, :]), k.turned(XB), ACT.Copy).then_inc(s_xt, 1)
                    if c == 13 and exists(i + 1):
                        wait(act, s_y2, i)
                        gate.place(act, i + 1, q, k.turned(TB_))

            pipeline(act, steps, -2, 2, NG - 4)

        @block.gpsimd
        def _(pool):
            def steps(i, p):
                if exists(i + 2):
                    n.low(pool, i + 2, p)
                if exists(i + 1):
                    gate.weigh(pool, i + 1)
                if exists(i + 3):
                    n.root(pool, i + 3, 1 - p)

            nc.gpsimd.memset(gate.parts[:, :, :].rearrange("p b c -> p (b c)"), 0.0).then_inc(gate.s_zero, 1)
            pool.wait_ge(gate.s_zero, 1)
            pipeline(pool, steps, -3, 2, NG - 4)

        @block.vector
        def _(dve):
            def weigh(g, c):
                if not exists(g):
                    return
                dve.wait_ge(s_g, CH * g + c + 1)
                if c % 2 == 0:
                    dve.wait_ge(s_wb, E0 * g + c // 2 + 1)
                wait(dve, s_y, CH * g + c - RING + 1)
                nc.vector.tensor_tensor(wh[:, c % RING, :], hid[:, c % RING, :], bank[WB + c // 2 % 2][:, 0:N],
                                        ALU.mult).then_inc(s_z, 1)

            CHOOSE = {1: (0,), 2: (1,), 3: (2,), 4: (3,), 5: (4,), 6: (5,), 7: (6,), 8: (7, 8), 9: (9,), 10: (10,),
                      11: (11,)}

            def steps(i, p):
                q = 1 - p
                for c in range(CH):
                    weigh(i, c)
                    if exists(i + 1):
                        gate.choose(dve, i + 1, bank[XB], CHOOSE.get(c, ()))
                    if c == 0 and exists(i + 2):
                        n.scale(dve, i + 2, p)
                    if c == 1 and exists(i + 2):
                        n.high(dve, i + 2, p)
                    if c == 7 and exists(i - 1):
                        dve.wait_ge(s_ytr, i)
                        out = bank[TB_][0:T, 0:GB * D].rearrange("p (b s e) -> p s b e", b=2, s=2)
                        h = k.H[:, group(i - 1), :].rearrange("p (s b) e -> p s b e", s=2)
                        nc.vector.tensor_tensor(h, h, out, ALU.add).then_inc(s_add, 1)
                    if exists(i + 3):
                        if c == 11:
                            n.stats(dve, i + 3, q, (0, 1))
                        if c == 12:
                            n.stats(dve, i + 3, q, (2, 3))
                        if c == 13:
                            n.aggregate(dve, i + 3, q, (0,))
                        if c == 14:
                            n.aggregate(dve, i + 3, q, (1,))
                            n.centre(dve, i + 3, q)
                            n.aggregate(dve, i + 3, q, (2,))

            pipeline(dve, steps, -3, 2, NG - 4)


def mix_time(k):
    nc = k.nc
    with ExitStack() as ctx:
        k.ctx = ctx
        n = Norm(k, "t")
        xt = k.sb("t_xt", [128, 2, GB, TE], F16)
        kc = k.sb("t_clipped", [T, 2, GB, D])
        ek = k.sb("t_exp_k", [T, 2, GB, D])
        er = k.sb("t_exp_r", [T, 2, GB, D])
        v = k.sb("t_v", [T, 2, GB, D])
        kv = k.sb("t_kv", [T, 2, GB, D])
        den = k.sb("t_den", [T, GB, D])
        inv = k.sb("t_inv", [T, GB, D])
        rw = k.sb("t_rw", [T, 2, GB, D])
        rt = k.sb("t_rwt", [128, 2, 2 * T])
        KVR, SUM, XB, RT, OUT = 0, 2, 4, 5, 6
        bank = k.bank
        (s_set, s_xt, s_kvr, s_clip, s_ek, s_er, s_v, s_kv, s_sum, s_den, s_inv, s_rw, s_rtr, s_rt, s_out, s_add) = (
            k.sem("t_" + x) for x in ("zeroed", "x_columns", "kvr", "clipped", "exp_k", "exp_r", "v_copied", "kv", "sums",
                                      "denominators", "inverses", "rw", "rw_turned", "rw_copied", "outputs", "added"))
        block = ctx.enter_context(nc.Block())

        def kvr(q, which):
            return bank[KVR + q][0:T, 0:6 * D].rearrange("p (b n e) -> p b n e", b=2, n=3)[:, :, which, :]

        @block.tensor
        def _(pe):
            def sums(g, p):
                if not exists(g):
                    return
                pe.wait_ge(s_kv, g + 1)
                wait(pe, s_rw, g - 1)
                nc.tensor.matmul(bank[SUM + p][0:T, 0:GB * D], k.time[:, :], kv[:, p, :, :].rearrange("p b e -> p (b e)"),
                                 start=True, stop=True)
                nc.tensor.matmul(bank[SUM + p][0:T, GB * D:2 * GB * D], k.c("tri")[0:T, :],
                                 ek[:, p, :, :].rearrange("p b e -> p (b e)"), start=True, stop=True).then_inc(s_sum, 1)

            def multiply(g, p):
                if not exists(g):
                    return
                pe.wait_ge(s_xt, g + 1)
                for b in range(GB):
                    if b % 2 == 0:
                        wait(pe, s_clip, 2 * g - 2 + b // 2 + 1)
                        wait(pe, s_er, 2 * g - 2 + b // 2 + 1)
                        wait(pe, s_v, 2 * g - 2 + b // 2 + 1)
                    terms = [(1, k.hi["kvra"]), (1, k.lo["kvra"]), (0, k.hi["kvrb"]), (0, k.lo["kvrb"])]
                    for m, (at, w) in enumerate(terms):
                        last = nc.tensor.matmul(bank[KVR + b // 2][0:T, b % 2 * 3 * D:(b % 2 + 1) * 3 * D],
                                                xt[:, p, b, at:at + T], w[:, :], start=m == 0, stop=m == 3)
                    if b % 2 == 1:
                        last.then_inc(s_kvr, 1)

            def turn_quotients(g, p):
                if not exists(g):
                    return
                pe.wait_ge(s_rw, g + 1)
                wait(pe, s_rt, g)
                for s in range(2):
                    last = nc.tensor.transpose(bank[RT][:, s * T:(s + 1) * T],
                                               rw[:, p, 2 * s:2 * s + 2, :].rearrange("p b e -> p (b e)"),
                                               k.c("ident")[0:T, 0:T])
                last.then_inc(s_rtr, 1)

            def output(g, p):
                if not exists(g):
                    return
                pe.wait_ge(s_rt, g + 1)
                wait(pe, s_add, g)
                for s in range(2):
                    last = nc.tensor.matmul(bank[OUT][0:T, s * 128:(s + 1) * 128], rt[:, p, s * T:(s + 1) * T],
                                            k.c("wo"), start=True, stop=True)
                last.then_inc(s_out, 1)

            def steps(i, p):
                q = 1 - p
                sums(i + 1, q)
                turn_quotients(i, p)
                multiply(i + 2, p)
                output(i, p)
                if exists(i + 3):
                    wait(pe, s_xt, i + 3)
                    n.turn(pe, i + 3, q, k.half(XB))

            pipeline(pe, steps, -4, 2, NG - 6)

        @block.scalar
        def _(act):
            def steps(i, p):
                q = 1 - p
                if exists(i):
                    act.wait_ge(s_rtr, i + 1)
                    wait(act, s_out, i - 1)
                    nc.scalar.activation(rt[:, p, :], bank[RT][:, 0:2 * T], ACT.Copy).then_inc(s_rt, 1)
                g = i + 2
                if exists(g):
                    wait(act, s_den, g - 1)
                    wait(act, s_kv, g - 1)
                    for b in range(2):
                        act.wait_ge(s_clip, 2 * g + b + 1)
                        nc.scalar.activation(er[:, p, 2 * b:2 * b + 2, :], kvr(b, 2), ACT.Exp, scale=-1.0 / WS1).then_inc(s_er, 1)
                        nc.scalar.activation(v[:, p, 2 * b:2 * b + 2, :], kvr(b, 1), ACT.Copy, scale=1.0 / WS1).then_inc(s_v, 1)
                    wait(act, s_sum, g - 1)
                    nc.scalar.activation(ek[:, p, :, :], kc[:, p, :, :], ACT.Exp, scale=1.0 / WS1).then_inc(s_ek, 1)
                if exists(i + 3):
                    act.wait_ge(n.tr, i + 4)
                    wait(act, s_kvr, 2 * (i + 2))
                    nc.scalar.activation(xt[:, q, :, 1:TE], k.turned(XB), ACT.Copy).then_inc(s_xt, 1)

            act.wait_ge(s_set, 1)
            pipeline(act, steps, -4, 2, NG - 6)

        @block.gpsimd
        def _(pool):
            def steps(i, p):
                if exists(i + 4):
                    n.root(pool, i + 4, p)
                if exists(i + 2):
                    g = i + 2
                    pool.wait_ge(s_ek, g + 1)
                    pool.wait_ge(s_v, 2 * g + 2)
                    wait(pool, s_sum, g - 1)
                    nc.gpsimd.tensor_tensor(kv[:, p, :, :], ek[:, p, :, :], v[:, p, :, :], ALU.mult).then_inc(s_kv, 1)
                if exists(i + 4):
                    n.low(pool, i + 4, p)

            nc.gpsimd.memset(xt[:, :, :, :].rearrange("p a b c -> p (a b c)"), 0.0).then_inc(s_set, 1)
            pool.wait_ge(s_set, 1)
            pipeline(pool, steps, -4, 2, NG - 6)

        @block.vector
        def _(dve):
            def clip(g, p, b):
                if not exists(g):
                    return
                if b == 0:
                    wait(dve, s_ek, g - 1)
                dve.wait_ge(s_kvr, 2 * g + b + 1)
                nc.vector.tensor_scalar(kc[:, p, 2 * b:2 * b + 2, :], kvr(b, 0), 30.0 * WS1, -60.0 * WS1,
                                        ALU.min, ALU.max).then_inc(s_clip, 1)

            def steps(i, p):
                q = 1 - p
                ahead = exists(i + 4)
                sums = bank[SUM + q][0:T, :].rearrange("p (w b e) -> p w b e", w=2, b=GB)
                if ahead:
                    n.stats(dve, i + 4, p)
                if exists(i + 1):
                    g = i + 1
                    dve.wait_ge(s_sum, g + 1)
                    dve.wait_ge(s_er, 2 * g + 2)
                    wait(dve, s_inv, g)
                    nc.vector.scalar_tensor_tensor(den[:, :, :], er[:, q, :, :], 1.0, sums[:, 1], ALU.add, ALU.mult).then_inc(s_den, 1)
                if ahead:
                    n.aggregate(dve, i + 4, p)
                    n.centre(dve, i + 4, p)
                clip(i + 2, p, 0)
                clip(i + 2, p, 1)
                if exists(i + 1):
                    g = i + 1
                    dve.wait_ge(s_den, g + 1)
                    wait(dve, s_rw, g)
                    nc.vector.reciprocal(inv[:, :, :], den[:, :, :]).then_inc(s_inv, 1)
                if ahead:
                    n.scale(dve, i + 4, p)
                if exists(i + 1):
                    g = i + 1
                    dve.wait_ge(s_inv, g + 1)
                    wait(dve, s_rtr, g - 1)
                    nc.vector.tensor_tensor(rw[:, q, :, :], inv[:, :, :], sums[:, 0], ALU.mult).then_inc(s_rw, 1)
                if ahead:
                    n.high(dve, i + 4, p)
                if exists(i):
                    dve.wait_ge(s_out, i + 1)
                    nc.vector.tensor_tensor(k.H[:, group(i), :], k.H[:, group(i), :],
                                            bank[OUT][0:T, 0:GB * D].rearrange("p (b e) -> p b e", b=GB),
                                            ALU.add).then_inc(s_add, 1)

            pipeline(dve, steps, -4, 2, NG - 6)


def mix_mlps(k, a_out):
    nc = k.nc
    with ExitStack() as ctx:
        k.ctx = ctx
        n = Norm(k, "m")
        gate = Gate(k, "m", E1, WSF, True, (k.hi["g1w"], k.lo["g1w"]), "g1b", "rev1")
        xt = k.sb("m_xt", [128, 2, N], F16)
        h1 = k.sb("m_h1", [128, 5, N])
        h2 = k.sb("m_h2", [128, 2, 3, N])
        hw = k.sb("m_h2w", [128, 2, 2, N])
        yt = k.sb("m_yt", [128, 2, N // 2])
        H1B, H2B, WB, YB, XB, TB_ = 0, 2, 4, 5, 6, 7
        bank = k.bank
        (s_xt, s_h1, s_a1, s_d1, s_h2, s_a2, s_wb, s_z, s_y, s_yt, s_ytr, s_add, s_store) = (k.sem("m_" + x) for x in (
            "x_columns", "first_layers", "firsts_by_scalar", "firsts_by_vector", "second_layers", "seconds", "weights_spread",
            "weighed", "outputs", "outputs_copied", "outputs_turned", "added", "stored"))
        block = ctx.enter_context(nc.Block())
        ORDER = (1, 2, 3, 4, 0)
        fb1, fb2 = k.c("fb1"), k.c("fb2")
        w2e = k.c("fw2e").rearrange("p (e m) -> p e m", e=E1)
        w3 = k.c("fw3").rearrange("p (i m) -> p i m", i=3)
        sel = k.ch("sel1").rearrange("p (j m) -> p j m", j=2)

        @block.sync
        def _(sp):
            def steps(i, p):
                sp.wait_ge(s_add, i + 1)
                sp.dma_start(a_out[:, group(i), :], k.H[:, group(i), :]).then_inc(s_store, 16)

            with sp.Fori(0, NG) as i:
                steps(i, 0)
            sp.wait_ge(s_store, 16 * NG)

        @block.tensor
        def _(pe):
            def first(g, p, j):
                if not exists(g):
                    return
                c = ORDER[j]
                if j % 2 == 0:
                    wait(pe, s_a1, 3 * g + j // 2)
                else:
                    wait(pe, s_d1, 2 * g + j // 2)
                for m, w in enumerate((k.hi["fw1"], k.lo["fw1"])):
                    last = nc.tensor.matmul(bank[H1B + j % 2][:, 0:N], w[:, c * 128:(c + 1) * 128], xt[:, p, :],
                                            start=m == 0, stop=m == 1)
                last.then_inc(s_h1, 1)

            def second(g, p, j):
                if not exists(g):
                    return
                pe.wait_ge(s_a1, 3 * g + j + 1)
                if j < 2:
                    pe.wait_ge(s_d1, 2 * g + j + 1)
                wait(pe, s_a2, 3 * g + j - 1 if j else 3 * g)
                at = bank[H2B + j % 2]
                if j < 2:
                    for s in range(2):
                        last = nc.tensor.matmul(at[s * D:(s + 1) * D, 0:N], w2e[:, 2 * j + s, :], h1[:, 1 + 2 * j + s, :],
                                                start=True, stop=True)
                else:
                    last = nc.tensor.matmul(at[:, 0:N], k.c("fw2s"), h1[:, 0, :], start=True, stop=True)
                last.then_inc(s_h2, 1)

            def spread(g, p, j):
                if not exists(g):
                    return
                if j == 0:
                    pe.wait_ge(gate.s_wt, g + 1)
                wait(pe, s_z, 2 * g + j)
                nc.tensor.matmul(bank[WB][:, 0:N], sel[:, j, :], gate.wt[:, p, :], start=True, stop=True).then_inc(s_wb, 1)

            def third(g, p):
                if not exists(g):
                    return
                pe.wait_ge(s_z, 2 * g + 2)
                pe.wait_ge(s_a2, 3 * g + 3)
                wait(pe, s_yt, g)
                for s in range(2):
                    cols = slice(s * (N // 2), (s + 1) * (N // 2))
                    out = bank[YB][s * D:(s + 1) * D, 0:N // 2]
                    nc.tensor.matmul(out, w3[:, 0, :], h2[:, p, 0, cols], start=True, stop=False)
                for s in range(2):
                    cols = slice(s * (N // 2), (s + 1) * (N // 2))
                    out = bank[YB][s * D:(s + 1) * D, 0:N // 2]
                    for m, w in enumerate((k.hi["fb3"], k.lo["fb3"])):
                        nc.tensor.matmul(out, w[:, :], gate.wt[:, p, cols], start=False, stop=False)
                for j in range(2):
                    for s in range(2):
                        cols = slice(s * (N // 2), (s + 1) * (N // 2))
                        last = nc.tensor.matmul(bank[YB][s * D:(s + 1) * D, 0:N // 2], w3[:, 1 + j, :], hw[:, p, j, cols],
                                                start=False, stop=j == 1)
                last.then_inc(s_y, 1)

            def turn_outputs(g, p):
                if not exists(g):
                    return
                pe.wait_ge(s_yt, g + 1)
                wait(pe, s_add, g)
                for b in range(2):
                    last = nc.tensor.transpose(bank[TB_][0:T, b * 128:(b + 1) * 128], yt[:, p, b * T:(b + 1) * T], k.c("ident"))
                last.then_inc(s_ytr, 1)

            def steps(i, p):
                q = 1 - p
                first(i, p, 0)
                first(i, p, 1)
                third(i - 2, p)
                first(i, p, 2)
                second(i, p, 0)
                first(i, p, 3)
                if exists(i - 1):
                    wait(pe, s_add, i - 2)
                    gate.turn(pe, i - 1, k.half(TB_))
                if exists(i + 1):
                    wait(pe, gate.s_dve, gate.OPS * i + 1)
                    n.turn(pe, i + 1, q, k.half(XB))
                first(i, p, 4)
                spread(i - 1, q, 0)
                second(i, p, 1)
                spread(i - 1, q, 1)
                turn_outputs(i - 2, p)
                second(i, p, 2)
                if exists(i + 1):
                    pe.wait_ge(s_xt, i + 2)
                    gate.multiply(pe, i + 1, xt[:, q, :], bank[XB])

            pe.wait_ge(gate.s_zero, 1)
            pipeline(pe, steps, -1, 4, NG - 4, NG + 1)

        @block.scalar
        def _(act):
            def first(g, p, j):
                if not exists(g):
                    return
                c = ORDER[j]
                act.wait_ge(s_h1, 5 * g + j + 1)
                wait(act, s_h2, 3 * (g - 1) + j // 2 + 1)
                nc.scalar.activation(h1[:, c, :], bank[H1B][:, 0:N], ACT.Relu, bias=fb1[:, c:c + 1], scale=1.0 / WSF).then_inc(s_a1, 1)

            def second(g, p, j):
                if not exists(g):
                    return
                c = (j + 1) % 3
                act.wait_ge(s_h2, 3 * g + j + 1)
                wait(act, s_y, g - 1)
                nc.scalar.activation(h2[:, p, c, :], bank[H2B + j % 2][:, 0:N], ACT.Relu, bias=fb2[:, c:c + 1]).then_inc(s_a2, 1)

            def steps(i, p):
                q = 1 - p
                first(i, p, 0)
                if exists(i):
                    gate.exponentiate(act, i)
                if exists(i - 2):
                    act.wait_ge(s_y, i - 1)
                    wait(act, s_ytr, i - 3)
                    nc.scalar.activation(yt[:, p, :], bank[YB][:, 0:N // 2], ACT.Identity, bias=k.c("sb3")).then_inc(s_yt, 1)
                first(i, p, 2)
                second(i, p, 0)
                if exists(i - 1):
                    wait(act, s_y, i - 2)
                    gate.place(act, i - 1, q, k.turned(TB_))
                if exists(i + 1):
                    act.wait_ge(n.tr, i + 2)
                    wait(act, s_h1, 5 * i)
                    wait(act, gate.s_log, i)
                    nc.scalar.activation(columns_of(xt[:, q, :]), k.turned(XB), ACT.Copy).then_inc(s_xt, 1)
                first(i, p, 4)
                second(i, p, 1)
                second(i, p, 2)
                if exists(i):
                    gate.tanh(act, i)

            pipeline(act, steps, -1, 4, NG - 4, NG + 1)

        @block.gpsimd
        def _(pool):
            def steps(i, p):
                if exists(i + 2):
                    n.root(pool, i + 2, p)
                if exists(i):
                    gate.weigh(pool, i)
                if exists(i + 2):
                    n.low(pool, i + 2, p)

            nc.gpsimd.memset(gate.parts[:, :, :].rearrange("p b c -> p (b c)"), 0.0).then_inc(gate.s_zero, 1)
            pool.wait_ge(gate.s_zero, 1)
            pipeline(pool, steps, -2, 4, NG - 4, NG + 1)

        @block.vector
        def _(dve):
            def first(g, p, j):
                if not exists(g):
                    return
                c = ORDER[j]
                dve.wait_ge(s_h1, 5 * g + j + 1)
                wait(dve, s_h2, 3 * (g - 1) + j // 2 + 1)
                nc.vector.tensor_scalar(h1[:, c, :], bank[H1B + 1][:, 0:N], fb1[:, c:c + 1], 0.0, ALU.add, ALU.max).then_inc(s_d1, 1)

            def weigh(g, p, j):
                if not exists(g):
                    return
                dve.wait_ge(s_wb, 2 * g + j + 1)
                dve.wait_ge(s_a2, 3 * g + j + 1)
                wait(dve, s_y, g - 1)
                nc.vector.tensor_tensor(hw[:, p, j, :], h2[:, p, 1 + j, :], bank[WB][:, 0:N], ALU.mult).then_inc(s_z, 1)

            def choose(g, *ops):
                if exists(g):
                    gate.choose(dve, g, bank[XB], ops)

            def steps(i, p):
                q = 1 - p
                two = exists(i + 2)
                choose(i, 0)
                first(i, p, 1)
                choose(i, 1)
                if two:
                    n.stats(dve, i + 2, p, (0, 1))
                choose(i, 2)
                if two:
                    n.stats(dve, i + 2, p, (2,))
                choose(i, 3)
                if two:
                    n.stats(dve, i + 2, p, (3,))
                choose(i, 4)
                if two:
                    n.aggregate(dve, i + 2, p, (0,))
                choose(i, 5, 6)
                first(i, p, 3)
                choose(i, 7, 8)
                if two:
                    n.aggregate(dve, i + 2, p, (1,))
                choose(i, 9)
                weigh(i - 1, q, 0)
                choose(i, 10, 11)
                if two:
                    n.aggregate(dve, i + 2, p, (2,))
                    n.centre(dve, i + 2, p)
                choose(i, 12)
                weigh(i - 1, q, 1)
                choose(i, 13)
                if exists(i - 2):
                    dve.wait_ge(s_ytr, i - 1)
                    out = bank[TB_][0:T, 0:GB * D].rearrange("p (b s e) -> p s b e", b=2, s=2)
                    h = k.H[:, group(i - 2), :].rearrange("p (s b) e -> p s b e", s=2)
                    nc.vector.tensor_tensor(h, h, out, ALU.add).then_inc(s_add, 1)
                choose(i, 14)
                if two:
                    n.scale(dve, i + 2, p)
                    n.high(dve, i + 2, p)

            pipeline(dve, steps, -2, 4, NG - 4, NG + 1)


def build(nc, a_x, a_txt, a_tw, a_f32, a_f16, a_out):
    with ExitStack() as ctx:
        k = Core(nc, ctx)
        embed(k, a_x, a_txt, a_tw, a_f32, a_f16)
        attend(k)
        mix_experts(k)
        mix_time(k)
        mix_mlps(k, a_out)


def lay_out(inputs):
    z = {n: np.asarray(a) for n, a in inputs.items()}
    f = {}

    def put(name, rows_, array):
        a = f.setdefault(name, np.zeros((128, pieces()[0][name]), np.float32))
        a[rows_] = array

    both = [slice(0, D), slice(D, 2 * D)]
    everywhere = slice(0, 128)
    x = z["x"].reshape(4, 4, 8, 3, 4, 16, 4, 16).transpose(0, 3, 5, 7, 1, 4, 6, 2)
    x = np.ascontiguousarray(x.reshape(4, 6, 128, 512).transpose(0, 2, 1, 3))
    txt = np.ascontiguousarray(z["txt"].transpose(1, 0, 2))
    put("tokw", everywhere, z["L0_tok_W"].T.reshape(6, 128, D).transpose(1, 0, 2).reshape(128, 6 * D))
    qkvb = z["L0_attn_qkv_b"]
    for r in both:
        put("tokb", r, z["L0_tok_b"][:, None])
        put("qkvw", r, z["L0_attn_qkv_w"])
        put("qb", r, qkvb[0:D, None])
        put("kb", r, qkvb[D:2 * D, None])
    put("vb", everywhere, np.repeat(qkvb[2 * D:].reshape(4, 1, 16), 2, 1).reshape(128, 1))
    put("pb", slice(0, 1), z["L0_attn_proj_b"])
    wp = np.zeros((4, 2, 16, 2, D), np.float32)
    for s in range(2):
        wp[:, s, :, s] = z["L0_attn_proj_w"].reshape(4, 16, D)
    put("wp", everywhere, wp.reshape(128, 2 * D))
    feature = np.arange(128) % D
    put("hmask", everywhere, feature[:, None] // HD == np.arange(HEADS))
    put("ident", everywhere, np.eye(128))
    put("rev0", everywhere, np.arange(E0, 0, -1))
    put("rev1", everywhere, np.arange(E1, 0, -1))
    for r in both:
        put("g0w", r, z["L0_ffn_Wg"])
        put("w1", r, z["L0_ffn_W1"].transpose(1, 0, 2).reshape(D, E0 * H0))
        kvrw = np.concatenate([z["L1_attn_Wk"], z["L1_attn_Wv"], z["L1_attn_Wr"]], 1)
        put("kvrw", r, kvrw)
        put("mix", r, np.concatenate([z[f"L1_attn_time_mix_{n}"].reshape(1, D) for n in "kvr"]).T)
        put("g1w", r, z["L1_ffn_gW"])
        put("sb3", r, z["L1_ffn_sb3"][:, None])
    put("g0b", everywhere, z["L0_ffn_bg"])
    put("g1b", everywhere, z["L1_ffn_gb"])
    put("b1", everywhere, z["L0_ffn_b1"].reshape(CH, 128).T)
    put("w2", everywhere, z["L0_ffn_W2"].reshape(CH, 128, D).transpose(1, 0, 2).reshape(128, CH * D))
    for i in range(2):
        put("b2", slice(i * E0, (i + 1) * E0), z["L0_ffn_b2"])
        put("fb3", slice(i * E1, (i + 1) * E1), z["L1_ffn_eb3"])
    wo = np.zeros((2, D, 2, D), np.float32)
    for s in range(2):
        wo[s, :, s] = z["L1_attn_Wo"]
    put("wo", everywhere, wo.reshape(128, 128))
    put("flip", slice(0, T), np.eye(T)[::-1])
    put("tri", slice(0, T), np.triu(np.ones((T, T))))
    fw1 = np.zeros((D, 5, 128), np.float32)
    fw1[:, 0, 0:D] = z["L1_ffn_sW1"]
    fw1[:, 1:] = z["L1_ffn_eW1"].transpose(1, 0, 2)
    for r in both:
        put("fw1", r, fw1.reshape(D, 640))
    fb1 = np.zeros((128, 5), np.float32)
    fb1[0:D, 0] = z["L1_ffn_sb1"]
    fb1[:, 1:] = z["L1_ffn_eb1"].T
    put("fb1", everywhere, fb1)
    put("fw2s", slice(0, D), z["L1_ffn_sW2"])
    put("fw2e", everywhere, z["L1_ffn_eW2"].transpose(1, 0, 2).reshape(128, E1 * D))
    put("fb2", everywhere, np.stack([z["L1_ffn_sb2"], z["L1_ffn_eb2"][0:2].reshape(-1), z["L1_ffn_eb2"][2:4].reshape(-1)], 1))
    put("fw3", everywhere, np.concatenate([z["L1_ffn_sW3"], z["L1_ffn_eW3"][0:2].reshape(128, D),
                                           z["L1_ffn_eW3"][2:4].reshape(128, D)], 1))
    h = {n: np.zeros((128, w), np.float16) for n, w in pieces()[1].items()}
    h["identh"][:] = np.eye(128)
    h["onesh"][0] = 1
    sel0 = h["sel0"].reshape(128, E0, 128)
    for e in range(E0):
        sel0[[e, E0 + e], e] = 0.5
    sel1 = h["sel1"].reshape(128, 2, 2, D)
    for e in range(E1):
        sel1[[e, E1 + e], e // 2, e % 2] = 0.5
    tw = np.concatenate([z["L1_attn_time_w"], np.zeros(T, np.float32)])[::-1]
    return dict(x=x, txt=txt, tw=np.ascontiguousarray(tw), f32=np.concatenate([f[n] for n in pieces()[0]], 1),
                f16=np.concatenate([h[n] for n in pieces()[1]], 1))


def kernel(**inputs):
    import concourse.bacc as bacc
    from concourse.bass_utils import run_bass_kernel_spmd

    arrays = lay_out(inputs)
    nc = bacc.Bacc("TRN2", target_bir_lowering=False, num_devices=1)
    args = [nc.dram_tensor(f"in_{n}", a.shape, mybir.dt.from_np(a.dtype), kind="ExternalInput").ap()
            for n, a in arrays.items()]
    out = nc.dram_tensor("out", (T, B, D), F32, kind="ExternalOutput").ap()
    build(nc, *args, out)
    r = run_bass_kernel_spmd(nc, [{f"in_{n}": a for n, a in arrays.items()}], core_ids=[0])
    return np.ascontiguousarray(r.results[0]["out"].transpose(1, 0, 2))
```

```python
from contextlib import ExitStack

import math

import numpy as np
import concourse.bass as bass
from concourse import mybir

ALU = mybir.AluOpType
ACT = mybir.ActivationFunctionType
F32 = mybir.dt.float32
F16 = mybir.dt.float16
X = mybir.AxisListType.X

B = 128
D = 64
PATCHES = 16
TEXT = 77
T = PATCHES + TEXT
GB = 4
AGG = 4
NG = B // GB
N = GB * T
TE = T + 1
EPS = 1e-5

HEADS, HD = 8, 8
WIN = 64
W1Q = T - WIN
PADS = WIN - W1Q
W1K = W1Q + 1
TP = 96
SCALE = float(HD) ** -0.5

E0, H0 = 8, 256
CH = E0 * H0 // 128
WS0 = 64.0
WSQ = 16.0
WS1 = 16.0
WSF = 16.0
E1 = 4


def wait(eng, sem, value):
    if isinstance(value, int) and value <= 0:
        return
    eng.wait_ge(sem, value)


UNROLL = 4


def pipeline(eng, steps, first, loop_from, loop_to, last=NG, pause_at=None, pause=None):
    def turns(start, end):
        with eng.Fori(0, (end - start) // UNROLL) as turn:
            i = eng.snap(turn * UNROLL + start)
            for j in range(UNROLL):
                steps(i + j, (start + j) % 2)

    for i in range(first, loop_from):
        steps(i, i % 2)
    if pause_at is None:
        turns(loop_from, loop_to)
    else:
        turns(loop_from, pause_at)
        pause()
        turns(pause_at, loop_to)
    for i in range(loop_to, last + 1):
        steps(i, i % 2)


def exists(g):
    return not isinstance(g, int) or 0 <= g < NG


def pieces():
    f32 = dict(tokw=6 * D, tokb=1, flip=T, ident=128, qkvw=3 * D, qb=1, kb=1, vb=1, pb=D, wp=2 * D, hmask=HEADS,
               g0w=E0, g0b=E0, rev0=E0, w1=E0 * H0, b1=CH, w2=CH * D, b2=D,
               kvrw=3 * D, mix=3, wo=128, tri=T,
               g1w=E1, g1b=E1, rev1=E1, fw1=5 * 128, fb1=5, fw2s=128, fw2e=E1 * D, fb2=3, fw3=3 * D,
               fb3=D, sb3=1)
    f16 = dict(identh=128, onesh=TP, sel0=E0 * 128, sel1=2 * 128)
    return f32, f16


def offsets(cols):
    at, out = 0, {}
    for name, n in cols.items():
        out[name] = (at, at + n)
        at += n
    return out, at



F32_AT, F32_COLS = offsets(pieces()[0])
FIRST_COLS = F32_AT["g0w"][0]
F16_AT, F16_COLS = offsets(pieces()[1])
SPLIT = dict(qkvw=(3 * D, WSQ), g0w=(E0, WS0), w1=(E0 * H0, WS0), b2=(D, 0.5), pb=(D, 1.0),
             kvra=(3 * D, WS1), kvrb=(3 * D, WS1), g1w=(E1, WSF), fw1=(5 * 128, WSF), fb3=(D, 0.5))


def rows(g, b=0):
    return slice(g * GB + b, g * GB + b + 1) if isinstance(g, int) else bass.ds(g * GB + b, 1)


def group(g):
    return slice(g * GB, g * GB + GB) if isinstance(g, int) else bass.ds(g * GB, GB)


class Core:

    def __init__(self, nc, ctx):
        self.nc, self.ctx = nc, ctx
        self.c32 = self.sb("consts32", [128, F32_COLS])
        self.c16 = self.sb("consts16", [128, F16_COLS], F16)
        self.H = self.sb("residual", [T, B, D])
        self.bank = [ctx.enter_context(nc.psum_tensor(f"bank{i}", [128, 512], F32)) for i in range(8)]
        self.hi = {n: self.sb(f"{n}_hi", [128, w], F16) for n, (w, _) in SPLIT.items()}
        self.lo = {n: self.sb(f"{n}_lo", [128, w], F16) for n, (w, _) in SPLIT.items()}
        self.stats = self.sb("stats", [T, 2, GB, 6])
        self.both = self.sb("means_squares", [T, 2, GB, 2])
        self.apart = self.sb("means_apart", [T, 2, GB])
        self.apart2 = self.sb("means_apart_squared", [T, 2, GB])
        self.var = self.sb("variances", [T, 2, GB])
        self.vareps = self.sb("var_eps", [T, 2, GB])
        self.rstd = self.sb("rstd", [T, 2, GB])
        self.time = self.sb("time_weights", [T, T])
        self.neghalf = self.sb("neghalf", [T, GB])
        self.eps = self.sb("eps", [T, GB])
        self.xc = self.sb("centred", [T, 2, GB, D])
        self.xn = self.sb("normed", [T, 2, GB, D])
        self.xs = self.sb("norm_parts", [T, 2, GB, 2 * D], F16)

    def sb(self, name, shape, dt=F32):
        return self.ctx.enter_context(self.nc.sbuf_tensor(name, shape, dt))

    def sem(self, name):
        return self.ctx.enter_context(self.nc.semaphore(name))

    def c(self, name):
        return self.c32[:, F32_AT[name][0]:F32_AT[name][1]]

    def ch(self, name):
        return self.c16[:, F16_AT[name][0]:F16_AT[name][1]]

    def half(self, i):
        return self.bank[i][:, :].bitcast(F16)

    def turned(self, i):
        return self.half(i)[:, 0:GB * TE].rearrange("p (b t) -> p b t", b=GB)[:, :, 0:T]


class Norm:

    EARLY = 2

    def __init__(self, k, phase, before=None):
        self.k, self.nc = k, k.nc
        (self.bn, self.mv, self.eps, self.rstd, self.xc, self.xn, self.hi, self.lo, self.tr) = (
            k.sem(f"{phase}_{n}") for n in ("bn", "mv", "eps", "rstd", "xc", "xn", "hi", "lo", "turned"))
        self.added = k.sem(f"{phase}_added")
        self.before, self.after = before, None
        if before:
            before.after = self

    def owner(self, g):
        if not isinstance(g, int):
            return self, g
        if g >= NG:
            return (self.after, g - NG) if self.after and g < NG + self.EARLY else (None, g)
        return (None, g) if g < (self.EARLY if self.before else 0) else (self, g)

    def two_ago(self, eng, of, g, count):
        if isinstance(g, int) and g < 2:
            if self.before:
                eng.wait_ge(of(self.before), count(NG + g - 2))
        else:
            eng.wait_ge(of(self), count(g - 2))

    def stats(self, dve, g, p, batches=range(GB)):
        k = self.k
        n, g = self.owner(g)
        if not n:
            return
        if 0 in batches:
            n.two_ago(dve, lambda m: m.mv, g, lambda h: AGG * h + 2)
            if n is not self:
                dve.wait_ge(self.added, g + 1)
        for b in batches:
            self.nc.vector.bn_stats(k.stats[:, p, b, :], k.H[:, rows(g, b), :]).then_inc(n.bn, 1)

    def aggregate(self, dve, g, p, parts=range(3)):
        k, even, odd = self.k, 1, 4
        n, g = self.owner(g)
        if not n:
            return
        st = k.stats[:, p, :, :]
        if 0 in parts:
            dve.wait_ge(n.bn, GB * g + GB)
            n.two_ago(dve, lambda m: m.xc, g, lambda h: h + 1)
            self.nc.vector.tensor_tensor(k.both[:, p, :, :], st[:, :, even:even + 2], st[:, :, odd:odd + 2],
                                         ALU.add).then_inc(n.mv, 1)
            self.nc.vector.tensor_tensor(k.apart[:, p, :], st[:, :, even], st[:, :, odd],
                                         ALU.subtract).then_inc(n.mv, 1)
        if 1 in parts:
            dve.wait_ge(n.mv, AGG * g + 2)
            self.nc.vector.scalar_tensor_tensor(k.apart2[:, p, :], k.apart[:, p, :], 0.25, k.apart[:, p, :],
                                                ALU.mult, ALU.mult).then_inc(n.mv, 1)
        if 2 in parts:
            dve.wait_ge(n.mv, AGG * g + 3)
            n.two_ago(dve, lambda m: m.eps, g, lambda h: h + 1)
            self.nc.vector.scalar_tensor_tensor(k.var[:, p, :], k.both[:, p, :, 1], 1.0 / D, k.apart2[:, p, :],
                                                ALU.mult, ALU.add).then_inc(n.mv, 1)

    def root(self, pool, g, p):
        k = self.k
        n, g = self.owner(g)
        if not n:
            return
        pool.wait_ge(n.mv, AGG * g + AGG)
        n.two_ago(pool, lambda m: m.rstd, g, lambda h: h + 1)
        self.nc.gpsimd.tensor_tensor(k.vareps[:, p, :], k.var[:, p, :], k.eps[:, :], ALU.add).then_inc(n.eps, 1)
        pool.wait_ge(n.eps, g + 1)
        n.two_ago(pool, lambda m: m.xn, g, lambda h: h + 1)
        self.nc.gpsimd.tensor_tensor(k.rstd[:, p, :], k.vareps[:, p, :], k.neghalf[:, :],
                                     ALU.pow).then_inc(n.rstd, 1)

    def centre(self, dve, g, p):
        k = self.k
        n, g = self.owner(g)
        if not n:
            return
        dve.wait_ge(n.mv, AGG * g + 1)
        self.nc.vector.scalar_tensor_tensor(k.xc[:, p, :, :], k.both[:, p, :, 0:1].broadcast_to([T, GB, D]), -0.5,
                                            k.H[:, group(g), :], ALU.mult, ALU.add).then_inc(n.xc, 1)

    def scale(self, dve, g, p):
        k = self.k
        n, g = self.owner(g)
        if not n:
            return
        dve.wait_ge(n.rstd, g + 1)
        dve.wait_ge(n.xc, g + 1)
        n.two_ago(dve, lambda m: m.lo, g, lambda h: h + 1)
        self.nc.vector.tensor_tensor(k.xn[:, p, :, :], k.xc[:, p, :, :],
                                     k.rstd[:, p, :].unsqueeze(2).broadcast_to([T, GB, D]),
                                     ALU.mult).then_inc(n.xn, 1)

    def high(self, dve, g, p):
        k = self.k
        n, g = self.owner(g)
        if not n:
            return
        dve.wait_ge(n.xn, g + 1)
        n.two_ago(dve, lambda m: m.tr, g, lambda h: h + 1)
        self.nc.vector.tensor_copy(k.xs[:, p, :, 0:D], k.xn[:, p, :, :]).then_inc(n.hi, 1)

    def high_by_scalar(self, act, g, p):
        k = self.k
        n, g = self.owner(g)
        if not n:
            return
        act.wait_ge(n.xn, g + 1)
        n.two_ago(act, lambda m: m.tr, g, lambda h: h + 1)
        self.nc.scalar.activation(k.xs[:, p, :, 0:D], k.xn[:, p, :, :], ACT.Copy).then_inc(n.hi, 1)

    def low(self, pool, g, p):
        k = self.k
        n, g = self.owner(g)
        if not n:
            return
        pool.wait_ge(n.hi, g + 1)
        self.nc.gpsimd.tensor_tensor(k.xs[:, p, :, D:2 * D], k.xn[:, p, :, :], k.xs[:, p, :, 0:D],
                                     ALU.subtract).then_inc(n.lo, 1)

    def turn(self, pe, g, p, out):
        k = self.k
        pe.wait_ge(self.lo, g + 1)
        for b in range(GB):
            last = self.nc.tensor.transpose(out[:, b * TE:b * TE + T], k.xs[:, p, b, :], k.ch("identh")[0:T, 0:T])
        last.then_inc(self.tr, 1)


class Embed:

    NT, KC, TT = 4, 6, 512

    def __init__(self, k, a_x, a_txt, a_tw, a_f32, a_f16):
        self.k, self.nc = k, k.nc
        self.a_x, self.a_txt, self.a_tw, self.a_f32, self.a_f16 = a_x, a_txt, a_tw, a_f32, a_f16
        self.pixels = k.sb("pixels", [128, self.NT, self.KC, self.TT])
        self.tokens_t = k.sb("tokens_t", [128, self.TT])
        self.tokens = k.sb("tokens", [128, 4, 128])
        self.mixed = k.sb("mixed", [128, 2, 3, D])
        self.onemix = k.sb("onemix", [128, 3])
        self.hankel = k.sb("hankel", [T, T])
        self.s_tw, self.s_flip, self.s_time = k.sem("time_loaded"), k.sem("time_flipped"), k.sem("time_copied")
        self.s_first, self.s_rest, self.s_halves = (k.sem("consts_" + n) for n in ("first", "rest", "f16"))
        self.s_half = k.sem("halves_set")
        self.s_put0 = k.sem("first_tokens_put")
        self.s_txt = [k.sem(f"text_loaded{i}") for i in range(2)]
        self.s_pix = [k.sem(f"pixels_loaded{i}") for i in range(self.NT)]
        self.s_prod, self.s_bias = k.sem("tokens_multiplied"), k.sem("tokens_biased")
        self.s_turn, self.s_tok, self.s_put = k.sem("tokens_turned"), k.sem("tokens_copied"), k.sem("tokens_put")
        self.s_mix, self.s_spl, self.s_big = k.sem("weights_mixed"), k.sem("weights_split"), k.sem("large_weights_high")
        self.s_low = k.sem("large_weights_low")
        self.splits = 0

    def load(self, sp):
        k = self.k
        sp.dma_start(k.c32[:, 0:FIRST_COLS], self.a_f32[:, 0:FIRST_COLS]).then_inc(self.s_first, 16)
        for i in range(2):
            sp.dma_start(self.pixels[:, i, :, :], self.a_x[i]).then_inc(self.s_pix[i], 16)
        backwards = bass.AP(tensor=self.a_tw.tensor, offset=1, ap=[[1, T], [1, T]])
        sp.dma_start(self.hankel[:, :], backwards).then_inc(self.s_tw, 16)
        sp.dma_start(k.c16[:, :], self.a_f16).then_inc(self.s_halves, 16)
        sp.dma_start(k.H[PATCHES:T, 0:B // 2, :], self.a_txt[:, 0:B // 2, :]).then_inc(self.s_txt[0], 16)

    def load_rest(self, sp):
        k = self.k
        sp.wait_ge(self.s_put, 7 * 16)
        for i in range(2, 4):
            sp.dma_start(self.pixels[:, i, :, :], self.a_x[i]).then_inc(self.s_pix[i], 16)
        sp.dma_start(k.H[PATCHES:T, B // 2:B, :], self.a_txt[:, B // 2:B, :]).then_inc(self.s_txt[1], 16)
        sp.dma_start(k.c32[:, FIRST_COLS:F32_COLS], self.a_f32[:, FIRST_COLS:F32_COLS]).then_inc(self.s_rest, 16)

    def turn_time(self, pe, out):
        pe.wait_ge(self.s_first, 16)
        pe.wait_ge(self.s_tw, 16)
        self.nc.tensor.matmul(out[0:T, 0:T], self.k.c("flip")[0:T, :], self.hankel[:, :], start=True, stop=True).then_inc(self.s_flip, 1)

    def multiply(self, pe, piece, product, cols):
        k, nc, half = self.k, self.nc, int(piece > 0)
        tokw = k.c("tokw").rearrange("p (c e) -> p c e", c=self.KC)
        pe.wait_ge(self.s_first, 16)
        for s in range(2):
            pe.wait_ge(self.s_pix[2 * half + s], 16)
        for ci in range(self.KC):
            for s in range(2):
                last = nc.tensor.matmul(product[s * D:s * D + D, 0:cols.stop - cols.start], tokw[:, ci, :],
                                        self.pixels[:, 2 * half + s, ci, cols], start=ci == 0, stop=ci == self.KC - 1)
        last.then_inc(self.s_prod, 1)

    def turn(self, pe, piece, turned, cols):
        pe.wait_ge(self.s_bias, piece + 1)
        for j in range(cols.start // 128, cols.stop // 128):
            at = j * 128 - cols.start
            last = self.nc.tensor.transpose(turned[:, at:at + 128], self.tokens_t[:, j * 128:(j + 1) * 128], self.k.c("ident"))
        last.then_inc(self.s_turn, 1)

    def bias(self, act, piece, product, cols):
        act.wait_ge(self.s_first, 16)
        act.wait_ge(self.s_prod, piece + 1)
        self.nc.scalar.activation(self.tokens_t[:, cols], product[:, 0:cols.stop - cols.start], ACT.Identity,
                                  bias=self.k.c("tokb")).then_inc(self.s_bias, 1)

    def copy(self, act, piece, turned, cols):
        half = int(piece > 0)
        act.wait_ge(self.s_turn, piece + 1)
        wait(act, self.s_put, half * 7 * 16)
        wait(act, self.s_put0, half * 16)
        self.nc.scalar.activation(self.tokens[:, :, :].rearrange("p j e -> p (j e)")[:, cols],
                                  turned[:, 0:cols.stop - cols.start], ACT.Copy).then_inc(self.s_tok, 1)

    def put(self, queue, piece, cols, tiles=(0, 1)):
        half = int(piece > 0)
        queue.wait_ge(self.s_tok, piece + 1)
        for s in tiles:
            for j in range(cols.start // 128, cols.stop // 128):
                b = (2 * half + s) * 32 + 8 * j
                done = self.s_put if b else self.s_put0
                queue.dma_start(self.k.H[0:PATCHES, b:b + 8, :], self.tokens[:, j, s * D:s * D + D]).then_inc(done, 16)

    def arrived(self, dve, q):
        dve.wait_ge(self.s_put, (q * 8 + 7) * 16)
        dve.wait_ge(self.s_txt[q], 16)

    def first_arrived(self, dve):
        dve.wait_ge(self.s_put0, 16)
        dve.wait_ge(self.s_txt[0], 16)

    def split(self, dve, name, src):
        k, nc = self.k, self.nc
        by = SPLIT[name][1]
        nc.vector.tensor_scalar(k.hi[name][:, :], src, by, None, ALU.mult).then_inc(self.s_spl, 1)
        self.splits += 1
        dve.wait_ge(self.s_spl, self.splits)
        nc.vector.scalar_tensor_tensor(k.lo[name][:, :], src, by, k.hi[name][:, :], ALU.mult,
                                       ALU.subtract).then_inc(self.s_spl, 1)
        self.splits += 1

    def first_weights(self, dve):
        k, nc = self.k, self.nc
        dve.wait_ge(self.s_first, 16)
        self.split(dve, "qkvw", k.c("qkvw"))
        self.split(dve, "pb", k.c("pb"))
        for name, by in (("vb", WSQ), ("wp", 1 / WSQ)):
            nc.vector.tensor_scalar(k.c(name), k.c(name), by, None, ALU.mult).then_inc(self.s_spl, 1)
            self.splits += 1

    FIRST_SPLITS = 6

    PART = 512

    def large_weights(self, act, at):
        k = self.k
        act.wait_ge(self.s_rest, 16)
        name, cols = ("w1", slice(at, at + self.PART)) if at < E0 * H0 else ("fw1", slice(0, 5 * 128))
        self.nc.scalar.activation(k.hi[name][:, cols], k.c(name)[:, cols], ACT.Copy, scale=SPLIT[name][1]).then_inc(self.s_big, 1)

    def low_of_large(self, dve, at):
        k = self.k
        dve.wait_ge(self.s_big, at // self.PART + 1)
        name, cols = ("w1", slice(at, at + self.PART)) if at < E0 * H0 else ("fw1", slice(0, 5 * 128))
        self.nc.vector.scalar_tensor_tensor(k.lo[name][:, cols], k.c(name)[:, cols], SPLIT[name][1],
                                            k.hi[name][:, cols], ALU.mult, ALU.subtract).then_inc(self.s_low, 1)

    def mix_weights(self, dve):
        k, nc = self.k, self.nc
        dve.wait_ge(self.s_rest, 16)
        nc.vector.tensor_scalar(self.onemix[:, :], k.c("mix"), -1.0, 1.0, ALU.mult, ALU.add).then_inc(self.s_mix, 1)
        dve.wait_ge(self.s_mix, 1)
        for m, mix in enumerate((k.c("mix"), self.onemix[:, :])):
            for n in range(3):
                nc.vector.tensor_scalar(self.mixed[:, m, n, :], k.c("kvrw")[:, n * D:(n + 1) * D], mix[:, n:n + 1], None,
                                        ALU.mult).then_inc(self.s_mix, 1)

    def small_weights(self, dve):
        k, nc = self.k, self.nc
        for e in (1, 3):
            for w, by in ((k.c("fb1")[:, 1 + e:2 + e], WSF), (k.c("fw2e")[:, e * D:(e + 1) * D], 1 / WSF)):
                nc.vector.tensor_scalar(w, w, by, None, ALU.mult).then_inc(self.s_mix, 1)
        for name in ("g0w", "b2", "g1w", "fb3"):
            self.split(dve, name, k.c(name))

    def split_mixed(self, dve):
        dve.wait_ge(self.s_mix, 7)
        for m, name in enumerate(("kvra", "kvrb")):
            self.split(dve, name, self.mixed[:, m, :, :].rearrange("p n e -> p (n e)"))


def embed_and_attend(k, *inputs):
    nc = k.nc
    with ExitStack() as ctx:
        k.ctx = ctx
        em = Embed(k, *inputs)
        n = k.norms["a"]
        xt = k.sb("a_xt", [128, 2, N], F16)
        qd = k.sb("a_q", [128, 2, 2, 2 * TP])
        ks = k.sb("a_k", [128, 2, 2, T + 1])
        km = k.sb("a_kmask", [128, 2, 2, HEADS, T + 1])
        v0 = k.sb("a_v0", [128, 2, 2, 4, 2, 16])
        v1 = k.sb("a_v1", [128, 2, 2, 4, 2, 16])
        mx = k.sb("a_max", [128, 2, 3, HEADS])
        e0 = k.sb("a_e0", [128, 2, 2, HEADS, WIN])
        e1 = k.sb("a_e1", [128, 2, HEADS, 32])
        sm = k.sb("a_sum", [128, 2, 3, HEADS])
        rs = k.sb("a_rsum", [128, 2, 3, HEADS])
        p0 = k.sb("a_p0t", [128, 2, 2, 512])
        p1 = k.sb("a_p1t", [128, 2, 256])
        ot = k.sb("a_ot", [128, 2, 384])
        S0, SW, TA, TB_, O, QK, XV = 0, 2, 3, 4, 5, 6, 7
        bank = k.bank
        (s_set, s_xt, s_qk, s_q, s_k, s_km, s_v, s_ve, s_s, s_mx, s_sub, s_exp, s_pad, s_sum, s_rs, s_p, s_pt, s_pe,
         s_o, s_oe, s_y) = (k.sem("a_" + x) for x in (
             "buffers_set", "x_columns", "qk_multiplied", "q_placed", "k_placed", "k_masked", "v_multiplied",
             "v_placed", "scores", "maxima", "less_max", "exps", "padding_weighted", "sums", "inverses", "probs",
             "probs_turned", "probs_t_copied", "gathered", "gathered_copied", "projected"))
        block = ctx.enter_context(nc.Block())
        VE = 6
        SETS = 6
        hq, lq = k.hi["qkvw"], k.lo["qkvw"]

        def pair_cols(ap):
            return ap.rearrange("p (q s t) -> p q s t", q=2, s=2)

        def quarter(i):
            return i - SECOND + 1 if isinstance(i, int) and SECOND <= i < SECOND + 4 else 0

        def columns_of_piece(piece):
            return slice((piece - 1) * 128, piece * 128) if piece else slice(0, 512)

        @block.sync
        def _(sp):
            em.load(sp)
            em.put(sp, 0, columns_of_piece(0), (0,))
            em.load_rest(sp)
            for piece in range(1, 5):
                em.put(sp, piece, columns_of_piece(piece))

        SECOND = 1
        ARRIVED = NG // 2 - 6

        @block.tensor
        def _(pe):
            def values(g, p):
                if not exists(g):
                    return
                pe.wait_ge(s_xt, g + 1)
                for b in range(GB):
                    for m, w in enumerate((hq, lq)):
                        out = bank[XV][0:T, 0:GB * D].rearrange("p (q j s f) -> p q s j f", q=2, j=4, s=2)
                        last = nc.tensor.matmul(out[:, b // 2, b % 2, :, :], xt[:, p, b * T:(b + 1) * T],
                                                w[:, 2 * D:3 * D], start=m == 0, stop=m == 1)
                last.then_inc(s_v, 1)

            def scores(g, p):
                if not exists(g):
                    return
                pe.wait_ge(s_q, 4 * g + 4)
                for q in range(2):
                    pe.wait_ge(s_km, 2 * g + q + 1)
                    wait(pe, s_sub, 3 * (g - 1) + q + 1)
                    nc.tensor.matmul(bank[S0 + q][:, :], qd[:, p, q, 0:2 * WIN],
                                     km[:, p, q, :, 0:WIN], start=True, stop=True).then_inc(s_s, 1)
                wait(pe, s_sub, 3 * g)
                for q in range(2):
                    last = nc.tensor.matmul(bank[SW][q * WIN:(q + 1) * WIN, 0:HEADS * W1K],
                                            qd[:, p, q, 2 * WIN:2 * TP],
                                            km[:, p, q, :, WIN:T + 1], start=True, stop=True)
                last.then_inc(s_s, 1)

            def project(g, p):
                if not exists(g):
                    return
                pe.wait_ge(s_oe, g + 1)
                pe.wait_ge(s_pe, 3 * g + 2)
                nc.tensor.matmul(bank[TB_][0:TP, 0:GB * D], k.ch("onesh"), k.hi["pb"][:, :].unsqueeze(1).broadcast_to([128, GB, D]),
                                 start=True, stop=False)
                nc.tensor.matmul(bank[TB_][0:TP, 0:GB * D], k.ch("onesh"), k.lo["pb"][:, :].unsqueeze(1).broadcast_to([128, GB, D]),
                                 start=False, stop=True)
                for b in range(GB):
                    q, s = b // 2, b % 2
                    y = bank[TB_][:, b * D:(b + 1) * D]
                    nc.tensor.matmul(y[0:WIN], ot[:, p, q * 128 + s * WIN:][:, 0:WIN], k.c("wp")[:, s * D:(s + 1) * D],
                                     start=False, stop=True, skip_group_check=True)
                    last = nc.tensor.matmul(y[WIN:TP], ot[:, p, 256 + q * 64 + s * 32:][:, 0:32],
                                            k.c("wp")[:, s * D:(s + 1) * D], start=False, stop=True,
                                            skip_group_check=True)
                last.then_inc(s_y, 1)

            def columns(g, p):
                if not exists(g):
                    return
                wait(pe, s_ve, VE * (g - 1))
                n.turn(pe, g, p, k.half(XV))

            def queries_keys(g, p):
                if not exists(g):
                    return
                pe.wait_ge(s_xt, g + 1)
                wait(pe, s_q, 4 * g)
                wait(pe, s_k, g)
                cols = pair_cols(xt[:, p, :])
                for m in range(2):
                    for s in range(2):
                        for i, w in enumerate((hq, lq)):
                            last = nc.tensor.matmul(bank[QK][s * D:(s + 1) * D, m * 2 * T:(m + 1) * 2 * T],
                                                    w[:, m * D:(m + 1) * D], cols[:, :, s, :], start=i == 0, stop=i == 1)
                last.then_inc(s_qk, 1)

            def turn_probs(g, p, part):
                if not exists(g):
                    return
                pe.wait_ge(s_p, 3 * g + part + 1)
                if part == 0:
                    wait(pe, s_pe, 3 * g)
                if part == 1:
                    wait(pe, n.added, g)
                if part == 2:
                    pe.wait_ge(s_pe, 3 * g + 1)
                if part < 2:
                    e = e0[:, p, part, :, :].rearrange("p h w -> p (h w)")
                    at = bank[TA if part == 0 else TB_]
                    for j in range(4):
                        last = nc.tensor.transpose(at[:, j * 128:(j + 1) * 128], e[:, j * 128:(j + 1) * 128], k.c("ident"))
                else:
                    e = e1[:, p, :, :].rearrange("p h w -> p (h w)")
                    for j in range(2):
                        last = nc.tensor.transpose(bank[TA][:, j * 128:(j + 1) * 128], e[:, j * 128:(j + 1) * 128], k.c("ident"))
                last.then_inc(s_pt, 1)

            def gather(g, p):
                if not exists(g):
                    return
                pe.wait_ge(s_ve, VE * g + VE)
                wait(pe, s_oe, g)
                if isinstance(g, int) and SECOND < g <= SECOND + 4:
                    pe.wait_ge(em.s_tok, g - SECOND + 1)
                for q in range(2):
                    pe.wait_ge(s_pe, 3 * g + q + 1)
                    for j in range(4):
                        nc.tensor.matmul(bank[O][32 * j:32 * j + 32, q * 128:(q + 1) * 128], v0[:, p, q, j, :, :].rearrange("p s f -> p (s f)"),
                                         p0[:, p, q, j * 128:(j + 1) * 128], start=True, stop=True)
                pe.wait_ge(s_pe, 3 * g + 3)
                for q in range(2):
                    for j in range(2):
                        last = nc.tensor.matmul(bank[O][64 * j:64 * j + 64, 256 + q * 64:256 + (q + 1) * 64],
                                                v1[:, p, q, 2 * j:2 * j + 2, :, :].rearrange("p j s f -> p (j s f)"),
                                                p1[:, p, j * 128 + q * 64:j * 128 + (q + 1) * 64], start=True, stop=True)
                last.then_inc(s_o, 1)

            def steps(i, p):
                queries_keys(i + 2, p)
                piece = quarter(i - 1)
                if piece:
                    em.turn(pe, piece, bank[O], columns_of_piece(piece))
                turn_probs(i, p, 0)
                values(i + 1, 1 - p)
                turn_probs(i, p, 1)
                turn_probs(i, p, 2)
                gather(i, p)
                scores(i + 2, p)
                columns(i + 3, 1 - p)
                project(i, p)
                piece = quarter(i)
                if piece:
                    em.multiply(pe, piece, bank[O], columns_of_piece(piece))

            em.multiply(pe, 0, bank[S0], columns_of_piece(0))
            em.turn(pe, 0, bank[S0 + 1], columns_of_piece(0))
            em.turn_time(pe, bank[TA])
            pe.wait_ge(em.s_tok, 1)
            pe.wait_ge(em.s_time, 1)
            pe.wait_ge(em.s_halves, 16)
            pe.wait_ge(em.s_spl, em.FIRST_SPLITS)
            pe.wait_ge(s_set, SETS)
            pipeline(pe, steps, -4, SECOND + 5, NG - 6)

        @block.scalar
        def _(act):
            def columns(g, p):
                if not exists(g):
                    return
                act.wait_ge(n.tr, g + 1)
                wait(act, s_qk, g - 1)
                wait(act, s_v, g - 1)
                nc.scalar.activation(xt[:, p, :].rearrange("p (b t) -> p b t", b=GB),
                                     k.turned(XV), ACT.Copy).then_inc(s_xt, 1)

            def place_keys(g, p):
                if not exists(g):
                    return
                act.wait_ge(s_qk, g + 1)
                wait(act, s_km, 2 * (g - 1))
                nc.scalar.activation(ks[:, p, :, 0:T], bank[QK][:, 2 * T:4 * T].rearrange("p (q t) -> p q t", q=2),
                                     ACT.Identity, bias=k.c("kb"), scale=1.0 / WSQ).then_inc(s_k, 1)

            def place_queries(g, p):
                if not exists(g):
                    return
                wait(act, s_s, 3 * (g - 1))
                for s in range(2):
                    src = bank[QK][s * D:(s + 1) * D, 0:2 * T].rearrange("p (q t) -> p q t", q=2)
                    for at, t, w in ((s * WIN, 0, WIN), (2 * WIN + s * 32, WIN, W1Q)):
                        nc.scalar.activation(qd[s * D:(s + 1) * D, p, :, at:at + w], src[:, :, t:t + w], ACT.Identity,
                                             bias=k.c("qb")[s * D:(s + 1) * D], scale=1.0 / WSQ).then_inc(s_q, 1)

            def place_values(g, p):
                if not exists(g):
                    return
                act.wait_ge(s_v, g + 1)
                wait(act, s_o, g - 1)
                v = bank[XV][:, 0:GB * D].rearrange("p (j f) -> p j f", f=16)
                for h in range(2):
                    own = slice(h * HD, h * HD + HD)
                    dst = v0[h * WIN:(h + 1) * WIN, p, :, :, :, :].rearrange("p q j s f -> p (q j s) f")
                    nc.scalar.activation(dst[:, :, own], v[0:WIN, :, own], ACT.Copy).then_inc(s_ve, 1)
                v = bank[XV][:, 0:GB * D].rearrange("p (i r s f) -> p i r s f", r=2, s=2, f=16)
                for h in range(4):
                    own, r = slice(h % 2 * HD, h % 2 * HD + HD), h // 2
                    dst = v1[32 * h:32 * h + W1Q, p, :, :, :, :].rearrange("p q (i r) s f -> p (q i) r s f", i=2)
                    nc.scalar.activation(dst[:, :, r, :, own], v[WIN:T, :, r, :, own], ACT.Copy).then_inc(s_ve, 1)

            def exps(g, p, part):
                if not exists(g):
                    return
                act.wait_ge(s_sub, 3 * g + part + 1)
                e = e0[:, p, part, :, :] if part < 2 else e1[:, p, :, 0:W1K]
                nc.scalar.activation(e, e, ACT.Exp, scale=SCALE).then_inc(s_exp, 1)

            def copy_probs(g, p, part):
                if not exists(g):
                    return
                act.wait_ge(s_pt, 3 * g + part + 1)
                wait(act, s_o, g - 1)
                if part < 2:
                    nc.scalar.activation(p0[:, p, part, :], bank[TA if part == 0 else TB_][:, :], ACT.Copy).then_inc(s_pe, 1)
                else:
                    nc.scalar.activation(p1[:, p, :], bank[TA][:, 0:256], ACT.Copy).then_inc(s_pe, 1)

            def copy_gathered(g, p):
                if not exists(g):
                    return
                act.wait_ge(s_o, g + 1)
                wait(act, s_y, g - 1)
                nc.scalar.activation(ot[:, p, :], bank[O][:, 0:384], ACT.Identity, bias=k.c("vb")).then_inc(s_oe, 1)

            def steps(i, p):
                place_keys(i + 2, p)
                piece = quarter(i - 1)
                if piece:
                    em.copy(act, piece, bank[O], columns_of_piece(piece))
                copy_probs(i, p, 0)
                n.high_by_scalar(act, i + 3, 1 - p)
                copy_probs(i, p, 1)
                exps(i + 1, 1 - p, 0)
                copy_probs(i, p, 2)
                place_queries(i + 2, p)
                exps(i + 1, 1 - p, 1)
                place_values(i + 1, 1 - p)
                exps(i + 1, 1 - p, 2)
                copy_gathered(i, p)
                columns(i + 3, 1 - p)
                piece = quarter(i)
                if piece:
                    em.bias(act, piece, bank[O], columns_of_piece(piece))
                if isinstance(i, int) and NG - 5 <= i < NG:
                    em.large_weights(act, (i - NG + 5) * em.PART)

            em.bias(act, 0, bank[S0], columns_of_piece(0))
            em.copy(act, 0, bank[S0 + 1], columns_of_piece(0))
            em.put(act, 0, columns_of_piece(0), (1,))
            act.wait_ge(em.s_flip, 1)
            nc.scalar.activation(k.time[:, :], bank[TA][0:T, 0:T], ACT.Copy).then_inc(em.s_time, 1)
            act.wait_ge(em.s_spl, em.FIRST_SPLITS)
            act.wait_ge(s_set, SETS)
            pipeline(act, steps, -4, SECOND + 5, NG - 6)

        @block.gpsimd
        def _(pool):
            def mask_keys(g, p):
                if not exists(g):
                    return
                pool.wait_ge(s_k, g + 1)
                wait(pool, s_s, 3 * (g - 1))
                for q in range(2):
                    nc.gpsimd.tensor_tensor(km[:, p, q, :, :], ks[:, p, q, :].unsqueeze(1).broadcast_to([128, HEADS, T + 1]),
                                            k.c("hmask").unsqueeze(2).broadcast_to([128, HEADS, T + 1]),
                                            ALU.mult).then_inc(s_km, 1)

            def probs(g, p, part):
                if not exists(g):
                    return
                pool.wait_ge(s_rs, 3 * g + part + 1)
                e, w = (e0[:, p, part, :, :], WIN) if part < 2 else (e1[:, p, :, 0:W1K], W1K)
                nc.gpsimd.tensor_tensor(e, e, rs[:, p, part, :].unsqueeze(2).broadcast_to([128, HEADS, w]),
                                        ALU.mult).then_inc(s_p, 1)

            def steps(i, p):
                mask_keys(i + 2, p)
                n.low(pool, i + 3, 1 - p)
                n.root(pool, i + 4, p)
                for part in range(3):
                    probs(i + 1, 1 - p, part)

            nc.gpsimd.memset(k.neghalf[:, :], -0.5).then_inc(em.s_half, 1)
            nc.gpsimd.memset(k.eps[:, :], EPS).then_inc(em.s_half, 1)
            pool.wait_ge(em.s_half, 2)
            pool.wait_ge(em.s_first, 16)
            nc.gpsimd.memset(qd[:, :, :, :].rearrange("p a b c -> p (a b c)"), 0.0).then_inc(s_set, 1)
            nc.gpsimd.memset(v0[:, :, :, :, :, :].rearrange("p a b c d e -> p (a b c d e)"), 0.0).then_inc(s_set, 1)
            nc.gpsimd.memset(v1[:, :, :, :, :, :].rearrange("p a b c d e -> p (a b c d e)"), 0.0).then_inc(s_set, 1)
            nc.gpsimd.memset(e1[:, :, :, :].rearrange("p a b c -> p (a b c)"), 0.0).then_inc(s_set, 1)
            for p in range(2):
                nc.gpsimd.tensor_copy(ks[:, p, :, T:T + 1], k.c("kb").unsqueeze(1).broadcast_to([128, 2, 1])).then_inc(s_set, 1)
            pool.wait_ge(s_set, SETS)
            pipeline(pool, steps, -4, 2, NG - 6)

        @block.vector
        def _(dve):
            def maxima(g, p, part):
                if not exists(g):
                    return
                dve.wait_ge(s_s, 3 * g + part + 1)
                src = bank[S0 + part][:, :].rearrange("p (h w) -> p h w", h=HEADS) if part < 2 else \
                    bank[SW][:, 0:HEADS * W1K].rearrange("p (h w) -> p h w", h=HEADS)
                nc.vector.tensor_reduce(mx[:, p, part, :], src, X, ALU.max).then_inc(s_mx, 1)

            def less_max(g, p, part):
                if not exists(g):
                    return
                dve.wait_ge(s_mx, 3 * g + part + 1)
                wait(dve, s_pt, 3 * (g - 2) + part + 1)
                w = WIN if part < 2 else W1K
                src = bank[(S0 + part) if part < 2 else SW][:, 0:HEADS * w].rearrange("p (h w) -> p h w", h=HEADS)
                dst = e0[:, p, part, :, :] if part < 2 else e1[:, p, :, 0:W1K]
                nc.vector.tensor_tensor(dst, src, mx[:, p, part, :].unsqueeze(2).broadcast_to([128, HEADS, w]),
                                        ALU.subtract).then_inc(s_sub, 1)

            def weigh_padding(g, p):
                if not exists(g):
                    return
                dve.wait_ge(s_exp, 3 * g + 3)
                nc.vector.tensor_scalar(e1[:, p, :, W1Q], e1[:, p, :, W1Q], float(PADS), None, ALU.mult).then_inc(s_pad, 1)

            def sums(g, p, part):
                if not exists(g):
                    return
                dve.wait_ge(s_exp, 3 * g + part + 1)
                if part == 2:
                    dve.wait_ge(s_pad, g + 1)
                e = e0[:, p, part, :, :] if part < 2 else e1[:, p, :, 0:W1K]
                nc.vector.tensor_reduce(sm[:, p, part, :], e, X, ALU.add).then_inc(s_sum, 1)

            def inverses(g, p, part):
                if not exists(g):
                    return
                dve.wait_ge(s_sum, 3 * g + part + 1)
                wait(dve, s_p, 3 * (g - 2) + part + 1)
                nc.vector.reciprocal(rs[:, p, part, :], sm[:, p, part, :]).then_inc(s_rs, 1)

            def add(g, p):
                if not exists(g):
                    return
                dve.wait_ge(s_y, g + 1)
                nc.vector.tensor_tensor(k.H[:, group(g), :], k.H[:, group(g), :],
                                        bank[TB_][0:T, 0:GB * D].rearrange("p (b e) -> p b e", b=GB), ALU.add).then_inc(n.added, 1)

            def steps(i, p):
                q = 1 - p
                if isinstance(i, int) and i + 4 == 8 // GB:
                    em.arrived(dve, 0)
                n.scale(dve, i + 3, q)
                maxima(i + 1, q, 0)
                add(i - 1, q)
                less_max(i + 1, q, 0)
                maxima(i + 1, q, 1)
                n.stats(dve, i + 4, p)
                less_max(i + 1, q, 1)
                n.aggregate(dve, i + 4, p, (0,))
                maxima(i + 1, q, 2)
                n.aggregate(dve, i + 4, p, (1,))
                n.centre(dve, i + 4, p)
                less_max(i + 1, q, 2)
                n.aggregate(dve, i + 4, p, (2,))
                sums(i + 1, q, 0)
                inverses(i + 1, q, 0)
                sums(i + 1, q, 1)
                weigh_padding(i + 1, q)
                inverses(i + 1, q, 1)
                sums(i + 1, q, 2)
                inverses(i + 1, q, 2)
                if isinstance(i, int) and NG - 4 <= i:
                    em.low_of_large(dve, (i - NG + 4) * em.PART)
                    if i == NG - 2:
                        em.mix_weights(dve)
                    if i == NG - 1:
                        em.small_weights(dve)
                    if i == NG:
                        em.split_mixed(dve)

            def second_half():
                em.arrived(dve, 1)

            em.first_weights(dve)
            em.first_arrived(dve)
            dve.wait_ge(s_set, SETS)
            pipeline(dve, steps, -4, 2, NG - 6, pause_at=ARRIVED, pause=second_half)


class Gate:

    def __init__(self, k, phase, experts, weight_scale, softmax_first, weights, bias, rev):
        self.k, self.nc, self.E, self.by, self.soft = k, k.nc, experts, weight_scale, softmax_first
        self.w, self.bias, self.rev = weights, k.c(bias), k.c(rev)
        s = [T, GB, experts]
        (self.logits, self.less, self.equal, self.first, self.exps, self.left, self.less2, self.equal2, self.second,
         self.either, self.sign, self.tilt, self.dense) = (k.sb(f"{phase}_{name}", s) for name in (
             "logits", "less_top", "equal", "first", "exps", "left", "less_top2", "equal2", "second", "either", "sign",
             "tilt", "dense"))
        (self.top, self.rank, self.top2, self.rank2, self.gap, self.half_tanh, self.total, self.inverse) = (
            k.sb(f"{phase}_{name}", [T, GB]) for name in (
                "top", "rank", "top2", "rank2", "gap", "half_tanh", "total", "inverse"))
        self.parts = k.sb(f"{phase}_parts", [T, GB, 128], F16)
        self.wt = k.sb(f"{phase}_wt", [128, 2, N], F16)
        (self.s_log, self.s_dve, self.s_act, self.s_pool, self.s_tr, self.s_wt, self.s_zero) = (
            k.sem(f"{phase}_g_" + n) for n in ("logits", "chain", "acted", "weighed", "turned", "placed", "zeroed"))
        self.OPS = 15 if softmax_first else 12
        self.ACTS = 2 if softmax_first else 1
        self.POOLS = 6

    def over(self, ap):
        return ap[:, :].unsqueeze(2).broadcast_to([T, GB, self.E])

    def multiply(self, pe, g, xt, out):
        for b in range(GB):
            for m, w in enumerate(self.w):
                last = self.nc.tensor.matmul(out[0:T, b * self.E:(b + 1) * self.E], xt[:, b * T:(b + 1) * T],
                                             w[:, 0:self.E], start=m == 0, stop=m == 1)
        last.then_inc(self.s_log, 1)

    def choose(self, dve, g, out, ops):
        v, E, at = self.nc.vector, self.E, self.OPS * g
        every = self.bias[0:T].unsqueeze(1).broadcast_to([T, GB, E])
        rev = self.rev[0:T].unsqueeze(1).broadcast_to([T, GB, E])
        logits = out[0:T, 0:GB * E].rearrange("p (b e) -> p b e", b=GB)
        done = self.s_dve
        for o in ops:
            if o == 0:
                dve.wait_ge(self.s_log, g + 1)
                v.scalar_tensor_tensor(self.logits[:, :, :], logits, 1.0 / self.by, every, ALU.mult,
                                       ALU.add).then_inc(done, 1)
            if o == 1:
                dve.wait_ge(done, at + 1)
                v.tensor_reduce(self.top[:, :], self.logits[:, :, :], X, ALU.max).then_inc(done, 1)
            if o == 2:
                dve.wait_ge(done, at + 2)
                v.tensor_tensor(self.less[:, :, :], self.logits[:, :, :], self.over(self.top),
                                ALU.subtract).then_inc(done, 1)
            if o == 3:
                dve.wait_ge(done, at + 3)
                v.scalar_tensor_tensor(self.equal[:, :, :], self.less[:, :, :], 0.0, rev, ALU.is_equal,
                                       ALU.mult).then_inc(done, 1)
            if o == 4:
                dve.wait_ge(done, at + 4)
                v.tensor_reduce(self.rank[:, :], self.equal[:, :, :], X, ALU.max).then_inc(done, 1)
            if o == 5:
                dve.wait_ge(done, at + 5)
                wait(dve, self.s_pool, self.POOLS * g)
                v.tensor_tensor(self.first[:, :, :], self.equal[:, :, :], self.over(self.rank),
                                ALU.is_equal).then_inc(done, 1)
            if o < 6:
                continue
            if self.soft:
                if o == 6:
                    dve.wait_ge(self.s_act, self.ACTS * g + 1)
                    v.tensor_reduce(self.total[:, :], self.exps[:, :, :], X, ALU.add).then_inc(done, 1)
                if o == 7:
                    dve.wait_ge(done, at + 6)
                    v.scalar_tensor_tensor(self.left[:, :, :], self.first[:, :, :], -3e38, self.exps[:, :, :],
                                           ALU.mult, ALU.add).then_inc(done, 1)
                if o == 8:
                    dve.wait_ge(done, at + 7)
                    v.reciprocal(self.inverse[:, :], self.total[:, :]).then_inc(done, 1)
                if o == 9:
                    dve.wait_ge(done, at + 8)
                    v.tensor_reduce(self.top2[:, :], self.left[:, :, :], X, ALU.max).then_inc(done, 1)
                if o == 10:
                    dve.wait_ge(done, at + 10)
                    v.tensor_tensor(self.less2[:, :, :], self.left[:, :, :], self.over(self.top2),
                                    ALU.subtract).then_inc(done, 1)
                if o == 11:
                    dve.wait_ge(done, at + 10)
                    v.scalar_tensor_tensor(self.gap[:, :], self.top2[:, :], 1.0, self.inverse[:, :], ALU.subtract,
                                           ALU.mult).then_inc(done, 1)
                if o == 12:
                    dve.wait_ge(done, at + 11)
                    v.scalar_tensor_tensor(self.equal2[:, :, :], self.less2[:, :, :], 0.0, rev, ALU.is_equal,
                                           ALU.mult).then_inc(done, 1)
                if o == 13:
                    dve.wait_ge(done, at + 13)
                    v.tensor_reduce(self.rank2[:, :], self.equal2[:, :, :], X, ALU.max).then_inc(done, 1)
                if o == 14:
                    dve.wait_ge(done, at + 14)
                    v.tensor_tensor(self.second[:, :, :], self.equal2[:, :, :], self.over(self.rank2),
                                    ALU.is_equal).then_inc(done, 1)
            else:
                dve.wait_ge(done, at + o)
                if o == 6:
                    v.scalar_tensor_tensor(self.left[:, :, :], self.first[:, :, :], -3e38, self.less[:, :, :],
                                           ALU.mult, ALU.add).then_inc(done, 1)
                if o == 7:
                    v.tensor_reduce(self.top2[:, :], self.left[:, :, :], X, ALU.max).then_inc(done, 1)
                if o == 8:
                    v.tensor_tensor(self.less2[:, :, :], self.left[:, :, :], self.over(self.top2),
                                    ALU.subtract).then_inc(done, 1)
                if o == 9:
                    v.scalar_tensor_tensor(self.equal2[:, :, :], self.less2[:, :, :], 0.0, rev, ALU.is_equal,
                                           ALU.mult).then_inc(done, 1)
                if o == 10:
                    v.tensor_reduce(self.rank2[:, :], self.equal2[:, :, :], X, ALU.max).then_inc(done, 1)
                if o == 11:
                    v.tensor_tensor(self.second[:, :, :], self.equal2[:, :, :], self.over(self.rank2),
                                    ALU.is_equal).then_inc(done, 1)

    def exponentiate(self, act, g):
        act.wait_ge(self.s_dve, self.OPS * g + 3)
        self.nc.scalar.activation(self.exps[:, :, :], self.less[:, :, :], ACT.Exp).then_inc(self.s_act, 1)

    def tanh(self, act, g):
        act.wait_ge(self.s_dve, self.OPS * g + (12 if self.soft else 8))
        self.nc.scalar.activation(self.half_tanh[:, :], (self.gap if self.soft else self.top2)[:, :], ACT.Tanh,
                                  scale=-0.5).then_inc(self.s_act, 1)

    def weigh(self, pool, g):
        v, E, at = self.nc.gpsimd, self.E, self.POOLS * g
        pool.wait_ge(self.s_act, self.ACTS * g + self.ACTS)
        pool.wait_ge(self.s_dve, self.OPS * g + self.OPS)
        v.tensor_tensor(self.either[:, :, :], self.first[:, :, :], self.second[:, :, :], ALU.add).then_inc(self.s_pool, 1)
        v.tensor_tensor(self.sign[:, :, :], self.first[:, :, :], self.second[:, :, :], ALU.subtract).then_inc(self.s_pool, 1)
        pool.wait_ge(self.s_pool, at + 2)
        v.tensor_tensor(self.tilt[:, :, :], self.sign[:, :, :], self.over(self.half_tanh), ALU.mult).then_inc(self.s_pool, 1)
        pool.wait_ge(self.s_pool, at + 3)
        v.tensor_tensor(self.dense[:, :, :], self.either[:, :, :], self.tilt[:, :, :], ALU.add).then_inc(self.s_pool, 1)
        wait(pool, self.s_tr, g)
        v.tensor_tensor(self.parts[:, :, 0:E], self.either[:, :, :], self.tilt[:, :, :], ALU.add).then_inc(self.s_pool, 1)
        pool.wait_ge(self.s_pool, at + 5)
        v.tensor_tensor(self.parts[:, :, E:2 * E], self.dense[:, :, :], self.parts[:, :, 0:E], ALU.subtract).then_inc(self.s_pool, 1)

    def turn(self, pe, g, out):
        pe.wait_ge(self.s_pool, self.POOLS * g + self.POOLS)
        for b in range(GB):
            last = self.nc.tensor.transpose(out[:, b * TE:b * TE + T], self.parts[:, b, :], self.k.ch("identh")[0:T, 0:T])
        last.then_inc(self.s_tr, 1)

    def place(self, act, g, p, turned):
        act.wait_ge(self.s_tr, g + 1)
        self.nc.scalar.activation(self.wt[:, p, :].rearrange("p (b t) -> p b t", b=GB), turned, ACT.Copy).then_inc(self.s_wt, 1)


def columns_of(ap):
    return ap.rearrange("p (b t) -> p b t", b=GB)


def mix_experts(k):
    nc = k.nc
    with ExitStack() as ctx:
        k.ctx = ctx
        n = k.norms["e"]
        gate = Gate(k, "e", E0, WS0, False, (k.hi["g0w"], k.lo["g0w"]), "g0b", "rev0")
        AHEAD, RING = 3, 4
        xt = k.sb("e_xt", [128, 2, N], F16)
        hid = k.sb("e_hidden", [128, RING, N])
        wh = k.sb("e_weighed", [128, RING, N])
        yt = k.sb("e_yt", [128, 2, N // 2])
        HB, WB, YB, XB, TB_ = 0, 2, 4, 6, 7
        bank = k.bank
        s_xt, s_h, s_g, s_wb, s_z, s_y, s_y2, s_yt, s_ytr = (k.sem("e_" + x) for x in (
            "x_columns", "hidden", "gelus", "weights_spread", "weighed", "chunkn.addeded", "outputs", "outputs_copied",
            "outputs_turned"))
        block = ctx.enter_context(nc.Block())
        w2 = k.c("w2").rearrange("p (c e) -> p c e", c=CH)
        b1 = k.c("b1")
        sel = k.ch("sel0").rearrange("p (e m) -> p e m", e=E0)

        @block.tensor
        def _(pe):
            def first(g, p, c):
                if not exists(g):
                    return
                if c == 0:
                    pe.wait_ge(s_xt, g + 1)
                wait(pe, s_g, CH * g + c - 1)
                for m, w in enumerate((k.hi["w1"], k.lo["w1"])):
                    last = nc.tensor.matmul(bank[HB + c % 2][:, 0:N], w[:, c * 128:(c + 1) * 128], xt[:, p, :],
                                            start=m == 0, stop=m == 1)
                last.then_inc(s_h, 1)

            def spread(g, p, e):
                if not exists(g):
                    return
                if e == 0:
                    pe.wait_ge(gate.s_wt, g + 1)
                wait(pe, s_z, CH * g + 2 * e - 2)
                nc.tensor.matmul(bank[WB + e % 2][:, 0:N], sel[:, e, :], gate.wt[:, p, :], start=True, stop=True).then_inc(s_wb, 1)

            def second(g, p, c):
                if not exists(g):
                    return
                pe.wait_ge(s_z, CH * g + c + 1)
                if c == 0:
                    wait(pe, s_yt, g - 1)
                for s in range(2):
                    last = nc.tensor.matmul(bank[YB + p][s * D:(s + 1) * D, 0:N // 2], w2[:, c, :],
                                            wh[:, c % RING, s * (N // 2):(s + 1) * (N // 2)], start=c == 0, stop=False)
                last.then_inc(s_y, 1)

            def biases(g, p):
                if not exists(g):
                    return
                for m, w in enumerate((k.hi["b2"], k.lo["b2"])):
                    for s in range(2):
                        last = nc.tensor.matmul(bank[YB + p][s * D:(s + 1) * D, 0:N // 2], w[:, :],
                                                gate.wt[:, p, s * (N // 2):(s + 1) * (N // 2)], start=False, stop=m == 1)
                last.then_inc(s_y2, 1)

            def turn_outputs(g, p):
                if not exists(g):
                    return
                pe.wait_ge(s_yt, g + 1)
                for b in range(2):
                    last = nc.tensor.transpose(bank[TB_][0:T, b * 128:(b + 1) * 128], yt[:, p, b * T:(b + 1) * T], k.c("ident"))
                last.then_inc(s_ytr, 1)

            def steps(i, p):
                q = 1 - p
                for c in range(CH):
                    ahead = c + AHEAD
                    first(i if ahead < CH else i + 1, p if ahead < CH else q, ahead % CH)
                    if c == 10 and exists(i + 2):
                        wait(pe, gate.s_dve, gate.OPS * (i + 1) + 1)
                        n.turn(pe, i + 2, p, k.half(XB))
                    if c == 14 and exists(i + 2):
                        pe.wait_ge(s_xt, i + 3)
                        gate.multiply(pe, i + 2, xt[:, p, :], bank[XB])
                    if c == 3:
                        turn_outputs(i - 1, q)
                    if c == 13 and exists(i + 1):
                        wait(pe, n.added, i)
                        gate.turn(pe, i + 1, k.half(TB_))
                    if c % 2 == 0:
                        e = c // 2 + 1
                        spread(i if e < E0 else i + 1, p if e < E0 else q, e % E0)
                    second(i, p, c)
                biases(i, p)

            pe.wait_ge(gate.s_zero, 1)
            pipeline(pe, steps, -2, 2, NG - 6)

        @block.scalar
        def _(act):
            def gelu(g, p, c):
                if not exists(g):
                    return
                act.wait_ge(s_h, CH * g + c + 1)
                wait(act, s_z, CH * g + c - RING + 1)
                nc.scalar.activation(hid[:, c % RING, :], bank[HB + c % 2][:, 0:N], ACT.Gelu, bias=b1[:, c:c + 1],
                                     scale=1.0 / WS0).then_inc(s_g, 1)

            def steps(i, p):
                q = 1 - p
                for c in range(CH):
                    ahead = c + AHEAD
                    gelu(i if ahead < CH else i + 1, p if ahead < CH else q, ahead % CH)
                    if c == 1 and exists(i - 1):
                        act.wait_ge(s_y2, i)
                        wait(act, s_ytr, i - 2)
                        nc.scalar.activation(yt[:, q, :], bank[YB + q][:, 0:N // 2], ACT.Copy).then_inc(s_yt, 1)
                    if c == 8 and exists(i + 1):
                        gate.tanh(act, i + 1)
                    if c == 12 and exists(i + 2):
                        act.wait_ge(n.tr, i + 3)
                        wait(act, s_h, CH * (i + 1))
                        wait(act, gate.s_log, i + 1)
                        nc.scalar.activation(columns_of(xt[:, p, :]), k.turned(XB), ACT.Copy).then_inc(s_xt, 1)
                    if c == 13 and exists(i + 1):
                        wait(act, s_y2, i)
                        gate.place(act, i + 1, q, k.turned(TB_))

            pipeline(act, steps, -2, 4, NG - 4)

        @block.gpsimd
        def _(pool):
            def steps(i, p):
                n.low(pool, i + 2, p)
                if exists(i + 1):
                    gate.weigh(pool, i + 1)
                n.root(pool, i + 3, 1 - p)

            nc.gpsimd.memset(gate.parts[:, :, :].rearrange("p b c -> p (b c)"), 0.0).then_inc(gate.s_zero, 1)
            pool.wait_ge(gate.s_zero, 1)
            pipeline(pool, steps, -3, 2, NG - 6)

        @block.vector
        def _(dve):
            def weigh(g, c):
                if not exists(g):
                    return
                dve.wait_ge(s_g, CH * g + c + 1)
                if c % 2 == 0:
                    dve.wait_ge(s_wb, E0 * g + c // 2 + 1)
                wait(dve, s_y, CH * g + c - RING + 1)
                nc.vector.tensor_tensor(wh[:, c % RING, :], hid[:, c % RING, :], bank[WB + c // 2 % 2][:, 0:N],
                                        ALU.mult).then_inc(s_z, 1)

            CHOOSE = {1: (0,), 2: (1,), 3: (2,), 4: (3,), 5: (4,), 6: (5,), 7: (6,), 8: (7, 8), 9: (9,), 10: (10,),
                      11: (11,)}

            def steps(i, p):
                q = 1 - p
                for c in range(CH):
                    weigh(i, c)
                    if exists(i + 1):
                        gate.choose(dve, i + 1, bank[XB], CHOOSE.get(c, ()))
                    if c == 0:
                        n.scale(dve, i + 2, p)
                    if c == 1:
                        n.high(dve, i + 2, p)
                    if c == 7 and exists(i - 1):
                        dve.wait_ge(s_ytr, i)
                        out = bank[TB_][0:T, 0:GB * D].rearrange("p (b s e) -> p s b e", b=2, s=2)
                        h = k.H[:, group(i - 1), :].rearrange("p (s b) e -> p s b e", s=2)
                        nc.vector.tensor_tensor(h, h, out, ALU.add).then_inc(n.added, 1)
                    if c == 11:
                        n.stats(dve, i + 3, q, (0, 1))
                    if c == 12:
                        n.stats(dve, i + 3, q, (2, 3))
                    if c == 13:
                        n.aggregate(dve, i + 3, q, (0,))
                    if c == 14:
                        n.aggregate(dve, i + 3, q, (1,))
                        n.centre(dve, i + 3, q)
                        n.aggregate(dve, i + 3, q, (2,))

            pipeline(dve, steps, -3, 2, NG - 6)


def mix_time(k):
    nc = k.nc
    with ExitStack() as ctx:
        k.ctx = ctx
        n = k.norms["t"]
        xt = k.sb("t_xt", [128, 2, GB, TE], F16)
        raw = k.sb("t_exp_raw", [T, 2, GB, D])
        ek = k.sb("t_exp_k", [T, 2, GB, D])
        er = k.sb("t_exp_r", [T, 2, GB, D])
        v = k.sb("t_v", [T, 2, GB, D])
        kv = k.sb("t_kv", [T, 2, GB, D])
        den = k.sb("t_den", [T, GB, D])
        inv = k.sb("t_inv", [T, GB, D])
        rw = k.sb("t_rw", [T, 2, GB, D])
        rt = k.sb("t_rwt", [128, 2, 2 * T])
        KVR, SUM, XB, RT, OUT = 0, 2, 4, 5, 6
        bank = k.bank
        (s_set, s_xt, s_kvr, s_raw, s_clip, s_er, s_v, s_kv, s_sum, s_den, s_inv, s_rw, s_rtr, s_rt, s_out) = (
            k.sem("t_" + x) for x in ("zeroed", "x_columns", "kvr", "exps_raw", "exps_clipped", "exp_r", "v_copied", "kv", "sums",
                                      "denominators", "inverses", "rw", "rw_turned", "rw_copied", "outputs"))
        block = ctx.enter_context(nc.Block())

        def kvr(q, which):
            return bank[KVR + q][0:T, 0:6 * D].rearrange("p (b n e) -> p b n e", b=2, n=3)[:, :, which, :]

        @block.tensor
        def _(pe):
            def sums(g, p):
                if not exists(g):
                    return
                pe.wait_ge(s_kv, g + 1)
                wait(pe, s_rw, g - 1)
                nc.tensor.matmul(bank[SUM + p][0:T, 0:GB * D], k.time[:, :], kv[:, p, :, :].rearrange("p b e -> p (b e)"),
                                 start=True, stop=True)
                nc.tensor.matmul(bank[SUM + p][0:T, GB * D:2 * GB * D], k.c("tri")[0:T, :],
                                 ek[:, p, :, :].rearrange("p b e -> p (b e)"), start=True, stop=True).then_inc(s_sum, 1)

            def multiply(g, p):
                if not exists(g):
                    return
                pe.wait_ge(s_xt, g + 1)
                for b in range(GB):
                    if b % 2 == 0:
                        wait(pe, s_raw, 2 * g - 2 + b // 2 + 1)
                        wait(pe, s_er, 2 * g - 2 + b // 2 + 1)
                        wait(pe, s_v, 2 * g - 2 + b // 2 + 1)
                    terms = [(1, k.hi["kvra"]), (1, k.lo["kvra"]), (0, k.hi["kvrb"]), (0, k.lo["kvrb"])]
                    for m, (at, w) in enumerate(terms):
                        last = nc.tensor.matmul(bank[KVR + b // 2][0:T, b % 2 * 3 * D:(b % 2 + 1) * 3 * D],
                                                xt[:, p, b, at:at + T], w[:, :], start=m == 0, stop=m == 3)
                    if b % 2 == 1:
                        last.then_inc(s_kvr, 1)

            def turn_quotients(g, p):
                if not exists(g):
                    return
                pe.wait_ge(s_rw, g + 1)
                wait(pe, s_rt, g)
                for s in range(2):
                    last = nc.tensor.transpose(bank[RT][:, s * T:(s + 1) * T],
                                               rw[:, p, 2 * s:2 * s + 2, :].rearrange("p b e -> p (b e)"),
                                               k.c("ident")[0:T, 0:T])
                last.then_inc(s_rtr, 1)

            def output(g, p):
                if not exists(g):
                    return
                pe.wait_ge(s_rt, g + 1)
                wait(pe, n.added, g)
                for s in range(2):
                    last = nc.tensor.matmul(bank[OUT][0:T, s * 128:(s + 1) * 128], rt[:, p, s * T:(s + 1) * T],
                                            k.c("wo"), start=True, stop=True)
                last.then_inc(s_out, 1)

            def steps(i, p):
                q = 1 - p
                multiply(i + 2, p)
                sums(i + 1, q)
                turn_quotients(i, p)
                output(i, p)
                if exists(i + 3):
                    wait(pe, s_xt, i + 3)
                    n.turn(pe, i + 3, q, k.half(XB))

            pipeline(pe, steps, -4, 2, NG - 6)

        @block.scalar
        def _(act):
            def steps(i, p):
                q = 1 - p
                if exists(i):
                    act.wait_ge(s_rtr, i + 1)
                    wait(act, s_out, i - 1)
                    nc.scalar.activation(rt[:, p, :], bank[RT][:, 0:2 * T], ACT.Copy).then_inc(s_rt, 1)
                g = i + 2
                if exists(g):
                    wait(act, s_den, g - 1)
                    wait(act, s_kv, g - 1)
                    wait(act, s_clip, g - 1)
                    for b in range(2):
                        act.wait_ge(s_kvr, 2 * g + b + 1)
                        nc.scalar.activation(raw[:, p, 2 * b:2 * b + 2, :], kvr(b, 0), ACT.Exp, scale=1.0 / WS1).then_inc(s_raw, 1)
                        nc.scalar.activation(er[:, p, 2 * b:2 * b + 2, :], kvr(b, 2), ACT.Exp, scale=-1.0 / WS1).then_inc(s_er, 1)
                        nc.scalar.activation(v[:, p, 2 * b:2 * b + 2, :], kvr(b, 1), ACT.Copy, scale=1.0 / WS1).then_inc(s_v, 1)
                if exists(i + 3):
                    act.wait_ge(n.tr, i + 4)
                    wait(act, s_kvr, 2 * (i + 2))
                    nc.scalar.activation(xt[:, q, :, 1:TE], k.turned(XB), ACT.Copy).then_inc(s_xt, 1)
                n.high_by_scalar(act, i + 4, p)

            act.wait_ge(s_set, 1)
            pipeline(act, steps, -4, 2, NG - 6)

        @block.gpsimd
        def _(pool):
            def steps(i, p):
                n.root(pool, i + 4, p)
                if exists(i + 2):
                    g = i + 2
                    pool.wait_ge(s_clip, g + 1)
                    pool.wait_ge(s_v, 2 * g + 2)
                    wait(pool, s_sum, g - 1)
                    nc.gpsimd.tensor_tensor(kv[:, p, :, :], ek[:, p, :, :], v[:, p, :, :], ALU.mult).then_inc(s_kv, 1)
                n.low(pool, i + 4, p)

            nc.gpsimd.memset(xt[:, :, :, :].rearrange("p a b c -> p (a b c)"), 0.0).then_inc(s_set, 1)
            pool.wait_ge(s_set, 1)
            pipeline(pool, steps, -4, 2, NG - 6)

        @block.vector
        def _(dve):
            def clip(g, p):
                if not exists(g):
                    return
                dve.wait_ge(s_raw, 2 * g + 2)
                wait(dve, s_sum, g - 1)
                nc.vector.tensor_scalar(ek[:, p, :, :], raw[:, p, :, :], math.exp(30.0), math.exp(-60.0),
                                        ALU.min, ALU.max).then_inc(s_clip, 1)

            def steps(i, p):
                q = 1 - p
                sums = bank[SUM + q][0:T, :].rearrange("p (w b e) -> p w b e", w=2, b=GB)
                n.stats(dve, i + 4, p)
                n.aggregate(dve, i + 4, p, (0,))
                n.centre(dve, i + 4, p)
                n.aggregate(dve, i + 4, p, (1,))
                if exists(i + 1):
                    g = i + 1
                    dve.wait_ge(s_sum, g + 1)
                    dve.wait_ge(s_er, 2 * g + 2)
                    wait(dve, s_inv, g)
                    nc.vector.scalar_tensor_tensor(den[:, :, :], er[:, q, :, :], 1.0, sums[:, 1], ALU.add, ALU.mult).then_inc(s_den, 1)
                n.aggregate(dve, i + 4, p, (2,))
                if exists(i + 1):
                    g = i + 1
                    dve.wait_ge(s_den, g + 1)
                    wait(dve, s_rw, g)
                    nc.vector.reciprocal(inv[:, :, :], den[:, :, :]).then_inc(s_inv, 1)
                clip(i + 2, p)
                n.scale(dve, i + 4, p)
                if exists(i + 1):
                    g = i + 1
                    dve.wait_ge(s_inv, g + 1)
                    wait(dve, s_rtr, g - 1)
                    nc.vector.tensor_tensor(rw[:, q, :, :], inv[:, :, :], sums[:, 0], ALU.mult).then_inc(s_rw, 1)
                if exists(i):
                    dve.wait_ge(s_out, i + 1)
                    nc.vector.tensor_tensor(k.H[:, group(i), :], k.H[:, group(i), :],
                                            bank[OUT][0:T, 0:GB * D].rearrange("p (b e) -> p b e", b=GB),
                                            ALU.add).then_inc(n.added, 1)

            pipeline(dve, steps, -4, 2, NG - 6)


def mix_mlps(k, a_out):
    nc = k.nc
    with ExitStack() as ctx:
        k.ctx = ctx
        n = k.norms["m"]
        gate = Gate(k, "m", E1, WSF, True, (k.hi["g1w"], k.lo["g1w"]), "g1b", "rev1")
        xt = k.sb("m_xt", [128, 2, N], F16)
        h1 = k.sb("m_h1", [128, 5, N])
        h2 = k.sb("m_h2", [128, 2, 3, N])
        hw = k.sb("m_h2w", [128, 2, 2, N])
        yt = k.sb("m_yt", [128, 2, N // 2])
        H1B, H2B, WB, YB, XB, TB_ = 0, 2, 4, 5, 6, 7
        bank = k.bank
        (s_xt, s_h1, s_a1, s_d1, s_h2, s_a2, s_wb, s_z, s_y, s_yt, s_ytr, s_store) = (k.sem("m_" + x) for x in (
            "x_columns", "first_layers", "firsts_by_scalar", "firsts_by_vector", "second_layers", "seconds", "weights_spread",
            "weighed", "outputs", "outputs_copied", "outputs_turned", "stored"))
        block = ctx.enter_context(nc.Block())
        ORDER = (1, 2, 3, 4, 0)
        fb1, fb2 = k.c("fb1"), k.c("fb2")
        w2e = k.c("fw2e").rearrange("p (e m) -> p e m", e=E1)
        w3 = k.c("fw3").rearrange("p (i m) -> p i m", i=3)
        sel = k.ch("sel1").rearrange("p (j m) -> p j m", j=2)

        @block.sync
        def _(sp):
            def steps(i, p):
                sp.wait_ge(n.added, i + 1)
                sp.dma_start(a_out[:, group(i), :], k.H[:, group(i), :]).then_inc(s_store, 16)

            with sp.Fori(0, NG) as i:
                steps(i, 0)
            sp.wait_ge(s_store, 16 * NG)

        @block.tensor
        def _(pe):
            def first(g, p, j):
                if not exists(g):
                    return
                c = ORDER[j]
                if j % 2 == 0:
                    wait(pe, s_a1, 3 * g + j // 2)
                else:
                    wait(pe, s_d1, 2 * g + j // 2)
                for m, w in enumerate((k.hi["fw1"], k.lo["fw1"])):
                    last = nc.tensor.matmul(bank[H1B + j % 2][:, 0:N], w[:, c * 128:(c + 1) * 128], xt[:, p, :],
                                            start=m == 0, stop=m == 1)
                last.then_inc(s_h1, 1)

            def second(g, p, j):
                if not exists(g):
                    return
                pe.wait_ge(s_a1, 3 * g + j + 1)
                if j < 2:
                    pe.wait_ge(s_d1, 2 * g + j + 1)
                wait(pe, s_a2, 3 * g + j - 1 if j else 3 * g)
                at = bank[H2B + j % 2]
                if j < 2:
                    for s in range(2):
                        last = nc.tensor.matmul(at[s * D:(s + 1) * D, 0:N], w2e[:, 2 * j + s, :], h1[:, 1 + 2 * j + s, :],
                                                start=True, stop=True)
                else:
                    last = nc.tensor.matmul(at[:, 0:N], k.c("fw2s"), h1[:, 0, :], start=True, stop=True)
                last.then_inc(s_h2, 1)

            def spread(g, p, j):
                if not exists(g):
                    return
                if j == 0:
                    pe.wait_ge(gate.s_wt, g + 1)
                wait(pe, s_z, 2 * g + j)
                nc.tensor.matmul(bank[WB][:, 0:N], sel[:, j, :], gate.wt[:, p, :], start=True, stop=True).then_inc(s_wb, 1)

            def third(g, p):
                if not exists(g):
                    return
                pe.wait_ge(s_z, 2 * g + 2)
                pe.wait_ge(s_a2, 3 * g + 3)
                wait(pe, s_yt, g)
                for s in range(2):
                    cols = slice(s * (N // 2), (s + 1) * (N // 2))
                    out = bank[YB][s * D:(s + 1) * D, 0:N // 2]
                    nc.tensor.matmul(out, w3[:, 0, :], h2[:, p, 0, cols], start=True, stop=False)
                for s in range(2):
                    cols = slice(s * (N // 2), (s + 1) * (N // 2))
                    out = bank[YB][s * D:(s + 1) * D, 0:N // 2]
                    for m, w in enumerate((k.hi["fb3"], k.lo["fb3"])):
                        nc.tensor.matmul(out, w[:, :], gate.wt[:, p, cols], start=False, stop=False)
                for j in range(2):
                    for s in range(2):
                        cols = slice(s * (N // 2), (s + 1) * (N // 2))
                        last = nc.tensor.matmul(bank[YB][s * D:(s + 1) * D, 0:N // 2], w3[:, 1 + j, :], hw[:, p, j, cols],
                                                start=False, stop=j == 1)
                last.then_inc(s_y, 1)

            def turn_outputs(g, p):
                if not exists(g):
                    return
                pe.wait_ge(s_yt, g + 1)
                wait(pe, n.added, g)
                for b in range(2):
                    last = nc.tensor.transpose(bank[TB_][0:T, b * 128:(b + 1) * 128], yt[:, p, b * T:(b + 1) * T], k.c("ident"))
                last.then_inc(s_ytr, 1)

            def steps(i, p):
                q = 1 - p
                first(i, p, 0)
                first(i, p, 1)
                third(i - 2, p)
                first(i, p, 2)
                second(i, p, 0)
                first(i, p, 3)
                if exists(i - 1):
                    wait(pe, n.added, i - 2)
                    gate.turn(pe, i - 1, k.half(TB_))
                if exists(i + 1):
                    wait(pe, gate.s_dve, gate.OPS * i + 1)
                    n.turn(pe, i + 1, q, k.half(XB))
                first(i, p, 4)
                spread(i - 1, q, 0)
                second(i, p, 1)
                spread(i - 1, q, 1)
                turn_outputs(i - 2, p)
                second(i, p, 2)
                if exists(i + 1):
                    pe.wait_ge(s_xt, i + 2)
                    gate.multiply(pe, i + 1, xt[:, q, :], bank[XB])

            pe.wait_ge(gate.s_zero, 1)
            pipeline(pe, steps, -1, 4, NG - 4, NG + 1)

        @block.scalar
        def _(act):
            def first(g, p, j):
                if not exists(g):
                    return
                c = ORDER[j]
                act.wait_ge(s_h1, 5 * g + j + 1)
                wait(act, s_h2, 3 * (g - 1) + j // 2 + 1)
                nc.scalar.activation(h1[:, c, :], bank[H1B][:, 0:N], ACT.Relu, bias=fb1[:, c:c + 1], scale=1.0 / WSF).then_inc(s_a1, 1)

            def second(g, p, j):
                if not exists(g):
                    return
                c = (j + 1) % 3
                act.wait_ge(s_h2, 3 * g + j + 1)
                wait(act, s_y, g - 1)
                nc.scalar.activation(h2[:, p, c, :], bank[H2B + j % 2][:, 0:N], ACT.Relu, bias=fb2[:, c:c + 1]).then_inc(s_a2, 1)

            def steps(i, p):
                q = 1 - p
                first(i, p, 0)
                if exists(i):
                    gate.exponentiate(act, i)
                if exists(i - 2):
                    act.wait_ge(s_y, i - 1)
                    wait(act, s_ytr, i - 3)
                    nc.scalar.activation(yt[:, p, :], bank[YB][:, 0:N // 2], ACT.Identity, bias=k.c("sb3")).then_inc(s_yt, 1)
                first(i, p, 2)
                second(i, p, 0)
                if exists(i - 1):
                    wait(act, s_y, i - 2)
                    gate.place(act, i - 1, q, k.turned(TB_))
                if exists(i + 1):
                    act.wait_ge(n.tr, i + 2)
                    wait(act, s_h1, 5 * i)
                    wait(act, gate.s_log, i)
                    nc.scalar.activation(columns_of(xt[:, q, :]), k.turned(XB), ACT.Copy).then_inc(s_xt, 1)
                first(i, p, 4)
                second(i, p, 1)
                second(i, p, 2)
                if exists(i):
                    gate.tanh(act, i)
                n.high_by_scalar(act, i + 2, p)

            pipeline(act, steps, -2, 4, NG - 4, NG + 1)

        @block.gpsimd
        def _(pool):
            def steps(i, p):
                n.root(pool, i + 2, p)
                if exists(i):
                    gate.weigh(pool, i)
                n.low(pool, i + 2, p)

            nc.gpsimd.memset(gate.parts[:, :, :].rearrange("p b c -> p (b c)"), 0.0).then_inc(gate.s_zero, 1)
            pool.wait_ge(gate.s_zero, 1)
            pipeline(pool, steps, -2, 4, NG - 4, NG + 1)

        @block.vector
        def _(dve):
            def first(g, p, j):
                if not exists(g):
                    return
                c = ORDER[j]
                dve.wait_ge(s_h1, 5 * g + j + 1)
                wait(dve, s_h2, 3 * (g - 1) + j // 2 + 1)
                nc.vector.tensor_scalar(h1[:, c, :], bank[H1B + 1][:, 0:N], fb1[:, c:c + 1], 0.0, ALU.add, ALU.max).then_inc(s_d1, 1)

            def weigh(g, p, j):
                if not exists(g):
                    return
                dve.wait_ge(s_wb, 2 * g + j + 1)
                dve.wait_ge(s_a2, 3 * g + j + 1)
                wait(dve, s_y, g - 1)
                nc.vector.tensor_tensor(hw[:, p, j, :], h2[:, p, 1 + j, :], bank[WB][:, 0:N], ALU.mult).then_inc(s_z, 1)

            def choose(g, *ops):
                if exists(g):
                    gate.choose(dve, g, bank[XB], ops)

            def steps(i, p):
                q = 1 - p
                choose(i, 0)
                first(i, p, 1)
                choose(i, 1)
                n.stats(dve, i + 2, p, (0, 1))
                choose(i, 2)
                n.stats(dve, i + 2, p, (2,))
                choose(i, 3)
                n.stats(dve, i + 2, p, (3,))
                choose(i, 4)
                n.aggregate(dve, i + 2, p, (0,))
                choose(i, 5, 6)
                first(i, p, 3)
                choose(i, 7, 8)
                n.aggregate(dve, i + 2, p, (1,))
                choose(i, 9)
                weigh(i - 1, q, 0)
                choose(i, 10, 11)
                n.aggregate(dve, i + 2, p, (2,))
                n.centre(dve, i + 2, p)
                choose(i, 12)
                weigh(i - 1, q, 1)
                choose(i, 13)
                if exists(i - 2):
                    dve.wait_ge(s_ytr, i - 1)
                    out = bank[TB_][0:T, 0:GB * D].rearrange("p (b s e) -> p s b e", b=2, s=2)
                    h = k.H[:, group(i - 2), :].rearrange("p (s b) e -> p s b e", s=2)
                    nc.vector.tensor_tensor(h, h, out, ALU.add).then_inc(n.added, 1)
                choose(i, 14)
                n.scale(dve, i + 2, p)

            pipeline(dve, steps, -2, 4, NG - 4, NG + 1)


def build(nc, a_x, a_txt, a_tw, a_f32, a_f16, a_out):
    with ExitStack() as ctx:
        k = Core(nc, ctx)
        k.norms = {}
        for phase, before in zip("aetm", (None, "a", "e", "t")):
            k.norms[phase] = Norm(k, phase, k.norms.get(before))
        embed_and_attend(k, a_x, a_txt, a_tw, a_f32, a_f16)
        mix_experts(k)
        mix_time(k)
        mix_mlps(k, a_out)


def lay_out(inputs):
    z = {n: np.asarray(a) for n, a in inputs.items()}
    f = {}

    def put(name, rows_, array):
        a = f.setdefault(name, np.zeros((128, pieces()[0][name]), np.float32))
        a[rows_] = array

    both = [slice(0, D), slice(D, 2 * D)]
    everywhere = slice(0, 128)
    x = z["x"].reshape(4, 4, 8, 3, 4, 16, 4, 16).transpose(0, 3, 5, 7, 1, 4, 6, 2)
    x = np.ascontiguousarray(x.reshape(4, 6, 128, 512).transpose(0, 2, 1, 3))
    txt = np.ascontiguousarray(z["txt"].transpose(1, 0, 2))
    put("tokw", everywhere, z["L0_tok_W"].T.reshape(6, 128, D).transpose(1, 0, 2).reshape(128, 6 * D))
    qkvb = z["L0_attn_qkv_b"]
    for r in both:
        put("tokb", r, z["L0_tok_b"][:, None])
        put("qkvw", r, z["L0_attn_qkv_w"])
        put("qb", r, qkvb[0:D, None])
        put("kb", r, qkvb[D:2 * D, None])
    put("vb", everywhere, np.repeat(qkvb[2 * D:].reshape(4, 1, 16), 2, 1).reshape(128, 1))
    put("pb", slice(0, 1), z["L0_attn_proj_b"])
    wp = np.zeros((4, 2, 16, 2, D), np.float32)
    for s in range(2):
        wp[:, s, :, s] = z["L0_attn_proj_w"].reshape(4, 16, D)
    put("wp", everywhere, wp.reshape(128, 2 * D))
    feature = np.arange(128) % D
    put("hmask", everywhere, feature[:, None] // HD == np.arange(HEADS))
    put("ident", everywhere, np.eye(128))
    put("rev0", everywhere, np.arange(E0, 0, -1))
    put("rev1", everywhere, np.arange(E1, 0, -1))
    for r in both:
        put("g0w", r, z["L0_ffn_Wg"])
        put("w1", r, z["L0_ffn_W1"].transpose(1, 0, 2).reshape(D, E0 * H0))
        kvrw = np.concatenate([z["L1_attn_Wk"], z["L1_attn_Wv"], z["L1_attn_Wr"]], 1)
        put("kvrw", r, kvrw)
        put("mix", r, np.concatenate([z[f"L1_attn_time_mix_{n}"].reshape(1, D) for n in "kvr"]).T)
        put("g1w", r, z["L1_ffn_gW"])
        put("sb3", r, z["L1_ffn_sb3"][:, None])
    put("g0b", everywhere, z["L0_ffn_bg"])
    put("g1b", everywhere, z["L1_ffn_gb"])
    put("b1", everywhere, z["L0_ffn_b1"].reshape(CH, 128).T)
    put("w2", everywhere, z["L0_ffn_W2"].reshape(CH, 128, D).transpose(1, 0, 2).reshape(128, CH * D))
    for i in range(2):
        put("b2", slice(i * E0, (i + 1) * E0), z["L0_ffn_b2"])
        put("fb3", slice(i * E1, (i + 1) * E1), z["L1_ffn_eb3"])
    wo = np.zeros((2, D, 2, D), np.float32)
    for s in range(2):
        wo[s, :, s] = z["L1_attn_Wo"]
    put("wo", everywhere, wo.reshape(128, 128))
    put("flip", slice(0, T), np.eye(T)[::-1])
    put("tri", slice(0, T), np.triu(np.ones((T, T))))
    fw1 = np.zeros((D, 5, 128), np.float32)
    fw1[:, 0, 0:D] = z["L1_ffn_sW1"]
    fw1[:, 1:] = z["L1_ffn_eW1"].transpose(1, 0, 2)
    for r in both:
        put("fw1", r, fw1.reshape(D, 640))
    fb1 = np.zeros((128, 5), np.float32)
    fb1[0:D, 0] = z["L1_ffn_sb1"]
    fb1[:, 1:] = z["L1_ffn_eb1"].T
    put("fb1", everywhere, fb1)
    put("fw2s", slice(0, D), z["L1_ffn_sW2"])
    put("fw2e", everywhere, z["L1_ffn_eW2"].transpose(1, 0, 2).reshape(128, E1 * D))
    put("fb2", everywhere, np.stack([z["L1_ffn_sb2"], z["L1_ffn_eb2"][0:2].reshape(-1), z["L1_ffn_eb2"][2:4].reshape(-1)], 1))
    put("fw3", everywhere, np.concatenate([z["L1_ffn_sW3"], z["L1_ffn_eW3"][0:2].reshape(128, D),
                                           z["L1_ffn_eW3"][2:4].reshape(128, D)], 1))
    h = {n: np.zeros((128, w), np.float16) for n, w in pieces()[1].items()}
    h["identh"][:] = np.eye(128)
    h["onesh"][0] = 1
    sel0 = h["sel0"].reshape(128, E0, 128)
    for e in range(E0):
        sel0[[e, E0 + e], e] = 0.5
    sel1 = h["sel1"].reshape(128, 2, 2, D)
    for e in range(E1):
        sel1[[e, E1 + e], e // 2, e % 2] = 0.5
    tw = np.concatenate([z["L1_attn_time_w"], np.zeros(T, np.float32)])[::-1]
    return dict(x=x, txt=txt, tw=np.ascontiguousarray(tw), f32=np.concatenate([f[n] for n in pieces()[0]], 1),
                f16=np.concatenate([h[n] for n in pieces()[1]], 1))


def kernel(**inputs):
    import concourse.bacc as bacc
    from concourse.bass_utils import run_bass_kernel_spmd

    arrays = lay_out(inputs)
    nc = bacc.Bacc("TRN2", target_bir_lowering=False, num_devices=1)
    args = [nc.dram_tensor(f"in_{n}", a.shape, mybir.dt.from_np(a.dtype), kind="ExternalInput").ap()
            for n, a in arrays.items()]
    out = nc.dram_tensor("out", (T, B, D), F32, kind="ExternalOutput").ap()
    build(nc, *args, out)
    r = run_bass_kernel_spmd(nc, [{f"in_{n}": a for n, a in arrays.items()}], core_ids=[0])
    return np.ascontiguousarray(r.results[0]["out"].transpose(1, 0, 2))
```
